# Optimizing a Trainium2 kernel written in Bass

```python
import numpy as np
import jax
import jax.numpy as jnp

def _softmax(x, axis=-1):
    return jax.nn.softmax(x, axis=axis)

def _gelu(x):
    return jax.nn.gelu(x, approximate=True)

def _silu(x):
    return jax.nn.silu(x)

def _sigmoid(x):
    return jax.nn.sigmoid(x)

def _layernorm(x, axis=-1, eps=1e-05):
    m = jnp.mean(x, axis=axis, keepdims=True)
    v = jnp.var(x, axis=axis, keepdims=True)
    return (x - m) / jnp.sqrt(v + eps)

def _scatter_add(tgt, idx, src, axis=0):
    return tgt.at[idx].add(src)

def _segment_sum(src, seg, n):
    return jax.ops.segment_sum(src, seg, n)
kernel_name = 'mk_macaron_d1_jaxref_r8_949e32'

def setup_inputs(seed: int=0):
    np.random.seed(seed)
    _w = jnp.asarray

    def _L0_attn_setup():
        import jax, jax.numpy as jnp
        import numpy as np
        N_HEAD = 16
        MAX_WAVELENGTH = 1250
        ROPE_PCT = 1.0

        def apply_p_rope(inputs, positions, head_dim, max_wavelength=MAX_WAVELENGTH, rope_percentage=ROPE_PCT):
            rope_angles = int(rope_percentage * head_dim // 2)
            nope_angles = head_dim // 2 - rope_angles
            fraction = 2.0 * jnp.arange(0, rope_angles) / head_dim
            timescale = max_wavelength ** fraction
            timescale = jnp.pad(timescale, (0, nope_angles), mode='constant', constant_values=(0, jnp.inf))
            sinusoid_inp = positions[..., None] / timescale[None, :]
            sin = jnp.sin(sinusoid_inp)
            cos = jnp.cos(sinusoid_inp)
            first_half, second_half = jnp.split(inputs, 2, axis=-1)
            first_part = first_half * cos - second_half * sin
            second_part = second_half * cos + first_half * sin
            return jnp.concatenate([first_part, second_part], axis=-1).astype(inputs.dtype)
        key = jax.random.key(seed)
        ks = jax.random.split(key, 4)
        B, T, C = (2, 256, 128)
        x = jax.random.normal(ks[0], (B, T, C), dtype=jnp.float32)
        W_attn = jax.random.normal(ks[1], (C, 3 * C), dtype=jnp.float32) * 0.02
        b_attn = jnp.zeros((3 * C,), dtype=jnp.float32)
        W_proj = jax.random.normal(ks[2], (C, C), dtype=jnp.float32) * 0.02
        b_proj = jnp.zeros((C,), dtype=jnp.float32)
        return {'x': x, 'W_attn': W_attn, 'b_attn': b_attn, 'W_proj': W_proj, 'b_proj': b_proj}
    _L0_attn_in = _L0_attn_setup()

    def _L0_ffn_setup():
        import jax, jax.numpy as jnp
        import numpy as np
        DIM = 128
        DEPTH = 2
        HEADS = 8
        DIM_HEAD = 64
        WINDOW = 64
        INNER = HEADS * DIM_HEAD
        HID = int(DIM * 4 * 2 / 3)
        B, N = (2, 1024)
        QK_SCALE = 8.0

        def shift_token(t):
            t1, t2 = jnp.split(t, 2, axis=-1)
            t2 = jnp.pad(t2, ((0, 0), (1, 0), (0, 0)))[:, :-1]
            return jnp.concatenate([t1, t2], axis=-1)

        def l2norm(t):
            return t / jnp.clip(jnp.linalg.norm(t, axis=-1, keepdims=True), 1e-12)

        def rotate_half(x):
            x1, x2 = jnp.split(x, 2, axis=-1)
            return jnp.concatenate([-x2, x1], axis=-1)

        def rotary_xpos(q, k):
            n = q.shape[-2]
            half_idx = jnp.arange(0, DIM_HEAD, 2, dtype=jnp.float32)
            inv_freq = 1.0 / 10000.0 ** (half_idx / DIM_HEAD)
            t = jnp.arange(n, dtype=jnp.float32)
            freqs = t[:, None] * inv_freq[None, :]
            freqs = jnp.concatenate([freqs, freqs], axis=-1)
            base = (half_idx + 0.4 * DIM_HEAD) / (1.4 * DIM_HEAD)
            power = (t - n // 2) / float(WINDOW // 2)
            scale = base[None, :] ** power[:, None]
            scale = jnp.concatenate([scale, scale], axis=-1)
            cos, sin = (jnp.cos(freqs), jnp.sin(freqs))
            q = q * cos * scale + rotate_half(q) * sin * scale
            k = k * cos / scale + rotate_half(k) * sin / scale
            return (q, k)

        def local_attention(q, k, v):
            b, h, n, d = q.shape
            w = n // WINDOW
            bq = q.reshape(b, h, w, WINDOW, d) * QK_SCALE
            bk = k.reshape(b, h, w, WINDOW, d)
            bv = v.reshape(b, h, w, WINDOW, d)

            def look_around(t):
                p = jnp.pad(t, ((0, 0), (0, 0), (1, 0), (0, 0), (0, 0)))
                return jnp.concatenate([p[:, :, :w], p[:, :, 1:]], axis=3)
            bk, bv = (look_around(bk), look_around(bv))
            bt = jnp.arange(n).reshape(w, WINDOW)
            btp = jnp.pad(bt, ((1, 0), (0, 0)), constant_values=-1)
            btk = jnp.concatenate([btp[:w], btp[1:]], axis=1)
            sim = jnp.einsum('bhwid,bhwjd->bhwij', bq, bk)
            i = bt[:, :, None]
            j = btk[:, None, :]
            mask = (i < j) | (i > j + WINDOW) | (j == -1)
            sim = jnp.where(mask, -jnp.finfo(sim.dtype).max, sim)
            attn = jax.nn.softmax(sim, axis=-1)
            out = jnp.einsum('bhwij,bhwjd->bhwid', attn, bv)
            return out.reshape(b, h, n, d)

        def _layer(x, wqkv, qs, ksc, wo, lg, lb, w1, b1, w2, b2):
            b, n, _ = x.shape
            h = shift_token(x)
            qkv = h @ wqkv
            q, k, v = jnp.split(qkv, 3, axis=-1)
            to_heads = lambda t: t.reshape(b, n, HEADS, DIM_HEAD).transpose(0, 2, 1, 3)
            q, k, v = (to_heads(q), to_heads(k), to_heads(v))
            q = l2norm(q) * qs
            k = l2norm(k) * ksc
            q, k = rotary_xpos(q, k)
            o = local_attention(q, k, v)
            o = o.transpose(0, 2, 1, 3).reshape(b, n, INNER)
            x = x + o @ wo
            h = shift_token(x)
            mu = h.mean(-1, keepdims=True)
            var = h.var(-1, keepdims=True)
            h = (h - mu) / jnp.sqrt(var + 1e-05) * lg + lb
            h = h @ w1 + b1
            a, g = jnp.split(h, 2, axis=-1)
            h = a * jax.nn.gelu(g, approximate=False)
            x = x + h @ w2 + b2
            return x
        key = jax.random.key(seed)
        ks = jax.random.split(key, 6)
        return {'x': jax.random.normal(ks[0], (B, N, DIM), jnp.float32), 'wqkv': jax.random.normal(ks[1], (DEPTH, DIM, 3 * INNER), jnp.float32) * 0.02, 'q_scale': jnp.ones((DEPTH, DIM_HEAD), jnp.float32), 'k_scale': jnp.ones((DEPTH, DIM_HEAD), jnp.float32), 'wo': jax.random.normal(ks[2], (DEPTH, INNER, DIM), jnp.float32) * 0.02, 'ln_g': jnp.ones((DEPTH, DIM), jnp.float32), 'ln_b': jnp.zeros((DEPTH, DIM), jnp.float32), 'w1': jax.random.normal(ks[3], (DEPTH, DIM, 2 * HID), jnp.float32) * 0.02, 'b1': jnp.zeros((DEPTH, 2 * HID), jnp.float32), 'w2': jax.random.normal(ks[4], (DEPTH, HID, DIM), jnp.float32) * 0.02, 'b2': jnp.zeros((DEPTH, DIM), jnp.float32)}
    _L0_ffn_in = _L0_ffn_setup()
    _d = {'L0_attn_x': _L0_attn_in['x'], 'L0_attn_W_attn': _L0_attn_in['W_attn'], 'L0_attn_b_attn': _L0_attn_in['b_attn'], 'L0_attn_W_proj': _L0_attn_in['W_proj'], 'L0_attn_b_proj': _L0_attn_in['b_proj'], 'L0_ffn_wqkv': _L0_ffn_in['wqkv'], 'L0_ffn_q_scale': _L0_ffn_in['q_scale'], 'L0_ffn_k_scale': _L0_ffn_in['k_scale'], 'L0_ffn_wo': _L0_ffn_in['wo'], 'L0_ffn_ln_g': _L0_ffn_in['ln_g'], 'L0_ffn_ln_b': _L0_ffn_in['ln_b'], 'L0_ffn_w1': _L0_ffn_in['w1'], 'L0_ffn_b1': _L0_ffn_in['b1'], 'L0_ffn_w2': _L0_ffn_in['w2'], 'L0_ffn_b2': _L0_ffn_in['b2']}
    _x0 = _d['L0_attn_x']
    _d['L0_attn_x'] = jax.random.normal(jax.random.fold_in(jax.random.key(seed), 1), (1, 2048, 128), dtype=_x0.dtype)
    del _x0
    return _d

def reference(L0_attn_x, L0_attn_W_attn, L0_attn_b_attn, L0_attn_W_proj, L0_attn_b_proj, L0_ffn_wqkv, L0_ffn_q_scale, L0_ffn_k_scale, L0_ffn_wo, L0_ffn_ln_g, L0_ffn_ln_b, L0_ffn_w1, L0_ffn_b1, L0_ffn_w2, L0_ffn_b2):

    def _L0_attn_ref(x, W_attn, b_attn, W_proj, b_proj):
        import jax, jax.numpy as jnp
        import numpy as np
        N_HEAD = 16
        MAX_WAVELENGTH = 1250
        ROPE_PCT = 1.0

        def apply_p_rope(inputs, positions, head_dim, max_wavelength=MAX_WAVELENGTH, rope_percentage=ROPE_PCT):
            rope_angles = int(rope_percentage * head_dim // 2)
            nope_angles = head_dim // 2 - rope_angles
            fraction = 2.0 * jnp.arange(0, rope_angles) / head_dim
            timescale = max_wavelength ** fraction
            timescale = jnp.pad(timescale, (0, nope_angles), mode='constant', constant_values=(0, jnp.inf))
            sinusoid_inp = positions[..., None] / timescale[None, :]
            sin = jnp.sin(sinusoid_inp)
            cos = jnp.cos(sinusoid_inp)
            first_half, second_half = jnp.split(inputs, 2, axis=-1)
            first_part = first_half * cos - second_half * sin
            second_part = second_half * cos + first_half * sin
            return jnp.concatenate([first_part, second_part], axis=-1).astype(inputs.dtype)
        B, T, C = x.shape
        H = N_HEAD
        D = C // H
        qkv = x @ W_attn + b_attn
        q, k, v = jnp.split(qkv, 3, axis=-1)

        def split_heads(t):
            return t.reshape(B, T, H, D).transpose(0, 2, 1, 3)
        q, k, v = (split_heads(q), split_heads(k), split_heads(v))
        positions = jnp.arange(T, dtype=q.dtype)
        q = apply_p_rope(q, positions, D)
        k = apply_p_rope(k, positions, D)
        scale = jnp.sqrt(D).astype(k.dtype)
        attn = jnp.einsum('bhqd,bhkd->bhqk', q, k) / scale
        causal_mask = jnp.tril(jnp.ones((T, T))).astype(bool)
        attn = jnp.where(causal_mask, attn, jnp.finfo(attn.dtype).min)
        attn = jax.nn.softmax(attn, axis=-1)
        y = jnp.einsum('bhqk,bhkd->bhqd', attn, v)
        y = y.transpose(0, 2, 1, 3).reshape(B, T, C)
        return y @ W_proj + b_proj

    def _L0_ffn_ref(x, wqkv, q_scale, k_scale, wo, ln_g, ln_b, w1, b1, w2, b2):
        import jax, jax.numpy as jnp
        import numpy as np
        DIM = 128
        DEPTH = 2
        HEADS = 8
        DIM_HEAD = 64
        WINDOW = 64
        INNER = HEADS * DIM_HEAD
        HID = int(DIM * 4 * 2 / 3)
        B, N = (2, 1024)
        QK_SCALE = 8.0

        def shift_token(t):
            t1, t2 = jnp.split(t, 2, axis=-1)
            t2 = jnp.pad(t2, ((0, 0), (1, 0), (0, 0)))[:, :-1]
            return jnp.concatenate([t1, t2], axis=-1)

        def l2norm(t):
            return t / jnp.clip(jnp.linalg.norm(t, axis=-1, keepdims=True), 1e-12)

        def rotate_half(x):
            x1, x2 = jnp.split(x, 2, axis=-1)
            return jnp.concatenate([-x2, x1], axis=-1)

        def rotary_xpos(q, k):
            n = q.shape[-2]
            half_idx = jnp.arange(0, DIM_HEAD, 2, dtype=jnp.float32)
            inv_freq = 1.0 / 10000.0 ** (half_idx / DIM_HEAD)
            t = jnp.arange(n, dtype=jnp.float32)
            freqs = t[:, None] * inv_freq[None, :]
            freqs = jnp.concatenate([freqs, freqs], axis=-1)
            base = (half_idx + 0.4 * DIM_HEAD) / (1.4 * DIM_HEAD)
            power = (t - n // 2) / float(WINDOW // 2)
            scale = base[None, :] ** power[:, None]
            scale = jnp.concatenate([scale, scale], axis=-1)
            cos, sin = (jnp.cos(freqs), jnp.sin(freqs))
            q = q * cos * scale + rotate_half(q) * sin * scale
            k = k * cos / scale + rotate_half(k) * sin / scale
            return (q, k)

        def local_attention(q, k, v):
            b, h, n, d = q.shape
            w = n // WINDOW
            bq = q.reshape(b, h, w, WINDOW, d) * QK_SCALE
            bk = k.reshape(b, h, w, WINDOW, d)
            bv = v.reshape(b, h, w, WINDOW, d)

            def look_around(t):
                p = jnp.pad(t, ((0, 0), (0, 0), (1, 0), (0, 0), (0, 0)))
                return jnp.concatenate([p[:, :, :w], p[:, :, 1:]], axis=3)
            bk, bv = (look_around(bk), look_around(bv))
            bt = jnp.arange(n).reshape(w, WINDOW)
            btp = jnp.pad(bt, ((1, 0), (0, 0)), constant_values=-1)
            btk = jnp.concatenate([btp[:w], btp[1:]], axis=1)
            sim = jnp.einsum('bhwid,bhwjd->bhwij', bq, bk)
            i = bt[:, :, None]
            j = btk[:, None, :]
            mask = (i < j) | (i > j + WINDOW) | (j == -1)
            sim = jnp.where(mask, -jnp.finfo(sim.dtype).max, sim)
            attn = jax.nn.softmax(sim, axis=-1)
            out = jnp.einsum('bhwij,bhwjd->bhwid', attn, bv)
            return out.reshape(b, h, n, d)

        def _layer(x, wqkv, qs, ksc, wo, lg, lb, w1, b1, w2, b2):
            b, n, _ = x.shape
            h = shift_token(x)
            qkv = h @ wqkv
            q, k, v = jnp.split(qkv, 3, axis=-1)
            to_heads = lambda t: t.reshape(b, n, HEADS, DIM_HEAD).transpose(0, 2, 1, 3)
            q, k, v = (to_heads(q), to_heads(k), to_heads(v))
            q = l2norm(q) * qs
            k = l2norm(k) * ksc
            q, k = rotary_xpos(q, k)
            o = local_attention(q, k, v)
            o = o.transpose(0, 2, 1, 3).reshape(b, n, INNER)
            x = x + o @ wo
            h = shift_token(x)
            mu = h.mean(-1, keepdims=True)
            var = h.var(-1, keepdims=True)
            h = (h - mu) / jnp.sqrt(var + 1e-05) * lg + lb
            h = h @ w1 + b1
            a, g = jnp.split(h, 2, axis=-1)
            h = a * jax.nn.gelu(g, approximate=False)
            x = x + h @ w2 + b2
            return x
        for l in range(DEPTH):
            x = _layer(x, wqkv[l], q_scale[l], k_scale[l], wo[l], ln_g[l], ln_b[l], w1[l], b1[l], w2[l], b2[l])
        return x
    x = L0_attn_x
    x = x + 0.5 * _L0_ffn_ref(_layernorm(x, axis=-1), L0_ffn_wqkv, L0_ffn_q_scale, L0_ffn_k_scale, L0_ffn_wo, L0_ffn_ln_g, L0_ffn_ln_b, L0_ffn_w1, L0_ffn_b1, L0_ffn_w2, L0_ffn_b2)
    x = x + _L0_attn_ref(_layernorm(x, axis=-1), L0_attn_W_attn, L0_attn_b_attn, L0_attn_W_proj, L0_attn_b_proj)
    x = x + 0.5 * _L0_ffn_ref(_layernorm(x, axis=-1), L0_ffn_wqkv, L0_ffn_q_scale, L0_ffn_k_scale, L0_ffn_wo, L0_ffn_ln_g, L0_ffn_ln_b, L0_ffn_w1, L0_ffn_b1, L0_ffn_w2, L0_ffn_b2)
    return x

_drawn_inputs = setup_inputs


def setup_inputs(seed=0):
    import zlib

    import numpy as np

    out = dict(_drawn_inputs(seed))
    spreads = {'L0_attn_b_attn': (0.0, 0.57),
     'L0_attn_b_proj': (0.0, 0.338),
     'L0_ffn_q_scale': (1.0, 0.6),
     'L0_ffn_k_scale': (1.0, 0.6),
     'L0_ffn_ln_g': (1.0, 0.6),
     'L0_ffn_ln_b': (0.0, 0.8),
     'L0_ffn_b1': (0.0, 0.8),
     'L0_ffn_b2': (0.0, 0.1)}
    factors = {'L0_attn_W_attn': 8.0,
     'L0_attn_W_proj': 4.395,
     'L0_ffn_wqkv': 3.432,
     'L0_ffn_wo': 3.408,
     'L0_ffn_w1': 5.311,
     'L0_ffn_w2': 5.219}
    for name, (base, spread) in spreads.items():
        noise = np.random.default_rng([zlib.crc32(name.encode()), seed]).standard_normal(out[name].shape)
        drawn = base * np.exp(spread * noise) if base else spread * noise
        out[name] = jnp.asarray(drawn.astype(out[name].dtype))
    for name, factor in factors.items():
        out[name] = (out[name] * factor).astype(out[name].dtype)
    return out
```

```python
from contextlib import ExitStack

import numpy as np
import concourse.bass as bass
from concourse import mybir

F32 = mybir.dt.float32
F32R = mybir.dt.float32r
BF16 = mybir.dt.bfloat16
ALU = mybir.AluOpType
ACT = mybir.ActivationFunctionType
AX_X = mybir.AxisListType.X

P = 128
T = 2048
C = 128
NT = T // P
LN_EPS = 1e-5
MASKED = -1.0e30

DEPTH = 2
HEADS, DH, WINDOW = 8, 64, 64
INNER = HEADS * DH
HID = int(C * 4 * 2 / 3)
CH = [(0, 128), (128, 128), (256, HID - 256)]
NC_ = len(CH)
QK_SCALE = 8.0

H2, D2 = 16, 8
SLOT = 32
NG = 4
HG = H2 // NG
NQ = T // 512
MROW = 24


def past(eng, sem, value):
    if isinstance(value, int) and value <= 0:
        return
    eng.wait_ge(sem, value)


def steps(eng, first, last):
    with eng.Fori(first // 2, last // 2) as pair:
        for slot in range(2):
            yield 2 * pair + slot, slot


def tiles(eng, n=NT):
    for i in range(2):
        yield i, i
    yield from steps(eng, 2, n)


def ln_vector(dve, nc, K, S, n):
    for i, _ in steps(dve, 0, NT):
        nc.vector.bn_stats(K.st6[:, i, :], K.x[:, i, :]).then_inc(S["ln_stat"], 1)
    dve.wait_ge(S["ln_stat"], 16 * (n + 1))
    for i in range(NT):
        nc.vector.bn_aggr(K.mv[:, i, :], K.st6[:, i, :]).then_inc(S["ln_aggr"], 1)
    dve.wait_ge(S["ln_aggr"], 16 * (n + 1))
    nc.vector.tensor_scalar(K.vare[:, :], K.mv[:, :, 1], LN_EPS, None, ALU.add).then_inc(S["ln_var"], 1)
    dve.wait_ge(S["ln_sd"], n + 1)
    nc.vector.reciprocal(K.rstd[:, :], K.sd[:, :]).then_inc(S["ln_rstd"], 1)
    dve.wait_ge(S["ln_rstd"], n + 1)
    for i, p in tiles(dve):
        nc.vector.tensor_scalar(K.y[:, i, :], K.x[:, i, :], K.mv[:, i, 0:1], K.rstd_at(i),
                                ALU.subtract, ALU.mult).then_inc(S["ln_y"], 1)


def ln_scalar(act, nc, K, S, n):
    act.wait_ge(S["ln_var"], n + 1)
    nc.scalar.activation(K.sd[:, :], K.vare[:, :], ACT.Sqrt).then_inc(S["ln_sd"], 1)


class Keep:

    def __init__(self, nc, stack):
        def sb(name, shape, dt=F32):
            return stack.enter_context(nc.sbuf_tensor(name, shape, dt))

        self.x = sb("x_tok", [P, NT, C])
        self.y = sb("y_tok", [P, NT, C])
        self.ident = sb("ident", [P, P])
        self.identb = sb("identb", [P, P], BF16)
        self.st6 = sb("st6", [P, NT, 6])
        self.mv = sb("mv", [P, NT, 2])
        self.vare = sb("vare", [P, NT])
        self.sd = sb("sd", [P, NT])
        self.rstd = sb("rstd", [P, NT])

    def rstd_at(self, i):
        return self.rstd[:, :].rearrange("p (i o) -> p i o", o=1)[:, i, :]


def ffn_block(nc, K, S, dram, which):
    with ExitStack() as stack:
        def sb(name, shape, dt=F32):
            return stack.enter_context(nc.sbuf_tensor(f"{name}_{which}", shape, dt))

        qk = sb("qk", [P, NT, 2 * INNER])
        v = sb("v", [P, NT + 1, HEADS, DH + 1])
        rc = sb("rc", [P, NT, 2, DH // 2])
        rs = sb("rs", [P, NT, 2, 2, DH // 2])
        wqkv = sb("wqkv", [P, 3 * INNER])
        wo = sb("wo", [P, INNER // P, C])
        w1 = sb("w1", [P, 2 * HID])
        w2 = sb("w2", [P, NC_, C])
        b1 = sb("b1", [P, 2 * NC_])
        lng = sb("lng", [P, 1])
        lnb = sb("lnb", [P, 1])
        qks = sb("qks", [P, 2, DH])
        maskf = sb("maskf", [P, 2, P])
        mask = sb("mask", [P, NT, P], BF16)
        ss = sb("ss", [P, NT, 2 * HEADS])
        nrm = sb("nrm", [P, NT, 2 * HEADS])
        mx = sb("mx", [P, 2, HEADS])
        rsum = sb("rsum", [P, 2, HEADS])
        ta = sb("ta", [P, 2, 2 * INNER])
        tb = sb("tb", [P, 2 * INNER])
        qk2 = sb("qk2", [P, 2, 2 * INNER])
        qkt = sb("qkt", [P, 2, 2 * INNER // P, P])
        sS = sb("sS", [P, 2 * HEADS * P])
        pt = sb("pt", [P, 2, HEADS, P])
        ot = sb("ot", [P, INNER])
        oT = sb("oT", [P, INNER // P, P])
        vs = sb("vs", [P, 2, HEADS, DH + 1])
        ve = sb("ve", [P, 2, HEADS, DH + 1])
        ps = stack.enter_context(nc.psum_tensor(f"ps_{which}", [P, 8, 512], F32))

        hs = sS[:, :].rearrange("p (i c) -> p i c", c=C)
        prob = sS[:, :].rearrange("p (s h k) -> p s h k", s=2, h=HEADS)
        sq = qkt[:, :, :, :].rearrange("p s b t -> p s (b t)")
        ys = pt[:, 0, 0:2, :]
        ht = pt[:, 0, 2:4, :]
        flat = qk[:, :, :].rearrange("p i n -> p (i n)")
        hT = flat[:, 0:T]
        hid = flat[:, T:T + 2 * NC_ * 512].rearrange("p (s c t) -> p s c t", s=2, c=NC_)
        gel = flat[:, T + 3072:T + 4096].rearrange("p (s t) -> p s t", s=2)
        hn = flat[:, T + 4096:T + 4352].rearrange("p (s t) -> p s t", s=2)
        hb = pt[:, :, 0:4, :].rearrange("p s a t -> p s (a t)")

        def qk_view(ap):
            return ap.rearrange("p (z m d) -> p z m d", z=2, d=DH // 2)

        def o_bank(ap):
            return ap[:, 6:8, 0:4 * (DH + 1)].rearrange("p b (h d) -> p b h d", d=DH + 1)

        block = stack.enter_context(nc.Block())

        @block.sync
        def _(sp):
            def load_qkv(l, L):
                past(sp, S["qkv"], 16 * L)
                past(sp, S["qk_out"], 16 * L)
                sp.dma_start(wqkv[:, :], dram["wqkv"][l]).then_inc(S["w_qkv"], 16)
                sp.dma_start(qks[:, 0, :], dram["q_scale"][l:l + 1, :].partition_broadcast(P)
                             .rearrange("p o d -> p (o d)")).then_inc(S["w_qkv"], 16)
                sp.dma_start(qks[:, 1, :], dram["k_scale"][l:l + 1, :].partition_broadcast(P)
                             .rearrange("p o d -> p (o d)")).then_inc(S["w_qkv"], 16)

            def load_wo(l, L):
                past(sp, S["wo_mm"], 16 * L)
                sp.dma_start(wo[:, :, :], dram["wo"][l].rearrange("(b p) n -> p b n", p=P)).then_inc(S["w_o"], 16)

            def load_mlp(l, L):
                past(sp, S["w2_mm"], 4 * L)
                past(sp, S["gelu"], 12 * L)
                past(sp, S["gate"], 12 * L)
                col = lambda ap: ap.rearrange("(p o) -> p o", o=1)
                sp.dma_start(w1[:, :], dram["w1"][l]).then_inc(S["w_mlp"], 16)
                sp.dma_start(lng[:, :], col(dram["ln_g"][l])).then_inc(S["w_mlp"], 16)
                sp.dma_start(lnb[:, :], col(dram["ln_b"][l])).then_inc(S["w_mlp"], 16)
                for c, (h0, hc) in enumerate(CH):
                    sp.dma_start(w2[0:hc, c, :], dram["w2"][l, h0:h0 + hc, :]).then_inc(S["w_mlp"], 16)
                    for half in range(2):
                        sp.dma_start(b1[0:hc, half * NC_ + c:half * NC_ + c + 1],
                                     col(dram["b1"][l, half * HID + h0:half * HID + h0 + hc])
                                     ).then_inc(S["w_mlp"], 16)
                hc = CH[-1][1]
                sp.dma_start(w2[hc:hc + 1, NC_ - 1, :], dram["b2"][l:l + 1, :]).then_inc(S["w_mlp"], 16)

            def shift():
                sp.dma_start(hs[:, :, 0:C // 2], K.y[:, :, 0:C // 2]).then_inc(S["shifted"], 16)
                sp.dma_start(hs[1:P, :, C // 2:C], K.y[0:P - 1, :, C // 2:C]).then_inc(S["shifted"], 16)
                sp.dma_start(hs[0:1, 1:NT, C // 2:C], K.y[P - 1:P, 0:NT - 1, C // 2:C]).then_inc(S["shifted"], 16)

            if which == 0:
                sp.dma_start(K.x[:, :, :], dram["x"].rearrange("(i p) c -> p i c", p=P)).then_inc(S["x_in"], 16)
                sp.dma_start(K.ident[:, :], dram["ident"]).then_inc(S["consts"], 16)
            sp.dma_start(maskf[:, :, :], dram["local_mask"]).then_inc(S["consts"], 16)
            sp.dma_start(rc[:, :, :, :], dram["rope_c"]).then_inc(S["rope_in"], 16)
            sp.dma_start(rs[:, :, :, :, :], dram["rope_s"]).then_inc(S["rope_in"], 16)
            load_qkv(0, DEPTH * which)
            load_wo(0, DEPTH * which)
            load_mlp(0, DEPTH * which)
            for l in range(DEPTH):
                L = DEPTH * which + l
                if l == 0:
                    sp.wait_ge(S["ln_y"], 16 * (2 * which + 1))
                else:
                    sp.wait_ge(S["y_mlp"], 4 * L)
                sp.wait_ge(S["shift_zero"], 2 * L + 1)
                shift()
                sp.wait_ge(S["v_out"], 16 * (L + 1))
                if l + 1 < DEPTH:
                    load_qkv(l + 1, L + 1)
                if l == 0:
                    sp.wait_ge(S["v_ones"], 2 * (which + 1))
                for i, p in tiles(sp):
                    past(sp, S["pv"], 16 * L + i - 1)
                    sp.dma_start(vs[:, p], v[:, i + 1]).then_inc(S["v_stage"][p], 16)
                    sp.dma_start(ve[0:64, p], v[0:64, i + 1]).then_inc(S["v_stage"][p], 16)
                    sp.dma_start(ve[64:P, p], v[64:P, i]).then_inc(S["v_stage"][p], 16)
                sp.wait_ge(S["y_attn"], 16 * (L + 1))
                sp.wait_ge(S["shift_zero"], 2 * L + 2)
                shift()
                if l + 1 < DEPTH:
                    load_wo(l + 1, L + 1)
                    load_mlp(l + 1, L + 1)
            if which == 1:
                sp.wait_ge(S["x_ffn"], which + 1)
                sp.dma_start(dram["out"].rearrange("(i p) c -> p i c", p=P), K.x[:, :, :]).then_inc(S["stored"], 16)
                sp.wait_ge(S["stored"], 16)

        @block.gpsimd
        def _(pool):
            nc.gpsimd.memset(v[:, 1:, :, DH:], 1.0).then_inc(S["v_ones"], 1)
            nc.gpsimd.memset(v[:, 0], 0.0).then_inc(S["v_ones"], 1)
            for l in range(DEPTH):
                L = DEPTH * which + l
                pool.wait_ge(S["shifted"], 48 * (2 * L + 1))
                for i, p in tiles(pool):
                    past(pool, S["tp"], 16 * L + i - 1)
                    nc.gpsimd.tensor_copy(ys[:, p, :], hs[:, i, :]).then_inc(S["ys"], 1)
                pool.wait_ge(S["rope_in"], 32 * (which + 1))
                pool.wait_ge(S["inv_norm"], L + 1)
                for i, p in tiles(pool):
                    nc.gpsimd.tensor_tensor(
                        qk[:, i].rearrange("p (h d) -> p h d", d=DH),
                        qk[:, i].rearrange("p (h d) -> p h d", d=DH),
                        ss[:, i].rearrange("p (h o) -> p h o", o=1).broadcast_to((P, 2 * HEADS, DH)),
                        ALU.mult).then_inc(S["unit"], 1)
                    pool.wait_ge(S["unit"], 16 * L + i + 1)
                    past(pool, S["rot"], 16 * L + i - 1)
                    nc.gpsimd.tensor_tensor(
                        qk_view(ta[:, p]), qk_view(qk[:, i]),
                        rc[:, i].rearrange("p z (o d) -> p z o d", o=1).broadcast_to((P, 2, 16, DH // 2)),
                        ALU.mult).then_inc(S["cos_part"], 1)

        @block.vector
        def _(dve):
            dve.wait_ge(S["x_in"], 16)
            dve.wait_ge(S["consts"], 32 + 16 * which)
            if which == 0:
                nc.vector.tensor_copy(K.identb[:, :], K.ident[:, :]).then_inc(S["const_b"], 1)
            nc.vector.tensor_copy(mask[:, 0, :], maskf[:, 0, :]).then_inc(S["const_b"], 1)
            nc.vector.tensor_copy(
                mask[:, 1:, :], maskf[:, 1:2, :].broadcast_to((P, NT - 1, P))).then_inc(S["const_b"], 1)
            if which == 1:
                dve.wait_ge(S["x_attn"], 4)
            ln_vector(dve, nc, K, S, 2 * which)
            for l in range(DEPTH):
                L = DEPTH * which + l
                if l == 0:
                    dve.wait_ge(S["ln_y"], 16 * (2 * which + 1))
                else:
                    dve.wait_ge(S["y_mlp"], 4 * L)
                nc.vector.memset(hs[0:1, 0, C // 2:C], 0.0).then_inc(S["shift_zero"], 1)
                dve.wait_ge(S["w_qkv"], 48 * (L + 1))
                for i, p in tiles(dve):
                    dve.wait_ge(S["squares"], 16 * L + i + 1)
                    nc.vector.tensor_reduce(ss[:, i], sq[:, p].rearrange("p (h d) -> p h d", d=DH),
                                            AX_X, ALU.add).then_inc(S["sumsq"], 1)
                    dve.wait_ge(S["qkv"], 16 * L + i + 1)
                    nc.vector.tensor_tensor(
                        qk[:, i].rearrange("p (z h d) -> p z h d", z=2, d=DH),
                        ps[:, 2 * p:2 * p + 2].rearrange("p z (h d) -> p z h d", d=DH),
                        qks[:, :, :].rearrange("p z (o d) -> p z o d", o=1).broadcast_to((P, 2, HEADS, DH)),
                        ALU.mult).then_inc(S["qk_out"], 1)
                dve.wait_ge(S["norms"], L + 1)
                nc.vector.tensor_scalar(nrm[:, :, :], nrm[:, :, :], 1e-12, None, ALU.max).then_inc(S["norm_max"], 1)
                dve.wait_ge(S["norm_max"], L + 1)
                nc.vector.reciprocal(ss[:, :, :], nrm[:, :, :]).then_inc(S["inv_norm"], 1)

                def rotate(i, p):
                    dve.wait_ge(S["cos_part"], 16 * L + i + 1)
                    past(dve, S["rot"], 16 * L + i)
                    for z in range(2):
                        half = qk[:, i, z * INNER:(z + 1) * INNER].rearrange("p (h a d) -> p h a d", a=2, d=DH // 2)
                        nc.vector.tensor_tensor(
                            tb[:, z * INNER:(z + 1) * INNER].rearrange("p (h a d) -> p h a d", a=2, d=DH // 2)[:, :, ::-1, :],
                            half,
                            rs[:, i, z].rearrange("p (o a) d -> p o a d", o=1).broadcast_to((P, HEADS, 2, DH // 2)),
                            ALU.mult).then_inc(S["sin_part"], 1)
                    dve.wait_ge(S["sin_part"], 2 * (16 * L + i) + 2)
                    past(dve, S["tq"], 16 * L + i - 1)
                    nc.vector.tensor_tensor(qk2[:, p], ta[:, p], tb[:, :], ALU.add).then_inc(S["rot"], 1)

                def soften(i, p):
                    scores = ps[:, 2:4].rearrange("p b (h k) -> p (b h) k", k=P)
                    dve.wait_ge(S["scores"], 16 * L + i + 1)
                    nc.vector.tensor_reduce(mx[:, p], scores, AX_X, ALU.max).then_inc(S["row_max"], 1)
                    dve.wait_ge(S["row_max"], 16 * L + i + 1)
                    past(dve, S["ptr"], 16 * L + i - 1)
                    nc.vector.tensor_tensor(
                        prob[:, p], scores,
                        mx[:, p].rearrange("p (h o) -> p h o", o=1).broadcast_to((P, HEADS, P)),
                        ALU.subtract).then_inc(S["less_max"], 1)

                def normalize(i, p):
                    dve.wait_ge(S["pv"], 16 * L + i + 1)
                    nc.vector.reciprocal(
                        rsum[:, p].rearrange("p (b h o) -> p b h o", b=2, o=1),
                        o_bank(ps)[:, :, :, DH:]).then_inc(S["row_sum"], 1)
                    dve.wait_ge(S["row_sum"], 16 * L + i + 1)
                    past(dve, S["otr"], 16 * L + i)
                    nc.vector.tensor_tensor(
                        ot[:, :].rearrange("p (b h d) -> p b h d", b=2, d=DH), o_bank(ps)[:, :, :, 0:DH],
                        rsum[:, p].rearrange("p (b h o) -> p b h o", b=2, o=1).broadcast_to((P, 2, 4, DH)),
                        ALU.mult).then_inc(S["o_norm"], 1)

                def add_attn(i):
                    dve.wait_ge(S["wo_mm"], 16 * L + i + 1)
                    nc.vector.tensor_tensor(K.y[:, i], K.y[:, i], ps[:, 1, 0:C], ALU.add).then_inc(S["y_attn"], 1)

                rotate(0, 0)
                rotate(1, 1)
                soften(0, 0)
                rotate(2, 0)
                soften(1, 1)
                normalize(0, 0)
                add_attn(0)
                with dve.Fori(1, NT // 2 - 1) as pair:
                    for p in range(2):
                        i = 2 * pair + p
                        rotate(i + 1, 1 - p)
                        soften(i, p)
                        normalize(i - 1, 1 - p)
                        add_attn(i - 1)
                rotate(NT - 1, 1)
                soften(NT - 2, 0)
                normalize(NT - 3, 1)
                add_attn(NT - 3)
                soften(NT - 1, 1)
                for i in (NT - 2, NT - 1):
                    normalize(i, i % 2)
                    add_attn(i)

                dve.wait_ge(S["y_attn"], 16 * (L + 1))
                nc.vector.memset(hs[0:1, 0, C // 2:C], 0.0).then_inc(S["shift_zero"], 1)
                nc.vector.memset(hid[64:P, :, NC_ - 1, :], 1.0).then_inc(S["hid_ones"], 1)
                dve.wait_ge(S["hid_ones"], L + 1)
                dve.wait_ge(S["shifted"], 48 * (2 * L + 2))
                for i, _ in steps(dve, 0, NT):
                    nc.vector.bn_stats(K.st6[:, i, :], hs[:, i, :]).then_inc(S["h_stat"], 1)
                dve.wait_ge(S["h_stat"], 16 * (L + 1))
                for i in range(NT):
                    nc.vector.bn_aggr(K.mv[:, i, :], K.st6[:, i, :]).then_inc(S["h_aggr"], 1)
                dve.wait_ge(S["h_aggr"], 16 * (L + 1))
                nc.vector.tensor_scalar(K.vare[:, :], K.mv[:, :, 1], LN_EPS, None, ALU.add).then_inc(S["h_var"], 1)
                dve.wait_ge(S["h_sd"], L + 1)
                nc.vector.reciprocal(K.rstd[:, :], K.sd[:, :]).then_inc(S["h_rstd"], 1)
                dve.wait_ge(S["h_rstd"], L + 1)

                def norm_group(g):
                    for i in range(4 * g, 4 * g + 4):
                        past(dve, S["h_tp"], 16 * L + i - 1)
                        nc.vector.tensor_scalar(hn[:, i % 2, :], hs[:, i, :], K.mv[:, i, 0:1], K.rstd[:, i:i + 1],
                                                ALU.subtract, ALU.mult).then_inc(S["h_norm"], 1)

                def add_mlp(g):
                    dve.wait_ge(S["w2_mm"], 4 * L + g + 1)
                    yg = K.y[:, 4 * g:4 * g + 4].rearrange("p i c -> p (i c)")
                    nc.vector.tensor_tensor(yg, yg, ps[:, 4 + g % 2, :], ALU.add).then_inc(S["y_mlp"], 1)

                dve.wait_ge(S["w_mlp"], 208 * (L + 1))
                norm_group(0)
                for g in range(NT // 4):
                    if g + 1 < NT // 4:
                        norm_group(g + 1)
                    past(dve, S["w2_mm"], 4 * L + g - 1)
                    for c, (_, hc) in enumerate(CH):
                        u = NC_ * g + c
                        dve.wait_ge(S["gelu"], 12 * L + u + 1)
                        nc.vector.scalar_tensor_tensor(
                            out=hid[0:hc, g % 2, c, :], in0=ps[0:hc, 2 * (u % 2), :], scalar=b1[0:hc, c:c + 1],
                            in1=gel[0:hc, u % 2, :], op0=ALU.add, op1=ALU.mult).then_inc(S["gate"], 1)
                    if g >= 1:
                        add_mlp(g - 1)
                add_mlp(NT // 4 - 1)
            dve.wait_ge(S["y_mlp"], 4 * DEPTH * (which + 1))
            nc.vector.scalar_tensor_tensor(
                out=K.x[:, :, :].rearrange("p i c -> p (i c)"), in0=K.y[:, :, :].rearrange("p i c -> p (i c)"),
                scalar=0.5, in1=K.x[:, :, :].rearrange("p i c -> p (i c)"),
                op0=ALU.mult, op1=ALU.add).then_inc(S["x_ffn"], 1)

        @block.scalar
        def _(act):
            ln_scalar(act, nc, K, S, 2 * which)
            for l in range(DEPTH):
                L = DEPTH * which + l
                if l == 0:
                    act.wait_ge(S["v_ones"], 2 * (which + 1))
                for i, p in tiles(act):
                    act.wait_ge(S["tp"], 16 * L + i + 1)
                    past(act, S["qkv"], 16 * L + i - 1)
                    nc.scalar.copy(ht[:, p, :], ps[:, 6 + p, 0:P]).then_inc(S["ht"], 1)
                    act.wait_ge(S["qkv"], 16 * L + i + 1)
                    past(act, S["sumsq"], 16 * L + i - 1)
                    nc.scalar.activation(sq[:, p], ps[:, 2 * p:2 * p + 2].rearrange("p b n -> p (b n)"),
                                         ACT.Square).then_inc(S["squares"], 1)
                    nc.scalar.copy(v[:, i + 1, :, 0:DH],
                                   ps[:, 4 + p].rearrange("p (h d) -> p h d", d=DH)).then_inc(S["v_out"], 1)
                act.wait_ge(S["sumsq"], 16 * (L + 1))
                nc.scalar.activation(nrm[:, :, :], ss[:, :, :], ACT.Sqrt).then_inc(S["norms"], 1)

                def out_qkt(i, p):
                    act.wait_ge(S["tq"], 16 * L + i + 1)
                    past(act, S["scores"], 16 * L + i)
                    nc.scalar.copy(qkt[:, p], ps[:, 0:2].rearrange("p b (c t) -> p (b c) t", t=P)).then_inc(S["qkt"], 1)

                def out_pt(i, p):
                    act.wait_ge(S["ptr"], 16 * L + i + 1)
                    past(act, S["pv"], 16 * L + i - 1)
                    nc.scalar.copy(pt[:, p], ps[:, 4:6].rearrange("p b (h t) -> p (b h) t", t=P)).then_inc(S["pt"], 1)

                def out_ot(i):
                    act.wait_ge(S["otr"], 16 * L + i + 1)
                    past(act, S["wo_mm"], 16 * L + i)
                    nc.scalar.copy(oT[:, :, :], ps[:, 0].rearrange("p (b t) -> p b t", t=P)).then_inc(S["ot"], 1)

                def exps(i, p):
                    act.wait_ge(S["less_max"], 16 * L + i + 1)
                    nc.scalar.activation(prob[:, p], prob[:, p], ACT.Exp).then_inc(S["exps"], 1)

                out_qkt(0, 0)
                exps(0, 0)
                out_qkt(1, 1)
                out_pt(0, 0)
                exps(1, 1)
                out_ot(0)
                for i, p in steps(act, 2, NT):
                    out_qkt(i, p)
                    out_pt(i - 1, 1 - p)
                    exps(i, p)
                    out_ot(i - 1)
                out_pt(NT - 1, 1)
                out_ot(NT - 1)

                act.wait_ge(S["h_var"], L + 1)
                nc.scalar.activation(K.sd[:, :], K.vare[:, :], ACT.Sqrt).then_inc(S["h_sd"], 1)
                act.wait_ge(S["w_mlp"], 208 * (L + 1))

                def out_ht(g):
                    act.wait_ge(S["h_tp"], 16 * L + 4 * g + 4)
                    nc.scalar.activation(hT[:, 512 * g:512 * g + 512], ps[:, 6 + g % 2, :], ACT.Identity,
                                         bias=lnb[:, :], scale=lng[:, :]).then_inc(S["hT"], 1)

                out_ht(0)
                for g in range(NT // 4):
                    if g + 1 < NT // 4:
                        out_ht(g + 1)
                    for c, (_, hc) in enumerate(CH):
                        u = NC_ * g + c
                        act.wait_ge(S["w1_mm"], 12 * L + u + 1)
                        past(act, S["gate"], 12 * L + u - 1)
                        nc.scalar.activation(gel[0:hc, u % 2, :], ps[0:hc, 2 * (u % 2) + 1, :], ACT.Gelu,
                                             bias=b1[0:hc, NC_ + c:NC_ + c + 1]).then_inc(S["gelu"], 1)

        @block.tensor
        def _(pe):
            pe.wait_ge(S["const_b"], 3 + 2 * which)
            for l in range(DEPTH):
                L = DEPTH * which + l

                def turn(i, p):
                    pe.wait_ge(S["ys"], 16 * L + i + 1)
                    past(pe, S["ht"], 16 * L + i - 1)
                    nc.tensor.transpose(ps[:, 6 + p, 0:P], ys[:, p, :], K.ident[:, :]).then_inc(S["tp"], 1)

                def project(i, p):
                    pe.wait_ge(S["ht"], 16 * L + i + 1)
                    past(pe, S["qk_out"], 16 * L + i - 1)
                    past(pe, S["v_out"], 16 * L + i - 1)
                    for z in range(3):
                        bank = 2 * p + z if z < 2 else 4 + p
                        mm = nc.tensor.matmul(ps[:, bank, :], ht[:, p, :], wqkv[:, INNER * z:INNER * (z + 1)],
                                              start=True, stop=True)
                    mm.then_inc(S["qkv"], 1)

                pe.wait_ge(S["w_qkv"], 48 * (L + 1))
                turn(0, 0)
                turn(1, 1)
                project(0, 0)
                with pe.Fori(1, NT // 2) as pair:
                    for p in range(2):
                        turn(2 * pair + p, p)
                        project(2 * pair + p - 1, 1 - p)
                project(NT - 1, 1)

                def turn_qk(i, p):
                    pe.wait_ge(S["rot"], 16 * L + i + 1)
                    past(pe, S["ot"], 16 * L + i - 1)
                    past(pe, S["y_attn"], 16 * L + i - 1)
                    for b in range(8):
                        mm = nc.tensor.transpose(ps[:, b // 4, (b % 4) * P:(b % 4 + 1) * P],
                                                 qk2[:, p, b * P:(b + 1) * P], K.ident[:, :])
                    mm.then_inc(S["tq"], 1)

                def score(i, p):
                    pe.wait_ge(S["qkt"], 16 * L + i + 1)
                    past(pe, S["less_max"], 16 * L + i)
                    for b in range(2):
                        nc.tensor.matmul(
                            ps[:, 2 + b].rearrange("p (h k) -> p h k", k=P), K.identb[:, :],
                            mask[:, i].rearrange("p (o k) -> p o k", o=1).broadcast_to((P, 4, P)),
                            start=True, stop=False, skip_group_check=True)
                    for h in range(HEADS):
                        r, b = DH * (h % 2), h // 2
                        out = ps[:, 2 + h % 2, b * P:(b + 1) * P]
                        nc.tensor.matmul(out[0:64, 0:64], qkt[r:r + DH, p, b, 0:64], qkt[r:r + DH, p, 4 + b, 0:64],
                                         start=False, stop=True, skip_group_check=True)
                        nc.tensor.matmul(out[0:64, 64:P], qkt[r:r + DH, p, b, 0:64],
                                         qkt[r:r + DH, 1 - p, 4 + b, 64:P],
                                         start=False, stop=True, skip_group_check=True)
                        mm = nc.tensor.matmul(out[64:P, :], qkt[r:r + DH, p, b, 64:P], qkt[r:r + DH, p, 4 + b, :],
                                              start=False, stop=True, skip_group_check=True)
                    mm.then_inc(S["scores"], 1)

                def turn_p(i, p):
                    pe.wait_ge(S["exps"], 16 * L + i + 1)
                    past(pe, S["pt"], 16 * L + i)
                    for h in range(HEADS):
                        mm = nc.tensor.transpose(ps[:, 4 + h // 4, (h % 4) * P:(h % 4 + 1) * P],
                                                 prob[:, p, h, :], K.ident[:, :])
                    mm.then_inc(S["ptr"], 1)

                def weigh(i, p, v_staged):
                    pe.wait_ge(S["pt"], 16 * L + i + 1)
                    pe.wait_ge(S["v_stage"][p], v_staged)
                    past(pe, S["o_norm"], 16 * L + i)
                    for h in range(HEADS):
                        out = o_bank(ps)[:, h // 4, h % 4, :]
                        s = 4 * (h % 2) + h // 2
                        nc.tensor.matmul(out[0:64], pt[:, p, s, 0:64], ve[:, p, h, :], start=True, stop=True)
                        mm = nc.tensor.matmul(out[64:P], pt[:, p, s, 64:P], vs[:, p, h, :], start=True, stop=True)
                    mm.then_inc(S["pv"], 1)

                def output(i, turned):
                    pe.wait_ge(S["o_norm"], 16 * L + i + 1)
                    pe.wait_ge(S["qkt"], turned)
                    for b in range(4):
                        mm = nc.tensor.transpose(ps[:, 0, b * P:(b + 1) * P], ot[:, b * P:(b + 1) * P], K.ident[:, :])
                    mm.then_inc(S["otr"], 1)
                    pe.wait_ge(S["ot"], 16 * L + i + 1)
                    for b in range(4):
                        mm = nc.tensor.matmul(ps[:, 1, 0:C], oT[:, b, :], wo[:, b, :], start=(b == 0), stop=(b == 3))
                    mm.then_inc(S["wo_mm"], 1)

                pe.wait_ge(S["w_o"], 16 * (L + 1))
                turn_qk(0, 0)
                score(0, 0)
                turn_qk(1, 1)
                turn_p(0, 0)
                score(1, 1)
                weigh(0, 0, 48 * (8 * L + 1))
                output(0, 16 * L + 2)
                with pe.Fori(1, NT // 2) as pair:
                    for p in range(2):
                        i = 2 * pair + p
                        turn_qk(i, p)
                        turn_p(i - 1, 1 - p)
                        score(i, p)
                        weigh(i - 1, 1 - p, 48 * (pair + (8 * L + p)))
                        output(i - 1, 16 * L + i + 1)
                turn_p(NT - 1, 1)
                weigh(NT - 1, 1, 48 * (8 * L + 8))
                output(NT - 1, 16 * L + NT)

                def turn_h(g):
                    past(pe, S["hT"], 4 * L + g - 1)
                    for i in range(4 * g, 4 * g + 4):
                        pe.wait_ge(S["h_norm"], 16 * L + i + 1)
                        nc.tensor.transpose(ps[:, 6 + g % 2, (i % 4) * P:(i % 4 + 1) * P], hn[:, i % 2, :],
                                            K.ident[:, :]).then_inc(S["h_tp"], 1)

                def down(g):
                    pe.wait_ge(S["gate"], 12 * L + NC_ * (g + 1))
                    past(pe, S["y_mlp"], 4 * L + g - 1)
                    for j in range(4):
                        for c, (_, hc) in enumerate(CH):
                            rows = hc + (c == NC_ - 1)
                            mm = nc.tensor.matmul(ps[:, 4 + g % 2, j * P:(j + 1) * P],
                                                  hid[0:rows, g % 2, c, j * P:(j + 1) * P], w2[0:rows, c, :],
                                                  start=(c == 0), stop=(c == NC_ - 1))
                    mm.then_inc(S["w2_mm"], 1)

                pe.wait_ge(S["w_mlp"], 208 * (L + 1))
                pe.wait_ge(S["y_attn"], 16 * (L + 1))
                turn_h(0)
                for g in range(NT // 4):
                    if g + 1 < NT // 4:
                        turn_h(g + 1)
                    pe.wait_ge(S["hT"], 4 * L + g + 1)
                    for c, (h0, hc) in enumerate(CH):
                        u = NC_ * g + c
                        past(pe, S["gate"], 12 * L + u - 1)
                        for half in range(2):
                            mm = nc.tensor.matmul(ps[0:hc, 2 * (u % 2) + half, :],
                                                  w1[:, half * HID + h0:half * HID + h0 + hc],
                                                  hT[:, 512 * g:512 * g + 512], start=True, stop=True)
                        mm.then_inc(S["w1_mm"], 1)
                        if c == 0 and g >= 1:
                            down(g - 1)
                down(NT // 4 - 1)
                pe.wait_ge(S["y_mlp"], 4 * (L + 1))


CHUNKS = (0, 2, 3, 1)
WORK = [(c, g) for c in CHUNKS for g in range(NG)]


def key_steps(n):
    return 4 * (WORK[n][0] + 1)


def max_units(n):
    c = WORK[n][0]
    return [(j, h, part) for j in range(4) for h in range(HG) for part in range(c + 1)]


def max_share(n, k):
    units, before = max_units(n), key_steps(n - 1) if n else 1
    over = max(before - 2, 1)
    lo, hi = min(k, over) * len(units) // over, min(k + 1, over) * len(units) // over
    return list(enumerate(units))[lo:hi]


MAX_BASE = [sum(len(max_units(m)) for m in range(n)) for n in range(len(WORK) + 1)]
KEY_BASE = [sum(key_steps(m) for m in range(n)) for n in range(len(WORK) + 1)]


def causal_block(nc, K, S, dram):
    with ExitStack() as stack:
        def sb(name, shape, dt=F32):
            return stack.enter_context(nc.sbuf_tensor(f"c_{name}", shape, dt))

        qs = sb("qs", [P, NT, H2, SLOT])
        ks = sb("ks", [P, NT, H2, SLOT])
        vv = sb("vv", [P, NT, H2, SLOT])
        kT = sb("kT", [P, NG, T], F32R)
        qmT = sb("qmT", [P, 2, 512], F32R)
        qT = sb("qT", [P, 2, 512], F32R)
        pr = sb("pr", [P, 2, HG, 512])
        watt = sb("watt", [P, 3 * C])
        batt = sb("batt", [P, 3 * C])
        wproj = sb("wproj", [P, C])
        bproj = sb("bproj", [P, C])
        r2c = sb("r2c", [P, NT, D2 // 2])
        r2s = sb("r2s", [P, NT, 2, D2 // 2])
        cmf = sb("cmf", [P, 2, P])
        cmask = sb("cmask", [P, 2, P], BF16)
        ys = sb("ys", [P, 2, C])
        ht = sb("ht", [P, 2, C])
        raw = sb("raw", [P, 2, 3 * C])
        ca = sb("ca", [P, 2, 2 * C])
        cb = sb("cb", [P, 2 * C])
        rr = sb("rr", [P, 2, 2 * C])
        hi = sb("hi", [P, 2, 2 * C], F32R)
        mparts = sb("mparts", [P, 2, 4 * HG, NQ])
        m16 = sb("m16", [P, 4 * HG])
        neg = sb("neg", [P, 4 * HG])
        neghi = sb("neghi", [P, 4 * HG], F32R)
        acc = sb("acc", [P, 512])
        rsum = sb("rsum", [P, 4, HG])
        o = sb("o", [P, NT, C])
        oT = sb("oT", [P, 2, 512])
        ps = stack.enter_context(nc.psum_tensor("c_ps", [P, 8, 512], F32))
        MX, ACC, MISC = 4, 6, 7

        def slots(ap):
            return ap.rearrange("p (h d) -> p h d", d=D2)

        block = stack.enter_context(nc.Block())

        @block.sync
        def _(sp):
            sp.dma_start(watt[:, :], dram["W_attn"]).then_inc(S["c_in"], 16)
            sp.dma_start(wproj[:, :], dram["W_proj"]).then_inc(S["c_in"], 16)
            sp.dma_start(batt[:, :], dram["b_attn"].partition_broadcast(P)).then_inc(S["c_in"], 16)
            sp.dma_start(bproj[:, :], dram["b_proj"].partition_broadcast(P)).then_inc(S["c_in"], 16)
            sp.dma_start(cmf[:, :, :], dram["causal_mask"]).then_inc(S["c_in"], 16)
            sp.dma_start(r2c[:, :, :], dram["rope2_c"]).then_inc(S["c_in"], 16)
            sp.dma_start(r2s[:, :, :, :], dram["rope2_s"]).then_inc(S["c_in"], 16)

        @block.gpsimd
        def _(pool):
            nc.gpsimd.memset(qs[:, :, :, MROW:], 0.0).then_inc(S["c_zero"], 1)
            nc.gpsimd.memset(ks[:, :, :, MROW:MROW + 2], 1.0).then_inc(S["c_zero"], 1)
            nc.gpsimd.memset(ks[:, :, :, MROW + 2:], 0.0).then_inc(S["c_zero"], 1)
            nc.gpsimd.memset(vv[:, :, :, D2:D2 + 1], 1.0).then_inc(S["c_zero"], 1)
            nc.gpsimd.memset(vv[:, :, :, D2 + 1:], 0.0).then_inc(S["c_zero"], 1)
            pool.wait_ge(S["c_in"], 16 * 7)
            pool.wait_ge(S["ln_y"], 32)

            def stage(i, p):
                past(pool, S["c_tp"], i - 1)
                nc.gpsimd.tensor_copy(ys[:, p, :], K.y[:, i, :]).then_inc(S["c_ys"], 1)

            def cosine(i, p):
                pool.wait_ge(S["c_biased"], i + 1)
                past(pool, S["c_rot"], i - 1)
                nc.gpsimd.tensor_tensor(
                    ca[:, p].rearrange("p (m d) -> p m d", d=4), raw[:, p, 0:2 * C].rearrange("p (m d) -> p m d", d=4),
                    r2c[:, i].rearrange("p (o d) -> p o d", o=1).broadcast_to((P, 64, 4)),
                    ALU.mult).then_inc(S["c_cos"], 1)

            stage(0, 0)
            stage(1, 1)
            cosine(0, 0)
            with pool.Fori(1, NT // 2) as pair:
                for p in range(2):
                    stage(2 * pair + p, p)
                    cosine(2 * pair + p - 1, 1 - p)
            cosine(NT - 1, 1)
            nc.gpsimd.tensor_tensor(
                K.x[:, :, :], K.x[:, :, :],
                bproj[:, :].rearrange("p (o c) -> p o c", o=1).broadcast_to((P, NT, C)), ALU.add).then_inc(S["c_xb"], 1)

        @block.vector
        def _(dve):
            dve.wait_ge(S["x_ffn"], 1)
            dve.wait_ge(S["c_in"], 16 * 7)
            nc.vector.tensor_copy(cmask[:, :, :], cmf[:, :, :]).then_inc(S["c_bias"], 1)
            ln_vector(dve, nc, K, S, 1)

            for i, p in tiles(dve):
                dve.wait_ge(S["c_qkv"], i + 1)
                past(dve, S["c_cos"], i - 1)
                past(dve, S["c_v"], i - 1)
                nc.vector.tensor_tensor(raw[:, p], ps[:, p, 0:3 * C], batt[:, :], ALU.add).then_inc(S["c_biased"], 1)
                dve.wait_ge(S["c_biased"], i + 1)
                past(dve, S["c_rot"], i)
                nc.vector.tensor_tensor(
                    cb[:, :].rearrange("p (h a d) -> p h a d", a=2, d=4),
                    raw[:, p, 0:2 * C].rearrange("p (h a d) -> p h a d", a=2, d=4)[:, :, ::-1, :],
                    r2s[:, i].rearrange("p (o a) d -> p o a d", o=1).broadcast_to((P, 32, 2, 4)),
                    ALU.mult).then_inc(S["c_sin"], 1)
                dve.wait_ge(S["c_sin"], i + 1)
                dve.wait_ge(S["c_cos"], i + 1)
                past(dve, S["c_lo"], 2 * i - 2)
                nc.vector.tensor_tensor(rr[:, p], ca[:, p], cb[:, :], ALU.add).then_inc(S["c_rot"], 1)
                dve.wait_ge(S["c_rot"], i + 1)
                past(dve, S["c_ks"], i - 1)
                nc.vector.tensor_copy(hi[:, p], rr[:, p]).then_inc(S["c_hi"], 1)
                dve.wait_ge(S["c_hi"], i + 1)
                nc.vector.tensor_tensor(qs[:, i, :, 16:24], slots(rr[:, p, 0:C]), slots(hi[:, p, 0:C].bitcast(F32)),
                                        ALU.subtract).then_inc(S["c_lo"], 1)
                nc.vector.tensor_tensor(ks[:, i, :, 8:16], slots(rr[:, p, C:]), slots(hi[:, p, C:].bitcast(F32)),
                                        ALU.subtract).then_inc(S["c_lo"], 1)

            def finish_max(n):
                c, g = WORK[n]
                dve.wait_ge(S["c_max"], MAX_BASE[n + 1])
                past(dve, S["c_neg"], n)
                nc.vector.tensor_reduce(m16[:, :], mparts[:, n % 2, :, 0:c + 1], AX_X, ALU.max).then_inc(S["c_mfin"], 1)
                dve.wait_ge(S["c_mfin"], n + 1)
                past(dve, S["c_mlo"], n)
                nc.vector.tensor_scalar(neg[:, :], m16[:, :], -1.0, None, ALU.mult).then_inc(S["c_neg"], 1)
                dve.wait_ge(S["c_neg"], n + 1)
                nc.vector.tensor_copy(neghi[:, :], neg[:, :]).then_inc(S["c_neghi"], 1)
                dve.wait_ge(S["c_neghi"], n + 1)
                dve.wait_ge(S["c_qm_tp"], n + 1)
                high = neghi[:, :].bitcast(F32).rearrange("p (j h) -> p j h", h=HG)
                nc.vector.tensor_copy(qs[:, 4 * c:4 * c + 4, HG * g:HG * (g + 1), MROW], high).then_inc(S["c_mrow"], 1)
                nc.vector.tensor_tensor(qs[:, 4 * c:4 * c + 4, HG * g:HG * (g + 1), MROW + 1],
                                        neg[:, :].rearrange("p (j h) -> p j h", h=HG), high,
                                        ALU.subtract).then_inc(S["c_mlo"], 1)

            def finish_out(n):
                c, g = WORK[n]
                dve.wait_ge(S["c_pv"], KEY_BASE[n + 1])
                past(dve, S["c_acc_tp"], n)
                nc.vector.tensor_copy(acc[:, :], ps[:, ACC, :]).then_inc(S["c_acc"], 1)
                dve.wait_ge(S["c_acc_tp"], n + 1)
                past(dve, S["c_o"], n)
                by_head = ps[:, MISC].rearrange("p (j h d) -> p j h d", j=4, d=SLOT)
                nc.vector.reciprocal(rsum[:, :, :], by_head[:, :, :, D2]).then_inc(S["c_rsum"], 1)
                dve.wait_ge(S["c_rsum"], n + 1)
                nc.vector.tensor_tensor(
                    o[:, 4 * c:4 * c + 4, 32 * g:32 * (g + 1)].rearrange("p j (h d) -> p j h d", d=D2),
                    by_head[:, :, :, 0:D2],
                    rsum[:, :, :].rearrange("p j (h o) -> p j h o", o=1).broadcast_to((P, 4, HG, D2)),
                    ALU.mult).then_inc(S["c_o"], 1)

            for n in range(len(WORK) + 1):
                if n < len(WORK):
                    for u, (j, h, part) in enumerate(max_units(n)):
                        unit = MAX_BASE[n] + u
                        width = 512 if part < WORK[n][0] else P * (j + 1)
                        dve.wait_ge(S["c_mx"], unit + 1)
                        if n >= 2:
                            dve.wait_ge(S["c_mfin"], n - 1)
                        nc.vector.tensor_reduce(mparts[:, n % 2, HG * j + h, part:part + 1],
                                                ps[:, MX + unit % 2, 0:width], AX_X, ALU.max).then_inc(S["c_max"], 1)
                    finish_max(n)
                if n >= 1:
                    finish_out(n - 1)

            dve.wait_ge(S["c_xb"], 1)
            for b in range(4):
                dve.wait_ge(S["c_proj"], b + 1)
                xb = K.x[:, 4 * b:4 * b + 4].rearrange("p i c -> p (i c)")
                nc.vector.tensor_tensor(xb, xb, ps[:, 2 + b % 2, :], ALU.add).then_inc(S["x_attn"], 1)

        @block.scalar
        def _(act):
            ln_scalar(act, nc, K, S, 1)
            act.wait_ge(S["c_zero"], 5)
            for i, p in tiles(act):
                act.wait_ge(S["c_tp"], i + 1)
                past(act, S["c_qkv"], i - 1)
                nc.scalar.copy(ht[:, p, :], ps[:, 2 + p, 0:P]).then_inc(S["c_ht"], 1)
                act.wait_ge(S["c_biased"], i + 1)
                nc.scalar.copy(vv[:, i, :, 0:D2], slots(raw[:, p, 2 * C:])).then_inc(S["c_v"], 1)
                act.wait_ge(S["c_hi"], i + 1)
                high = hi[:, p, :].bitcast(F32)
                nc.scalar.copy(qs[:, i, :, 0:16].rearrange("p h (a d) -> p h a d", a=2),
                               high[:, 0:C].rearrange("p (h o d) -> p h o d", o=1, d=D2)
                               .broadcast_to((P, H2, 2, D2))).then_inc(S["c_qs"], 1)
                nc.scalar.copy(ks[:, i, :, :].rearrange("p h (a d) -> p h a d", a=2)[:, :, :, 0:D2],
                               high[:, C:].rearrange("p (h o d) -> p h o d", o=1, d=D2)
                               .broadcast_to((P, H2, 2, D2))).then_inc(S["c_ks"], 1)
            for u in range(4 * NG):
                act.wait_ge(S["c_kt_tp"], u + 1)
                nc.scalar.copy(kT[:, u // 4, 512 * (u % 4):512 * (u % 4) + 512], ps[:, u % 4, :]).then_inc(S["c_kt"], 1)

            def out_qm(n):
                act.wait_ge(S["c_qm_tp"], n + 1)
                past(act, S["c_mx"], MAX_BASE[n - 1] if n else 0)
                nc.scalar.copy(qmT[:, n % 2], ps[:, MISC]).then_inc(S["c_qm"], 1)

            out_qm(0)
            for n in range(len(WORK) + 1):
                if n >= 1:
                    c = WORK[n - 1][0]
                    for kt in range(key_steps(n - 1)):
                        step = KEY_BASE[n - 1] + kt
                        off = P * max(0, kt - 4 * c)
                        for pair in range(2):
                            unit = 2 * step + pair
                            act.wait_ge(S["c_st"], unit + 1)
                            past(act, S["c_pv"], step - 1)
                            nc.scalar.activation(pr[:, step % 2, 2 * pair:2 * pair + 2, off:],
                                                 ps[:, 2 * (unit % 2):2 * (unit % 2) + 2, off:], ACT.Exp,
                                                 scale=float(D2) ** -0.5).then_inc(S["c_exp"], 1)
                if n < len(WORK):
                    act.wait_ge(S["c_q_tp"], n + 1)
                    past(act, S["c_st"], 2 * KEY_BASE[n - 1] if n else 0)
                    nc.scalar.copy(qT[:, n % 2], ps[:, MISC]).then_inc(S["c_q"], 1)
                if n + 1 < len(WORK):
                    out_qm(n + 1)
            for b in range(4):
                act.wait_ge(S["c_ot_tp"], b + 1)
                past(act, S["c_proj"], b - 1)
                nc.scalar.copy(oT[:, b % 2], ps[:, b % 2]).then_inc(S["c_ot"], 1)

        @block.tensor
        def _(pe):
            def turn(i, p):
                pe.wait_ge(S["c_ys"], i + 1)
                past(pe, S["c_ht"], i - 1)
                nc.tensor.transpose(ps[:, 2 + p, 0:P], ys[:, p, :], K.ident[:, :]).then_inc(S["c_tp"], 1)

            def project(i, p):
                pe.wait_ge(S["c_ht"], i + 1)
                past(pe, S["c_biased"], i - 1)
                nc.tensor.matmul(ps[:, p, 0:3 * C], ht[:, p, :], watt[:, :], start=True, stop=True).then_inc(S["c_qkv"], 1)

            pe.wait_ge(S["c_in"], 16 * 7)
            turn(0, 0)
            turn(1, 1)
            project(0, 0)
            with pe.Fori(1, NT // 2) as pair:
                for p in range(2):
                    turn(2 * pair + p, p)
                    project(2 * pair + p - 1, 1 - p)
            project(NT - 1, 1)

            def group(ap, t, g):
                return ap[:, t, HG * g:HG * (g + 1)].rearrange("p h s -> p (h s)")

            pe.wait_ge(S["c_ks"], NT)
            pe.wait_ge(S["c_lo"], 2 * NT)
            pe.wait_ge(S["c_bias"], 1)
            for u in range(4 * NG):
                past(pe, S["c_kt"], u - 3)
                for j in range(4):
                    mm = nc.tensor.transpose(ps[:, u % 4, P * j:P * (j + 1)], group(ks, 4 * (u % 4) + j, u // 4),
                                             K.ident[:, :])
                mm.then_inc(S["c_kt_tp"], 1)

            def turn_queries(n, done):
                c, g = WORK[n]
                for j in range(4):
                    mm = nc.tensor.transpose(ps[:, MISC, P * j:P * (j + 1)], group(qs, 4 * c + j, g), K.ident[:, :])
                mm.then_inc(done, 1)

            def max_unit(n, u, j, h, part):
                c, g = WORK[n]
                unit = MAX_BASE[n] + u
                last = part == c
                width = P * (j + 1) if last else 512
                rows = slice(SLOT * h, SLOT * h + MROW)
                past(pe, S["c_max"], unit - 1)
                out = ps[:, MX + unit % 2, :]
                mm = nc.tensor.matmul(out[:, 0:width], qmT[rows, n % 2, P * j:P * (j + 1)],
                                      kT[rows, g, 512 * part:512 * part + width], start=True, stop=True)
                if last:
                    mm = nc.tensor.matmul(out[:, width - P:width], K.identb[:, :], cmask[:, 0, :],
                                          start=False, stop=True, skip_group_check=True)
                mm.then_inc(S["c_mx"], 1)

            def score_pair(n, kt, pair):
                c, g = WORK[n]
                unit = 2 * (KEY_BASE[n] + kt) + pair
                off = P * max(0, kt - 4 * c)
                past(pe, S["c_exp"], unit - 1)
                for a in range(2):
                    rows = slice(SLOT * (2 * pair + a), SLOT * (2 * pair + a) + MROW + 2)
                    out = ps[:, 2 * (unit % 2) + a, :]
                    mm = nc.tensor.matmul(out[:, off:], kT[rows, g, P * kt:P * (kt + 1)], qT[rows, n % 2, off:],
                                          start=True, stop=True)
                    if kt >= 4 * c:
                        mm = nc.tensor.matmul(out[:, off:off + P], K.identb[:, :], cmask[:, 1, :],
                                              start=False, stop=True, skip_group_check=True)
                mm.then_inc(S["c_st"], 1)

            def weigh(n, kt):
                c, g = WORK[n]
                step = KEY_BASE[n] + kt
                off = P * max(0, kt - 4 * c)
                pe.wait_ge(S["c_exp"], 2 * step + 2)
                if kt == 0:
                    past(pe, S["c_acc"], n)
                for h in range(HG):
                    mm = nc.tensor.matmul(ps[SLOT * h:SLOT * (h + 1), ACC, off:], vv[:, kt, HG * g + h, :],
                                          pr[:, step % 2, h, off:], start=(kt == 0), stop=(kt >= 4 * c),
                                          skip_group_check=True)
                mm.then_inc(S["c_pv"], 1)

            turn_queries(0, S["c_qm_tp"])
            for n in range(len(WORK) + 1):
                if n < len(WORK):
                    pe.wait_ge(S["c_qm"], n + 1)
                if n >= 1:
                    pe.wait_ge(S["c_q"], n)
                    for kt in range(key_steps(n - 1)):
                        score_pair(n - 1, kt, 0)
                        if n < len(WORK):
                            for u, (j, h, part) in max_share(n, kt):
                                max_unit(n, u, j, h, part)
                        score_pair(n - 1, kt, 1)
                        if kt >= 1:
                            weigh(n - 1, kt - 1)
                    weigh(n - 1, key_steps(n - 1) - 1)
                else:
                    for u, (j, h, part) in enumerate(max_units(0)):
                        max_unit(0, u, j, h, part)
                if n < len(WORK):
                    pe.wait_ge(S["c_mrow"], n + 1)
                    pe.wait_ge(S["c_mlo"], n + 1)
                    pe.wait_ge(S["c_qm"], n + 1)
                    turn_queries(n, S["c_q_tp"])
                if n >= 1:
                    pe.wait_ge(S["c_acc"], n)
                    if n < len(WORK):
                        pe.wait_ge(S["c_q"], n + 1)
                    for j in range(4):
                        mm = nc.tensor.transpose(ps[:, MISC, P * j:P * (j + 1)], acc[:, P * j:P * (j + 1)],
                                                 K.ident[:, :])
                    mm.then_inc(S["c_acc_tp"], 1)
                if n + 1 < len(WORK):
                    pe.wait_ge(S["c_q"], n + 1)
                    past(pe, S["c_o"], n)
                    turn_queries(n + 1, S["c_qm_tp"])

            pe.wait_ge(S["c_o"], len(WORK))
            for b in range(4):
                past(pe, S["c_ot"], b - 1)
                for j in range(4):
                    mm = nc.tensor.transpose(ps[:, b % 2, P * j:P * (j + 1)], o[:, 4 * b + j, :], K.ident[:, :])
                mm.then_inc(S["c_ot_tp"], 1)
                pe.wait_ge(S["c_ot"], b + 1)
                past(pe, S["x_attn"], b - 1)
                for j in range(4):
                    mm = nc.tensor.matmul(ps[:, 2 + b % 2, P * j:P * (j + 1)], oT[:, b % 2, P * j:P * (j + 1)],
                                          wproj[:, :], start=True, stop=True)
                mm.then_inc(S["c_proj"], 1)


def build(nc, dram):
    with ExitStack() as stack:
        K = Keep(nc, stack)
        S = {name: stack.enter_context(nc.semaphore(name)) for name in SEMS.split()}
        S["v_stage"] = [stack.enter_context(nc.semaphore(f"v_stage{p}")) for p in range(2)]
        ffn_block(nc, K, S, dram, 0)
        causal_block(nc, K, S, dram)
        ffn_block(nc, K, S, dram, 1)


SEMS = """x_in consts rope_in const_b x_attn x_ffn stored
ln_stat ln_aggr ln_var ln_sd ln_rstd ln_y
w_qkv w_o w_mlp shift_zero shifted v_ones
ys tp ht qkv squares v_out sumsq qk_out norms norm_max inv_norm
unit cos_part sin_part rot tq qkt scores row_max less_max exps ptr pt pv row_sum o_norm otr ot wo_mm y_attn
hid_ones h_stat h_aggr h_var h_sd h_rstd h_norm h_tp hT w1_mm gelu gate w2_mm y_mlp
c_in c_zero c_bias c_ys c_tp c_ht c_qkv c_biased c_cos c_sin c_rot c_hi c_qs c_ks c_lo c_v
c_kt_tp c_kt c_qm_tp c_qm c_mx c_max c_mfin c_neg c_neghi c_mrow c_mlo c_q_tp c_q
c_st c_exp c_pv c_acc c_acc_tp c_rsum c_o c_ot_tp c_ot c_proj c_xb"""


def constants():
    f = np.float32
    t = np.arange(T, dtype=f)
    half = np.arange(0, DH, 2, dtype=f)
    inv = (f(1.0) / np.power(f(10000.0), half / f(DH), dtype=f)).astype(f)
    freq = t[:, None] * inv[None, :]
    base = (half + f(0.4 * DH)) / f(1.4 * DH)
    power = (t - f(T // 2)) / f(WINDOW // 2)
    scale = np.power(base[None, :], power[:, None], dtype=f)
    c, s = np.cos(freq), np.sin(freq)
    cq, sq = f(QK_SCALE) * (c * scale), f(QK_SCALE) * (s * scale)
    ck, sk = c / scale, s / scale
    by_tile = lambda a: np.ascontiguousarray(a.reshape(NT, P, *a.shape[1:]).swapaxes(0, 1).astype(f))
    rope_c = by_tile(np.stack([cq, ck], 1))
    rope_s = by_tile(np.stack([np.stack([sq, -sq], 1), np.stack([sk, -sk], 1)], 1))
    r = np.arange(P)[:, None]
    k = np.arange(P)[None, :]
    w, q = r // 64, r % 64
    i = 64 * w + q
    j = np.where((w == 0) & (k >= 64), k - P, k)
    banned = (j > i) | (j < i - WINDOW)
    local = np.stack([np.where(banned | (j < 0), MASKED, 0.0), np.where(banned, MASKED, 0.0)], 1).astype(f)
    frac = (f(2.0) * np.arange(D2 // 2, dtype=f)) / f(D2)
    ang = t[:, None] / np.power(f(1250.0), frac, dtype=f)[None, :]
    c2, s2 = np.cos(ang), np.sin(ang)
    causal = np.stack([np.where(k > r, MASKED, 0.0), np.where(r > k, MASKED, 0.0)], 1).astype(f)
    return {"ident": np.eye(P, dtype=f), "local_mask": local, "rope_c": rope_c, "rope_s": rope_s,
            "rope2_c": by_tile(c2), "rope2_s": by_tile(np.stack([-s2, s2], 1)), "causal_mask": causal}


_INS = {"x": "L0_attn_x", "W_attn": "L0_attn_W_attn", "b_attn": "L0_attn_b_attn", "W_proj": "L0_attn_W_proj",
        "b_proj": "L0_attn_b_proj", "wqkv": "L0_ffn_wqkv", "q_scale": "L0_ffn_q_scale", "k_scale": "L0_ffn_k_scale",
        "wo": "L0_ffn_wo", "ln_g": "L0_ffn_ln_g", "ln_b": "L0_ffn_ln_b", "w1": "L0_ffn_w1", "b1": "L0_ffn_b1",
        "w2": "L0_ffn_w2", "b2": "L0_ffn_b2"}


def kernel(**inputs):
    import concourse.bacc as _bacc
    from concourse.bass_utils import run_bass_kernel_spmd as _run

    nc = _bacc.Bacc("TRN2", target_bir_lowering=False, num_devices=1)
    arrays, dram = {}, {}
    given = {short: np.ascontiguousarray(inputs[name]) for short, name in _INS.items()}
    given["x"] = given["x"].reshape(T, C)
    for name, a in {**given, **constants()}.items():
        arrays[f"in_{name}"] = a
        dram[name] = nc.dram_tensor(f"in_{name}", a.shape, mybir.dt.from_np(a.dtype), kind="ExternalInput").ap()
    dram["out"] = nc.dram_tensor("out_0", (T, C), F32, kind="ExternalOutput").ap()
    build(nc, dram)
    r = _run(nc, [arrays], core_ids=[0])
    return r.results[0]["out_0"].reshape(1, T, C)
```

```python
from contextlib import ExitStack

import numpy as np
import concourse.bass as bass
from concourse import mybir

F32 = mybir.dt.float32
F32R = mybir.dt.float32r
BF16 = mybir.dt.bfloat16
ALU = mybir.AluOpType
ACT = mybir.ActivationFunctionType
AX_X = mybir.AxisListType.X

P = 128
T = 2048
C = 128
NT = T // P
LN_EPS = 1e-5
MASKED = -1.0e30

DEPTH = 2
HEADS, DH, WINDOW = 8, 64, 64
INNER = HEADS * DH
HID = int(C * 4 * 2 / 3)
CH = [(0, 128), (128, 128), (256, HID - 256)]
NC_ = len(CH)
QK_SCALE = 8.0

H2, D2 = 16, 8
SLOT = 32
NG = 4
HG = H2 // NG
NQ = T // 512
MROW = 24


def past(eng, sem, value):
    if isinstance(value, int) and value <= 0:
        return
    eng.wait_ge(sem, value)


def steps(eng, first, last):
    with eng.Fori(first // 2, last // 2) as pair:
        for slot in range(2):
            yield 2 * pair + slot, slot


def tiles(eng, n=NT):
    for i in range(2):
        yield i, i
    yield from steps(eng, 2, n)


def ln_vector(dve, nc, K, S, n):
    for i, _ in steps(dve, 0, NT):
        nc.vector.bn_stats(K.st6[:, i, :], K.x[:, i, :]).then_inc(S["ln_stat"], 1)
    dve.wait_ge(S["ln_stat"], 16 * (n + 1))
    for i in range(NT):
        nc.vector.bn_aggr(K.mv[:, i, :], K.st6[:, i, :]).then_inc(S["ln_aggr"], 1)
    dve.wait_ge(S["ln_aggr"], 16 * (n + 1))
    nc.vector.tensor_scalar(K.vare[:, :], K.mv[:, :, 1], LN_EPS, None, ALU.add).then_inc(S["ln_var"], 1)
    dve.wait_ge(S["ln_sd"], n + 1)
    nc.vector.reciprocal(K.rstd[:, :], K.sd[:, :]).then_inc(S["ln_rstd"], 1)
    dve.wait_ge(S["ln_rstd"], n + 1)
    for i, p in tiles(dve):
        nc.vector.tensor_scalar(K.y[:, i, :], K.x[:, i, :], K.mv[:, i, 0:1], K.rstd_at(i),
                                ALU.subtract, ALU.mult).then_inc(S["ln_y"], 1)


def ln_scalar(act, nc, K, S, n):
    act.wait_ge(S["ln_var"], n + 1)
    nc.scalar.activation(K.sd[:, :], K.vare[:, :], ACT.Sqrt).then_inc(S["ln_sd"], 1)


class Keep:

    def __init__(self, nc, stack):
        def sb(name, shape, dt=F32):
            return stack.enter_context(nc.sbuf_tensor(name, shape, dt))

        self.x = sb("x_tok", [P, NT, C])
        self.y = sb("y_tok", [P, NT, C])
        self.ident = sb("ident", [P, P])
        self.identb = sb("identb", [P, P], BF16)
        self.st6 = sb("st6", [P, NT, 6])
        self.mv = sb("mv", [P, NT, 2])
        self.vare = sb("vare", [P, NT])
        self.sd = sb("sd", [P, NT])
        self.rstd = sb("rstd", [P, NT])

    def rstd_at(self, i):
        return self.rstd[:, :].rearrange("p (i o) -> p i o", o=1)[:, i, :]


def ffn_block(nc, K, S, dram, which):
    with ExitStack() as stack:
        def sb(name, shape, dt=F32):
            return stack.enter_context(nc.sbuf_tensor(f"{name}_{which}", shape, dt))

        qk = sb("qk", [P, NT, 2 * INNER])
        v = sb("v", [P, NT + 1, HEADS, DH + 1])
        rc = sb("rc", [P, NT, 2, DH // 2])
        rs = sb("rs", [P, NT, 2, 2, DH // 2])
        wqkv = sb("wqkv", [P, 3 * INNER])
        wo = sb("wo", [P, INNER // P, C])
        w1 = sb("w1", [P, 2 * HID])
        w2 = sb("w2", [P, NC_, C])
        b1 = sb("b1", [P, 2 * NC_])
        lng = sb("lng", [P, 1])
        lnb = sb("lnb", [P, 1])
        qks = sb("qks", [P, 2, DH])
        maskf = sb("maskf", [P, 2, P])
        mask = sb("mask", [P, NT, P], BF16)
        ss = sb("ss", [P, NT, 2 * HEADS])
        nrm = sb("nrm", [P, NT, 2 * HEADS])
        mx = sb("mx", [P, 2, HEADS])
        rsum = sb("rsum", [P, 2, HEADS])
        ta = sb("ta", [P, 2, 2 * INNER])
        tb = sb("tb", [P, 2 * INNER])
        qk2 = sb("qk2", [P, 2, 2 * INNER])
        qkt = sb("qkt", [P, 2, 2 * INNER // P, P])
        sS = sb("sS", [P, 2 * HEADS * P])
        pt = sb("pt", [P, HEADS, P])
        ot = sb("ot", [P, INNER])
        oT = sb("oT", [P, INNER // P, P])
        vs = sb("vs", [P, 2, HEADS, DH + 1])
        ve = sb("ve", [P, 2, HEADS, DH + 1])
        ps = stack.enter_context(nc.psum_tensor(f"ps_{which}", [P, 8, 512], F32))

        hs = sS[:, :].rearrange("p (i c) -> p i c", c=C)
        prob = sS[:, :].rearrange("p (s h k) -> p s h k", s=2, h=HEADS)
        sq = qkt[:, :, :, :].rearrange("p s b t -> p s (b t)")
        ys = pt[:, 0:2, :]
        ht = pt[:, 2:4, :]
        flat = qk[:, :, :].rearrange("p i n -> p (i n)")
        hT = flat[:, 0:T]
        hid = flat[:, T:T + 2 * NC_ * 512].rearrange("p (s c t) -> p s c t", s=2, c=NC_)
        gel = flat[:, T + 3072:T + 4096].rearrange("p (s t) -> p s t", s=2)
        hn = flat[:, T + 4096:T + 4352].rearrange("p (s t) -> p s t", s=2)

        def qk_view(ap):
            return ap.rearrange("p (z m d) -> p z m d", z=2, d=DH // 2)

        def o_bank(ap):
            return ap[:, 6:8, 0:4 * (DH + 1)].rearrange("p b (h d) -> p b h d", d=DH + 1)

        block = stack.enter_context(nc.Block())

        @block.sync
        def _(sp):
            def load_qkv(l, L):
                past(sp, S["qkv"], 16 * L)
                past(sp, S["qk_out"], 16 * L)
                sp.dma_start(wqkv[:, :], dram["wqkv"][l]).then_inc(S["w_qkv"], 16)
                sp.dma_start(qks[:, 0, :], dram["q_scale"][l:l + 1, :].partition_broadcast(P)
                             .rearrange("p o d -> p (o d)")).then_inc(S["w_qkv"], 16)
                sp.dma_start(qks[:, 1, :], dram["k_scale"][l:l + 1, :].partition_broadcast(P)
                             .rearrange("p o d -> p (o d)")).then_inc(S["w_qkv"], 16)

            def load_wo(l, L):
                past(sp, S["wo_mm"], 16 * L)
                sp.dma_start(wo[:, :, :], dram["wo"][l].rearrange("(b p) n -> p b n", p=P)).then_inc(S["w_o"], 16)

            def load_mlp(l, L):
                past(sp, S["w2_mm"], 4 * L)
                past(sp, S["gelu"], 12 * L)
                past(sp, S["gate"], 12 * L)
                col = lambda ap: ap.rearrange("(p o) -> p o", o=1)
                sp.dma_start(w1[:, :], dram["w1"][l]).then_inc(S["w_mlp"], 16)
                sp.dma_start(lng[:, :], col(dram["ln_g"][l])).then_inc(S["w_mlp"], 16)
                sp.dma_start(lnb[:, :], col(dram["ln_b"][l])).then_inc(S["w_mlp"], 16)
                for c, (h0, hc) in enumerate(CH):
                    sp.dma_start(w2[0:hc, c, :], dram["w2"][l, h0:h0 + hc, :]).then_inc(S["w_mlp"], 16)
                    for half in range(2):
                        sp.dma_start(b1[0:hc, half * NC_ + c:half * NC_ + c + 1],
                                     col(dram["b1"][l, half * HID + h0:half * HID + h0 + hc])
                                     ).then_inc(S["w_mlp"], 16)
                hc = CH[-1][1]
                sp.dma_start(w2[hc:hc + 1, NC_ - 1, :], dram["b2"][l:l + 1, :]).then_inc(S["w_mlp"], 16)

            def shift():
                sp.dma_start(hs[:, :, 0:C // 2], K.y[:, :, 0:C // 2]).then_inc(S["shifted"], 16)
                sp.dma_start(hs[1:P, :, C // 2:C], K.y[0:P - 1, :, C // 2:C]).then_inc(S["shifted"], 16)
                sp.dma_start(hs[0:1, 1:NT, C // 2:C], K.y[P - 1:P, 0:NT - 1, C // 2:C]).then_inc(S["shifted"], 16)

            if which == 0:
                sp.dma_start(K.x[:, :, :], dram["x"].rearrange("(i p) c -> p i c", p=P)).then_inc(S["x_in"], 16)
                sp.dma_start(K.ident[:, :], dram["ident"]).then_inc(S["consts"], 16)
            sp.dma_start(maskf[:, :, :], dram["local_mask"]).then_inc(S["consts"], 16)
            sp.dma_start(rc[:, :, :, :], dram["rope_c"]).then_inc(S["rope_in"], 16)
            sp.dma_start(rs[:, :, :, :, :], dram["rope_s"]).then_inc(S["rope_in"], 16)
            load_qkv(0, DEPTH * which)
            load_wo(0, DEPTH * which)
            load_mlp(0, DEPTH * which)
            for l in range(DEPTH):
                L = DEPTH * which + l
                if l == 0:
                    sp.wait_ge(S["ln_y"], 16 * (2 * which + 1))
                else:
                    sp.wait_ge(S["y_mlp"], 4 * L)
                sp.wait_ge(S["shift_zero"], 2 * L + 1)
                shift()
                sp.wait_ge(S["v_out"], 16 * (L + 1))
                if l + 1 < DEPTH:
                    load_qkv(l + 1, L + 1)
                if l == 0:
                    sp.wait_ge(S["v_ones"], 2 * (which + 1))
                for i, p in tiles(sp):
                    past(sp, S["pv"], 16 * L + i - 1)
                    sp.dma_start(vs[:, p], v[:, i + 1]).then_inc(S["v_stage"][p], 16)
                    sp.dma_start(ve[0:64, p], v[0:64, i + 1]).then_inc(S["v_stage"][p], 16)
                    sp.dma_start(ve[64:P, p], v[64:P, i]).then_inc(S["v_stage"][p], 16)
                sp.wait_ge(S["y_attn"], 16 * (L + 1))
                sp.wait_ge(S["shift_zero"], 2 * L + 2)
                shift()
                if l + 1 < DEPTH:
                    load_wo(l + 1, L + 1)
                    load_mlp(l + 1, L + 1)
            if which == 1:
                sp.wait_ge(S["x_ffn"], which + 1)
                sp.dma_start(dram["out"].rearrange("(i p) c -> p i c", p=P), K.x[:, :, :]).then_inc(S["stored"], 16)
                sp.wait_ge(S["stored"], 16)

        @block.gpsimd
        def _(pool):
            nc.gpsimd.memset(v[:, 1:, :, DH:], 1.0).then_inc(S["v_ones"], 1)
            nc.gpsimd.memset(v[:, 0], 0.0).then_inc(S["v_ones"], 1)
            for l in range(DEPTH):
                L = DEPTH * which + l
                pool.wait_ge(S["shifted"], 48 * (2 * L + 1))
                for i, p in tiles(pool):
                    past(pool, S["tp"], 16 * L + i - 1)
                    nc.gpsimd.tensor_copy(ys[:, p, :], hs[:, i, :]).then_inc(S["ys"], 1)
                pool.wait_ge(S["rope_in"], 32 * (which + 1))
                pool.wait_ge(S["inv_norm"], L + 1)
                for i, p in tiles(pool):
                    nc.gpsimd.tensor_tensor(
                        qk[:, i].rearrange("p (h d) -> p h d", d=DH),
                        qk[:, i].rearrange("p (h d) -> p h d", d=DH),
                        ss[:, i].rearrange("p (h o) -> p h o", o=1).broadcast_to((P, 2 * HEADS, DH)),
                        ALU.mult).then_inc(S["unit"], 1)
                    pool.wait_ge(S["unit"], 16 * L + i + 1)
                    past(pool, S["rot"], 16 * L + i - 1)
                    nc.gpsimd.tensor_tensor(
                        qk_view(ta[:, p]), qk_view(qk[:, i]),
                        rc[:, i].rearrange("p z (o d) -> p z o d", o=1).broadcast_to((P, 2, 16, DH // 2)),
                        ALU.mult).then_inc(S["cos_part"], 1)

        @block.vector
        def _(dve):
            dve.wait_ge(S["x_in"], 16)
            dve.wait_ge(S["consts"], 32 + 16 * which)
            if which == 0:
                nc.vector.tensor_copy(K.identb[:, :], K.ident[:, :]).then_inc(S["const_b"], 1)
            nc.vector.tensor_copy(mask[:, 0, :], maskf[:, 0, :]).then_inc(S["const_b"], 1)
            nc.vector.tensor_copy(
                mask[:, 1:, :], maskf[:, 1:2, :].broadcast_to((P, NT - 1, P))).then_inc(S["const_b"], 1)
            if which == 1:
                dve.wait_ge(S["x_attn"], 4)
            ln_vector(dve, nc, K, S, 2 * which)
            for l in range(DEPTH):
                L = DEPTH * which + l
                if l == 0:
                    dve.wait_ge(S["ln_y"], 16 * (2 * which + 1))
                else:
                    dve.wait_ge(S["y_mlp"], 4 * L)
                nc.vector.memset(hs[0:1, 0, C // 2:C], 0.0).then_inc(S["shift_zero"], 1)
                dve.wait_ge(S["w_qkv"], 48 * (L + 1))
                for i, p in tiles(dve):
                    dve.wait_ge(S["squares"], 16 * L + i + 1)
                    nc.vector.tensor_reduce(ss[:, i], sq[:, p].rearrange("p (h d) -> p h d", d=DH),
                                            AX_X, ALU.add).then_inc(S["sumsq"], 1)
                    dve.wait_ge(S["qkv"], 16 * L + i + 1)
                    nc.vector.tensor_tensor(
                        qk[:, i].rearrange("p (z h d) -> p z h d", z=2, d=DH),
                        ps[:, 2 * p:2 * p + 2].rearrange("p z (h d) -> p z h d", d=DH),
                        qks[:, :, :].rearrange("p z (o d) -> p z o d", o=1).broadcast_to((P, 2, HEADS, DH)),
                        ALU.mult).then_inc(S["qk_out"], 1)
                dve.wait_ge(S["norms"], L + 1)
                nc.vector.tensor_scalar(nrm[:, :, :], nrm[:, :, :], 1e-12, None, ALU.max).then_inc(S["norm_max"], 1)
                dve.wait_ge(S["norm_max"], L + 1)
                nc.vector.reciprocal(ss[:, :, :], nrm[:, :, :]).then_inc(S["inv_norm"], 1)

                def rotate(i, p):
                    dve.wait_ge(S["cos_part"], 16 * L + i + 1)
                    past(dve, S["rot"], 16 * L + i)
                    for z in range(2):
                        half = qk[:, i, z * INNER:(z + 1) * INNER].rearrange("p (h a d) -> p h a d", a=2, d=DH // 2)
                        nc.vector.tensor_tensor(
                            tb[:, z * INNER:(z + 1) * INNER].rearrange("p (h a d) -> p h a d", a=2, d=DH // 2)[:, :, ::-1, :],
                            half,
                            rs[:, i, z].rearrange("p (o a) d -> p o a d", o=1).broadcast_to((P, HEADS, 2, DH // 2)),
                            ALU.mult).then_inc(S["sin_part"], 1)
                    dve.wait_ge(S["sin_part"], 2 * (16 * L + i) + 2)
                    past(dve, S["tq"], 16 * L + i - 1)
                    past(dve, S["tk"], 16 * L + i - 1)
                    nc.vector.tensor_tensor(qk2[:, p], ta[:, p], tb[:, :], ALU.add).then_inc(S["rot"], 1)

                def soften(i, p):
                    scores = ps[:, 2:4].rearrange("p b (h k) -> p (b h) k", k=P)
                    dve.wait_ge(S["scores"], 16 * L + i + 1)
                    nc.vector.tensor_reduce(mx[:, p], scores, AX_X, ALU.max).then_inc(S["row_max"], 1)
                    dve.wait_ge(S["row_max"], 16 * L + i + 1)
                    past(dve, S["ptr"], 16 * L + i - 1)
                    nc.vector.tensor_tensor(
                        prob[:, p], scores,
                        mx[:, p].rearrange("p (h o) -> p h o", o=1).broadcast_to((P, HEADS, P)),
                        ALU.subtract).then_inc(S["less_max"], 1)

                def normalize(i, p):
                    dve.wait_ge(S["pv"], 16 * L + i + 1)
                    nc.vector.reciprocal(
                        rsum[:, p].rearrange("p (b h o) -> p b h o", b=2, o=1),
                        o_bank(ps)[:, :, :, DH:]).then_inc(S["row_sum"], 1)
                    dve.wait_ge(S["row_sum"], 16 * L + i + 1)
                    past(dve, S["otr"], 16 * L + i)
                    nc.vector.tensor_tensor(
                        ot[:, :].rearrange("p (b h d) -> p b h d", b=2, d=DH), o_bank(ps)[:, :, :, 0:DH],
                        rsum[:, p].rearrange("p (b h o) -> p b h o", b=2, o=1).broadcast_to((P, 2, 4, DH)),
                        ALU.mult).then_inc(S["o_norm"], 1)

                def add_attn(i):
                    dve.wait_ge(S["wo_mm"], 16 * L + i + 1)
                    nc.vector.tensor_tensor(K.y[:, i], K.y[:, i], ps[:, 0, 0:C], ALU.add).then_inc(S["y_attn"], 1)

                def step(i, p):
                    if not isinstance(i, int) or i < NT:
                        soften(i, p)
                    if not isinstance(i, int) or 2 <= i:
                        add_attn(i - 2)
                    if not isinstance(i, int) or i + 2 < NT:
                        rotate(i + 2, p)
                    if not isinstance(i, int) or 1 <= i <= NT:
                        normalize(i - 1, 1 - p)

                rotate(0, 0)
                rotate(1, 1)
                for i in range(2):
                    step(i, i)
                for i, p in steps(dve, 2, NT - 2):
                    step(i, p)
                for i in range(NT - 2, NT + 2):
                    step(i, i % 2)

                dve.wait_ge(S["y_attn"], 16 * (L + 1))
                nc.vector.memset(hs[0:1, 0, C // 2:C], 0.0).then_inc(S["shift_zero"], 1)
                nc.vector.memset(hid[64:P, :, NC_ - 1, :], 1.0).then_inc(S["hid_ones"], 1)
                dve.wait_ge(S["hid_ones"], L + 1)
                dve.wait_ge(S["shifted"], 48 * (2 * L + 2))
                for i, _ in steps(dve, 0, NT):
                    nc.vector.bn_stats(K.st6[:, i, :], hs[:, i, :]).then_inc(S["h_stat"], 1)
                dve.wait_ge(S["h_stat"], 16 * (L + 1))
                for i in range(NT):
                    nc.vector.bn_aggr(K.mv[:, i, :], K.st6[:, i, :]).then_inc(S["h_aggr"], 1)
                dve.wait_ge(S["h_aggr"], 16 * (L + 1))
                nc.vector.tensor_scalar(K.vare[:, :], K.mv[:, :, 1], LN_EPS, None, ALU.add).then_inc(S["h_var"], 1)
                dve.wait_ge(S["h_sd"], L + 1)
                nc.vector.reciprocal(K.rstd[:, :], K.sd[:, :]).then_inc(S["h_rstd"], 1)
                dve.wait_ge(S["h_rstd"], L + 1)

                def norm_group(g):
                    for i in range(4 * g, 4 * g + 4):
                        past(dve, S["h_tp"], 16 * L + i - 1)
                        nc.vector.tensor_scalar(hn[:, i % 2, :], hs[:, i, :], K.mv[:, i, 0:1], K.rstd[:, i:i + 1],
                                                ALU.subtract, ALU.mult).then_inc(S["h_norm"], 1)

                def add_mlp(g):
                    dve.wait_ge(S["w2_mm"], 4 * L + g + 1)
                    yg = K.y[:, 4 * g:4 * g + 4].rearrange("p i c -> p (i c)")
                    nc.vector.tensor_tensor(yg, yg, ps[:, 4 + g % 2, :], ALU.add).then_inc(S["y_mlp"], 1)

                dve.wait_ge(S["w_mlp"], 208 * (L + 1))
                norm_group(0)
                for g in range(NT // 4):
                    if g + 1 < NT // 4:
                        norm_group(g + 1)
                    past(dve, S["w2_mm"], 4 * L + g - 1)
                    for c, (_, hc) in enumerate(CH):
                        u = NC_ * g + c
                        dve.wait_ge(S["gelu"], 12 * L + u + 1)
                        nc.vector.scalar_tensor_tensor(
                            out=hid[0:hc, g % 2, c, :], in0=ps[0:hc, 2 * (u % 2), :], scalar=b1[0:hc, c:c + 1],
                            in1=gel[0:hc, u % 2, :], op0=ALU.add, op1=ALU.mult).then_inc(S["gate"], 1)
                    if g >= 1:
                        add_mlp(g - 1)
                add_mlp(NT // 4 - 1)
            dve.wait_ge(S["y_mlp"], 4 * DEPTH * (which + 1))
            nc.vector.scalar_tensor_tensor(
                out=K.x[:, :, :].rearrange("p i c -> p (i c)"), in0=K.y[:, :, :].rearrange("p i c -> p (i c)"),
                scalar=0.5, in1=K.x[:, :, :].rearrange("p i c -> p (i c)"),
                op0=ALU.mult, op1=ALU.add).then_inc(S["x_ffn"], 1)

        @block.scalar
        def _(act):
            ln_scalar(act, nc, K, S, 2 * which)
            for l in range(DEPTH):
                L = DEPTH * which + l
                if l == 0:
                    act.wait_ge(S["v_ones"], 2 * (which + 1))
                for i, p in tiles(act):
                    act.wait_ge(S["tp"], 16 * L + i + 1)
                    past(act, S["qkv"], 16 * L + i - 1)
                    nc.scalar.copy(ht[:, p, :], ps[:, 6 + p, 0:P]).then_inc(S["ht"], 1)
                    act.wait_ge(S["qkv"], 16 * L + i + 1)
                    past(act, S["sumsq"], 16 * L + i - 1)
                    nc.scalar.activation(sq[:, p], ps[:, 2 * p:2 * p + 2].rearrange("p b n -> p (b n)"),
                                         ACT.Square).then_inc(S["squares"], 1)
                    nc.scalar.copy(v[:, i + 1, :, 0:DH],
                                   ps[:, 4 + p].rearrange("p (h d) -> p h d", d=DH)).then_inc(S["v_out"], 1)
                act.wait_ge(S["sumsq"], 16 * (L + 1))
                nc.scalar.activation(nrm[:, :, :], ss[:, :, :], ACT.Sqrt).then_inc(S["norms"], 1)

                def out_turned(i, p, z):
                    act.wait_ge(S["tq" if z == 0 else "tk"], 16 * L + i + 1)
                    past(act, S["scores"], 16 * L + i)
                    nc.scalar.copy(qkt[:, p, 4 * z:4 * z + 4], ps[:, z].rearrange("p (c t) -> p c t", t=P)
                                   ).then_inc(S["qt" if z == 0 else "kt"], 1)

                def out_pt(i, p):
                    act.wait_ge(S["ptr"], 16 * L + i + 1)
                    past(act, S["pv"], 16 * L + i)
                    nc.scalar.copy(pt[:, :, :], ps[:, 4:6].rearrange("p b (h t) -> p (b h) t", t=P)).then_inc(S["pt"], 1)

                def out_ot(i):
                    act.wait_ge(S["otr"], 16 * L + i + 1)
                    past(act, S["wo_mm"], 16 * L + i)
                    nc.scalar.copy(oT[:, :, :], ps[:, 0].rearrange("p (b t) -> p b t", t=P)).then_inc(S["ot"], 1)

                def exps(i, p):
                    act.wait_ge(S["less_max"], 16 * L + i + 1)
                    nc.scalar.activation(prob[:, p], prob[:, p], ACT.Exp).then_inc(S["exps"], 1)

                def step(i, p):
                    if not isinstance(i, int) or 2 <= i:
                        out_ot(i - 2)
                    if not isinstance(i, int) or 1 <= i <= NT:
                        out_pt(i - 1, 1 - p)
                    if not isinstance(i, int) or i + 1 < NT:
                        out_turned(i + 1, 1 - p, 1)
                    if not isinstance(i, int) or i < NT:
                        exps(i, p)
                    if not isinstance(i, int) or i + 1 < NT:
                        out_turned(i + 1, 1 - p, 0)

                out_turned(0, 0, 1)
                out_turned(0, 0, 0)
                for i in range(2):
                    step(i, i)
                for i, p in steps(act, 2, NT - 2):
                    step(i, p)
                for i in range(NT - 2, NT + 2):
                    step(i, i % 2)

                act.wait_ge(S["h_var"], L + 1)
                nc.scalar.activation(K.sd[:, :], K.vare[:, :], ACT.Sqrt).then_inc(S["h_sd"], 1)
                act.wait_ge(S["w_mlp"], 208 * (L + 1))

                def out_ht(g):
                    act.wait_ge(S["h_tp"], 16 * L + 4 * g + 4)
                    nc.scalar.activation(hT[:, 512 * g:512 * g + 512], ps[:, 6 + g % 2, :], ACT.Identity,
                                         bias=lnb[:, :], scale=lng[:, :]).then_inc(S["hT"], 1)

                out_ht(0)
                for g in range(NT // 4):
                    if g + 1 < NT // 4:
                        out_ht(g + 1)
                    for c, (_, hc) in enumerate(CH):
                        u = NC_ * g + c
                        act.wait_ge(S["w1_mm"], 12 * L + u + 1)
                        past(act, S["gate"], 12 * L + u - 1)
                        nc.scalar.activation(gel[0:hc, u % 2, :], ps[0:hc, 2 * (u % 2) + 1, :], ACT.Gelu,
                                             bias=b1[0:hc, NC_ + c:NC_ + c + 1]).then_inc(S["gelu"], 1)

        @block.tensor
        def _(pe):
            pe.wait_ge(S["const_b"], 3 + 2 * which)
            for l in range(DEPTH):
                L = DEPTH * which + l

                def turn(i, p):
                    pe.wait_ge(S["ys"], 16 * L + i + 1)
                    past(pe, S["ht"], 16 * L + i - 1)
                    nc.tensor.transpose(ps[:, 6 + p, 0:P], ys[:, p, :], K.ident[:, :]).then_inc(S["tp"], 1)

                def project(i, p):
                    pe.wait_ge(S["ht"], 16 * L + i + 1)
                    past(pe, S["qk_out"], 16 * L + i - 1)
                    past(pe, S["v_out"], 16 * L + i - 1)
                    for z in range(3):
                        bank = 2 * p + z if z < 2 else 4 + p
                        mm = nc.tensor.matmul(ps[:, bank, :], ht[:, p, :], wqkv[:, INNER * z:INNER * (z + 1)],
                                              start=True, stop=True)
                    mm.then_inc(S["qkv"], 1)

                pe.wait_ge(S["w_qkv"], 48 * (L + 1))
                turn(0, 0)
                turn(1, 1)
                project(0, 0)
                with pe.Fori(1, NT // 2) as pair:
                    for p in range(2):
                        turn(2 * pair + p, p)
                        project(2 * pair + p - 1, 1 - p)
                project(NT - 1, 1)

                def turn_k(i, p):
                    pe.wait_ge(S["rot"], 16 * L + i + 1)
                    past(pe, S["kt"], 16 * L + i)
                    for b in range(4):
                        mm = nc.tensor.transpose(ps[:, 1, b * P:(b + 1) * P],
                                                 qk2[:, p, (4 + b) * P:(5 + b) * P], K.ident[:, :])
                    mm.then_inc(S["tk"], 1)

                def turn_q(i, p):
                    past(pe, S["qt"], 16 * L + i)
                    past(pe, S["y_attn"], 16 * L + i - 2)
                    for b in range(4):
                        mm = nc.tensor.transpose(ps[:, 0, b * P:(b + 1) * P], qk2[:, p, b * P:(b + 1) * P],
                                                 K.ident[:, :])
                    mm.then_inc(S["tq"], 1)

                def score(i, p):
                    pe.wait_ge(S["kt"], 16 * L + i + 1)
                    pe.wait_ge(S["qt"], 16 * L + i + 1)
                    past(pe, S["less_max"], 16 * L + i)
                    for b in range(2):
                        nc.tensor.matmul(
                            ps[:, 2 + b].rearrange("p (h k) -> p h k", k=P), K.identb[:, :],
                            mask[:, i].rearrange("p (o k) -> p o k", o=1).broadcast_to((P, 4, P)),
                            start=True, stop=False, skip_group_check=True)
                    for h in range(HEADS):
                        r, b = DH * (h % 2), h // 2
                        out = ps[:, 2 + h % 2, b * P:(b + 1) * P]
                        nc.tensor.matmul(out[0:64, 0:64], qkt[r:r + DH, p, b, 0:64], qkt[r:r + DH, p, 4 + b, 0:64],
                                         start=False, stop=True, skip_group_check=True)
                        nc.tensor.matmul(out[0:64, 64:P], qkt[r:r + DH, p, b, 0:64],
                                         qkt[r:r + DH, 1 - p, 4 + b, 64:P],
                                         start=False, stop=True, skip_group_check=True)
                        mm = nc.tensor.matmul(out[64:P, :], qkt[r:r + DH, p, b, 64:P], qkt[r:r + DH, p, 4 + b, :],
                                              start=False, stop=True, skip_group_check=True)
                    mm.then_inc(S["scores"], 1)

                def turn_p(i, p):
                    pe.wait_ge(S["exps"], 16 * L + i + 1)
                    past(pe, S["pt"], 16 * L + i)
                    for h in range(HEADS):
                        mm = nc.tensor.transpose(ps[:, 4 + h // 4, (h % 4) * P:(h % 4 + 1) * P],
                                                 prob[:, p, h, :], K.ident[:, :])
                    mm.then_inc(S["ptr"], 1)

                def weigh(i, p, heads, v_staged):
                    if heads[0] == 0:
                        pe.wait_ge(S["pt"], 16 * L + i + 1)
                        pe.wait_ge(S["v_stage"][p], v_staged)
                        past(pe, S["o_norm"], 16 * L + i)
                    for h in heads:
                        out = o_bank(ps)[:, h // 4, h % 4, :]
                        s = 4 * (h % 2) + h // 2
                        nc.tensor.matmul(out[0:64], pt[:, s, 0:64], ve[:, p, h, :], start=True, stop=True)
                        mm = nc.tensor.matmul(out[64:P], pt[:, s, 64:P], vs[:, p, h, :], start=True, stop=True)
                    if heads[-1] == HEADS - 1:
                        mm.then_inc(S["pv"], 1)

                def turn_o(i, q_out):
                    pe.wait_ge(S["o_norm"], 16 * L + i + 1)
                    pe.wait_ge(S["qt"], q_out)
                    for b in range(4):
                        mm = nc.tensor.transpose(ps[:, 0, b * P:(b + 1) * P], ot[:, b * P:(b + 1) * P], K.ident[:, :])
                    mm.then_inc(S["otr"], 1)

                def output(i):
                    pe.wait_ge(S["ot"], 16 * L + i + 1)
                    for b in range(4):
                        mm = nc.tensor.matmul(ps[:, 0, 0:C], oT[:, b, :], wo[:, b, :], start=(b == 0), stop=(b == 3))
                    mm.then_inc(S["wo_mm"], 1)

                def step(i, p, v_staged):
                    static = isinstance(i, int)
                    if not static or i < NT:
                        score(i, p)
                    if not static or 2 <= i:
                        turn_o(i - 2, 16 * L + (min(i + 1, NT) if static else i + 1))
                    if not static or 1 <= i <= NT:
                        turn_p(i - 1, 1 - p)
                    if not static or 2 <= i:
                        output(i - 2)
                    if not static or i + 1 < NT:
                        turn_k(i + 1, 1 - p)
                    if not static or 1 <= i <= NT:
                        weigh(i - 1, 1 - p, range(0, 4), v_staged)
                    if not static or i + 1 < NT:
                        turn_q(i + 1, 1 - p)
                    if not static or 1 <= i <= NT:
                        weigh(i - 1, 1 - p, range(4, HEADS), v_staged)

                pe.wait_ge(S["w_o"], 16 * (L + 1))
                turn_k(0, 0)
                turn_q(0, 0)
                for i in range(2):
                    step(i, i, 48 * (8 * L + 1))
                with pe.Fori(1, NT // 2 - 1) as pair:
                    for p in range(2):
                        step(2 * pair + p, p, 48 * (pair + (8 * L + p)))
                for i in range(NT - 2, NT + 2):
                    step(i, i % 2, 48 * (8 * L + min(i - 1, NT - 1) // 2 + 1))

                def turn_h(g):
                    past(pe, S["hT"], 4 * L + g - 1)
                    for i in range(4 * g, 4 * g + 4):
                        pe.wait_ge(S["h_norm"], 16 * L + i + 1)
                        nc.tensor.transpose(ps[:, 6 + g % 2, (i % 4) * P:(i % 4 + 1) * P], hn[:, i % 2, :],
                                            K.ident[:, :]).then_inc(S["h_tp"], 1)

                def down(g):
                    pe.wait_ge(S["gate"], 12 * L + NC_ * (g + 1))
                    past(pe, S["y_mlp"], 4 * L + g - 1)
                    for j in range(4):
                        for c, (_, hc) in enumerate(CH):
                            rows = hc + (c == NC_ - 1)
                            mm = nc.tensor.matmul(ps[:, 4 + g % 2, j * P:(j + 1) * P],
                                                  hid[0:rows, g % 2, c, j * P:(j + 1) * P], w2[0:rows, c, :],
                                                  start=(c == 0), stop=(c == NC_ - 1))
                    mm.then_inc(S["w2_mm"], 1)

                pe.wait_ge(S["w_mlp"], 208 * (L + 1))
                pe.wait_ge(S["y_attn"], 16 * (L + 1))
                turn_h(0)
                for g in range(NT // 4):
                    if g + 1 < NT // 4:
                        turn_h(g + 1)
                    pe.wait_ge(S["hT"], 4 * L + g + 1)
                    for c, (h0, hc) in enumerate(CH):
                        u = NC_ * g + c
                        past(pe, S["gate"], 12 * L + u - 1)
                        for half in range(2):
                            mm = nc.tensor.matmul(ps[0:hc, 2 * (u % 2) + half, :],
                                                  w1[:, half * HID + h0:half * HID + h0 + hc],
                                                  hT[:, 512 * g:512 * g + 512], start=True, stop=True)
                        mm.then_inc(S["w1_mm"], 1)
                        if c == 0 and g >= 1:
                            down(g - 1)
                down(NT // 4 - 1)
                pe.wait_ge(S["y_mlp"], 4 * (L + 1))


CHUNKS = (0, 2, 3, 1)
WORK = [(c, g) for c in CHUNKS for g in range(NG)]


def key_steps(n):
    return 4 * (WORK[n][0] + 1)


def max_units(n):
    c = WORK[n][0]
    return [(j, h, part) for j in range(4) for h in range(HG) for part in range(c + 1)]


def max_share(n, k):
    units, before = max_units(n), key_steps(n - 1)
    over = before - (3 if before > 4 else 2)
    lo, hi = min(k, over) * len(units) // over, min(k + 1, over) * len(units) // over
    return list(enumerate(units))[lo:hi]


MAX_BASE = [sum(len(max_units(m)) for m in range(n)) for n in range(len(WORK) + 1)]
KEY_BASE = [sum(key_steps(m) for m in range(n)) for n in range(len(WORK) + 1)]


def causal_block(nc, K, S, dram):
    with ExitStack() as stack:
        def sb(name, shape, dt=F32):
            return stack.enter_context(nc.sbuf_tensor(f"c_{name}", shape, dt))

        qs = sb("qs", [P, NT, H2, SLOT])
        ks = sb("ks", [P, NT, H2, SLOT])
        vv = sb("vv", [P, NT, H2, SLOT])
        kT = sb("kT", [P, NG, T], F32R)
        qmT = sb("qmT", [P, 2, HG, 512], F32R)
        qT = sb("qT", [P, 2, HG, 512], F32R)
        own = sb("own", [P, HG])
        pr = sb("pr", [P, 2, HG, 512])
        watt = sb("watt", [P, 3 * C])
        batt = sb("batt", [P, 3 * C])
        wproj = sb("wproj", [P, C])
        bproj = sb("bproj", [P, C])
        r2c = sb("r2c", [P, NT, D2 // 2])
        r2s = sb("r2s", [P, NT, 2, D2 // 2])
        cmf = sb("cmf", [P, 2, P])
        cmask = sb("cmask", [P, 2, P], BF16)
        spare = pr[:, :, :, :].rearrange("p s h t -> p (s h t)")
        def part(at, n, slots=2):
            return spare[:, at:at + n * slots].rearrange("p (s n) -> p s n", s=slots)

        raw = part(0, 3 * C)
        ca = part(768, 2 * C)
        rr = part(1280, 2 * C)
        ys = part(1792, C)
        ht = part(2048, C)
        cb = part(2304, 2 * C, 1)
        oT = part(0, 512)
        hi = sb("hi", [P, 2, 2 * C], F32R)
        mparts = sb("mparts", [P, 2, 4 * HG, NQ])
        m16 = sb("m16", [P, 4 * HG])
        neg = sb("neg", [P, 4 * HG])
        neghi = sb("neghi", [P, 4 * HG], F32R)
        acc = sb("acc", [P, 512])
        rsum = sb("rsum", [P, 4, HG])
        o = K.y[:, :, :]
        ps = stack.enter_context(nc.psum_tensor("c_ps", [P, 8, 512], F32))
        MX, ACC, MISC = 4, 6, 7

        def slots(ap):
            return ap.rearrange("p (h d) -> p h d", d=D2)

        block = stack.enter_context(nc.Block())

        @block.sync
        def _(sp):
            sp.dma_start(watt[:, :], dram["W_attn"]).then_inc(S["c_in"], 16)
            sp.dma_start(wproj[:, :], dram["W_proj"]).then_inc(S["c_in"], 16)
            sp.dma_start(batt[:, :], dram["b_attn"].partition_broadcast(P)).then_inc(S["c_in"], 16)
            sp.dma_start(bproj[:, :], dram["b_proj"].partition_broadcast(P)).then_inc(S["c_in"], 16)
            sp.dma_start(cmf[:, :, :], dram["causal_mask"]).then_inc(S["c_in"], 16)
            sp.dma_start(own[:, :], dram["own"]).then_inc(S["c_in"], 16)
            sp.dma_start(r2c[:, :, :], dram["rope2_c"]).then_inc(S["c_in"], 16)
            sp.dma_start(r2s[:, :, :, :], dram["rope2_s"]).then_inc(S["c_in"], 16)

        @block.gpsimd
        def _(pool):
            nc.gpsimd.memset(qs[:, :, :, MROW:], 0.0).then_inc(S["c_zero"], 1)
            nc.gpsimd.memset(ks[:, :, :, MROW:MROW + 2], 1.0).then_inc(S["c_zero"], 1)
            nc.gpsimd.memset(ks[:, :, :, MROW + 2:], 0.0).then_inc(S["c_zero"], 1)
            nc.gpsimd.memset(vv[:, :, :, D2:D2 + 1], 1.0).then_inc(S["c_zero"], 1)
            nc.gpsimd.memset(vv[:, :, :, D2 + 1:], 0.0).then_inc(S["c_zero"], 1)
            pool.wait_ge(S["c_in"], 16 * 8)
            pool.wait_ge(S["ln_y"], 32)

            def stage(i, p):
                past(pool, S["c_tp"], i - 1)
                nc.gpsimd.tensor_copy(ys[:, p, :], K.y[:, i, :]).then_inc(S["c_ys"], 1)

            def cosine(i, p):
                pool.wait_ge(S["c_biased"], i + 1)
                past(pool, S["c_rot"], i - 1)
                nc.gpsimd.tensor_tensor(
                    ca[:, p].rearrange("p (m d) -> p m d", d=4), raw[:, p, 0:2 * C].rearrange("p (m d) -> p m d", d=4),
                    r2c[:, i].rearrange("p (o d) -> p o d", o=1).broadcast_to((P, 64, 4)),
                    ALU.mult).then_inc(S["c_cos"], 1)

            stage(0, 0)
            stage(1, 1)
            cosine(0, 0)
            with pool.Fori(1, NT // 2) as pair:
                for p in range(2):
                    stage(2 * pair + p, p)
                    cosine(2 * pair + p - 1, 1 - p)
            cosine(NT - 1, 1)
            nc.gpsimd.tensor_tensor(
                K.x[:, :, :], K.x[:, :, :],
                bproj[:, :].rearrange("p (o c) -> p o c", o=1).broadcast_to((P, NT, C)), ALU.add).then_inc(S["c_xb"], 1)

        @block.vector
        def _(dve):
            dve.wait_ge(S["x_ffn"], 1)
            dve.wait_ge(S["c_in"], 16 * 8)
            nc.vector.tensor_copy(cmask[:, :, :], cmf[:, :, :]).then_inc(S["c_bias"], 1)
            ln_vector(dve, nc, K, S, 1)

            for i, p in tiles(dve):
                dve.wait_ge(S["c_qkv"], i + 1)
                past(dve, S["c_cos"], i - 1)
                past(dve, S["c_v"], i - 1)
                nc.vector.tensor_tensor(raw[:, p], ps[:, p, 0:3 * C], batt[:, :], ALU.add).then_inc(S["c_biased"], 1)
                dve.wait_ge(S["c_biased"], i + 1)
                past(dve, S["c_rot"], i)
                nc.vector.tensor_tensor(
                    cb[:, 0].rearrange("p (h a d) -> p h a d", a=2, d=4),
                    raw[:, p, 0:2 * C].rearrange("p (h a d) -> p h a d", a=2, d=4)[:, :, ::-1, :],
                    r2s[:, i].rearrange("p (o a) d -> p o a d", o=1).broadcast_to((P, 32, 2, 4)),
                    ALU.mult).then_inc(S["c_sin"], 1)
                dve.wait_ge(S["c_sin"], i + 1)
                dve.wait_ge(S["c_cos"], i + 1)
                past(dve, S["c_lo"], 2 * i - 2)
                nc.vector.tensor_tensor(rr[:, p], ca[:, p], cb[:, 0], ALU.add).then_inc(S["c_rot"], 1)
                dve.wait_ge(S["c_rot"], i + 1)
                past(dve, S["c_ks"], i - 1)
                nc.vector.tensor_copy(hi[:, p], rr[:, p]).then_inc(S["c_hi"], 1)
                dve.wait_ge(S["c_hi"], i + 1)
                nc.vector.tensor_tensor(qs[:, i, :, 16:24], slots(rr[:, p, 0:C]), slots(hi[:, p, 0:C].bitcast(F32)),
                                        ALU.subtract).then_inc(S["c_lo"], 1)
                nc.vector.tensor_tensor(ks[:, i, :, 8:16], slots(rr[:, p, C:]), slots(hi[:, p, C:].bitcast(F32)),
                                        ALU.subtract).then_inc(S["c_lo"], 1)

            def finish_max(n):
                c, g = WORK[n]
                dve.wait_ge(S["c_max"], MAX_BASE[n + 1])
                past(dve, S["c_neg"], n)
                nc.vector.tensor_reduce(m16[:, :], mparts[:, n % 2, :, 0:c + 1], AX_X, ALU.max).then_inc(S["c_mfin"], 1)
                dve.wait_ge(S["c_mfin"], n + 1)
                past(dve, S["c_mlo"], n)
                nc.vector.tensor_scalar(neg[:, :], m16[:, :], -1.0, None, ALU.mult).then_inc(S["c_neg"], 1)
                dve.wait_ge(S["c_neg"], n + 1)
                nc.vector.tensor_copy(neghi[:, :], neg[:, :]).then_inc(S["c_neghi"], 1)
                dve.wait_ge(S["c_neghi"], n + 1)
                dve.wait_ge(S["c_qm_tp"], n + 1)
                high = neghi[:, :].bitcast(F32).rearrange("p (j h) -> p j h", h=HG)
                nc.vector.tensor_copy(qs[:, 4 * c:4 * c + 4, HG * g:HG * (g + 1), MROW], high).then_inc(S["c_mrow"], 1)
                nc.vector.tensor_tensor(qs[:, 4 * c:4 * c + 4, HG * g:HG * (g + 1), MROW + 1],
                                        neg[:, :].rearrange("p (j h) -> p j h", h=HG), high,
                                        ALU.subtract).then_inc(S["c_mlo"], 1)

            def take_out(n):
                dve.wait_ge(S["c_pv"], KEY_BASE[n + 1])
                past(dve, S["c_acc_tp"], n)
                nc.vector.tensor_copy(acc[:, :], ps[:, ACC, :]).then_inc(S["c_acc"], 1)

            def finish_out(n):
                c, g = WORK[n]
                dve.wait_ge(S["c_acc_tp"], n + 1)
                past(dve, S["c_o"], n)
                by_head = ps[:, MISC].rearrange("p (j h d) -> p j h d", j=4, d=SLOT)
                nc.vector.reciprocal(rsum[:, :, :], by_head[:, :, :, D2]).then_inc(S["c_rsum"], 1)
                dve.wait_ge(S["c_rsum"], n + 1)
                nc.vector.tensor_tensor(
                    o[:, 4 * c:4 * c + 4, 32 * g:32 * (g + 1)].rearrange("p j (h d) -> p j h d", d=D2),
                    by_head[:, :, :, 0:D2],
                    rsum[:, :, :].rearrange("p j (h o) -> p j h o", o=1).broadcast_to((P, 4, HG, D2)),
                    ALU.mult).then_inc(S["c_o"], 1)

            def unit_max(n, u, j, h, part):
                unit = MAX_BASE[n] + u
                width = 512 if part < WORK[n][0] else P * (j + 1)
                dve.wait_ge(S["c_mx"], unit + 1)
                past(dve, S["c_mfin"], n - 1)
                nc.vector.tensor_reduce(mparts[:, n % 2, HG * j + h, part:part + 1],
                                        ps[:, MX + unit % 2, 0:width], AX_X, ALU.max).then_inc(S["c_max"], 1)

            for u, (j, h, part) in enumerate(max_units(0)):
                unit_max(0, u, j, h, part)
            finish_max(0)
            for n in range(1, len(WORK) + 1):
                for kt in range(key_steps(n - 1)):
                    if n < len(WORK):
                        for u, (j, h, part) in max_share(n, kt):
                            unit_max(n, u, j, h, part)
                    if n >= 2 and kt == 0:
                        take_out(n - 2)
                    if n >= 2 and kt == 1:
                        finish_out(n - 2)
                if n < len(WORK):
                    finish_max(n)
            take_out(len(WORK) - 1)
            finish_out(len(WORK) - 1)

            dve.wait_ge(S["c_xb"], 1)
            for b in range(4):
                dve.wait_ge(S["c_proj"], b + 1)
                xb = K.x[:, 4 * b:4 * b + 4].rearrange("p i c -> p (i c)")
                nc.vector.tensor_tensor(xb, xb, ps[:, 2 + b % 2, :], ALU.add).then_inc(S["x_attn"], 1)

        @block.scalar
        def _(act):
            ln_scalar(act, nc, K, S, 1)
            act.wait_ge(S["c_zero"], 5)
            for i, p in tiles(act):
                act.wait_ge(S["c_tp"], i + 1)
                past(act, S["c_qkv"], i - 1)
                nc.scalar.copy(ht[:, p, :], ps[:, 2 + p, 0:P]).then_inc(S["c_ht"], 1)
                act.wait_ge(S["c_biased"], i + 1)
                nc.scalar.copy(vv[:, i, :, 0:D2], slots(raw[:, p, 2 * C:])).then_inc(S["c_v"], 1)
                act.wait_ge(S["c_hi"], i + 1)
                high = hi[:, p, :].bitcast(F32)
                nc.scalar.copy(qs[:, i, :, 0:16].rearrange("p h (a d) -> p h a d", a=2),
                               high[:, 0:C].rearrange("p (h o d) -> p h o d", o=1, d=D2)
                               .broadcast_to((P, H2, 2, D2))).then_inc(S["c_qs"], 1)
                nc.scalar.copy(ks[:, i, :, :].rearrange("p h (a d) -> p h a d", a=2)[:, :, :, 0:D2],
                               high[:, C:].rearrange("p (h o d) -> p h o d", o=1, d=D2)
                               .broadcast_to((P, H2, 2, D2))).then_inc(S["c_ks"], 1)
            for u in range(4 * NG):
                act.wait_ge(S["c_kt_tp"], u + 1)
                nc.scalar.copy(kT[:, u // 4, 512 * (u % 4):512 * (u % 4) + 512], ps[:, u % 4, :]).then_inc(S["c_kt"], 1)

            def spread(n, heads, out, turned, done):
                act.wait_ge(turned, n + 1)
                for h in heads:
                    nc.scalar.activation(out[:, n % 2, h], ps[:, MISC], ACT.Identity,
                                         scale=own[:, h:h + 1]).then_inc(done, 1)

            def spread_qm(n, heads):
                past(act, S["c_mx"], MAX_BASE[n - 1] if n else 0)
                spread(n, heads, qmT, S["c_qm_tp"], S["c_qm"])

            def spread_q(n, heads):
                past(act, S["c_st"], 2 * KEY_BASE[n - 1] if n else 0)
                spread(n, heads, qT, S["c_q_tp"], S["c_q"])

            def exps(n, kt, pair):
                c = WORK[n][0]
                step = KEY_BASE[n] + kt
                off = P * max(0, kt - 4 * c)
                unit = 2 * step + pair
                act.wait_ge(S["c_st"], unit + 1)
                past(act, S["c_pv"], step - 1)
                nc.scalar.activation(pr[:, step % 2, 2 * pair:2 * pair + 2, off:],
                                     ps[:, 2 * (unit % 2):2 * (unit % 2) + 2, off:], ACT.Exp,
                                     scale=float(D2) ** -0.5).then_inc(S["c_exp"], 1)

            spread_qm(0, range(HG))
            spread_qm(1, range(HG))
            spread_q(0, range(HG))
            for n in range(1, len(WORK) + 1):
                last, mid = key_steps(n - 1) - 1, key_steps(n - 1) // 2
                for kt in range(last + 1):
                    exps(n - 1, kt, 0)
                    if n + 1 < len(WORK) and kt == mid + 1:
                        spread_qm(n + 1, (2, 3))
                    if n < len(WORK) and kt == last:
                        spread_q(n, (0, 1))
                    exps(n - 1, kt, 1)
                    if n + 1 < len(WORK) and kt == mid:
                        spread_qm(n + 1, (0, 1))
                    if n < len(WORK) and kt == last:
                        spread_q(n, (2, 3))
            for b in range(4):
                act.wait_ge(S["c_ot_tp"], b + 1)
                past(act, S["c_proj"], b - 1)
                nc.scalar.copy(oT[:, b % 2], ps[:, b % 2]).then_inc(S["c_ot"], 1)

        @block.tensor
        def _(pe):
            def turn(i, p):
                pe.wait_ge(S["c_ys"], i + 1)
                past(pe, S["c_ht"], i - 1)
                nc.tensor.transpose(ps[:, 2 + p, 0:P], ys[:, p, :], K.ident[:, :]).then_inc(S["c_tp"], 1)

            def project(i, p):
                pe.wait_ge(S["c_ht"], i + 1)
                past(pe, S["c_biased"], i - 1)
                nc.tensor.matmul(ps[:, p, 0:3 * C], ht[:, p, :], watt[:, :], start=True, stop=True).then_inc(S["c_qkv"], 1)

            pe.wait_ge(S["c_in"], 16 * 8)
            turn(0, 0)
            turn(1, 1)
            project(0, 0)
            with pe.Fori(1, NT // 2) as pair:
                for p in range(2):
                    turn(2 * pair + p, p)
                    project(2 * pair + p - 1, 1 - p)
            project(NT - 1, 1)

            def group(ap, t, g):
                return ap[:, t, HG * g:HG * (g + 1)].rearrange("p h s -> p (h s)")

            pe.wait_ge(S["c_ks"], NT)
            pe.wait_ge(S["c_lo"], 2 * NT)
            pe.wait_ge(S["c_bias"], 1)
            for u in range(4 * NG):
                past(pe, S["c_kt"], u - 3)
                for j in range(4):
                    mm = nc.tensor.transpose(ps[:, u % 4, P * j:P * (j + 1)], group(ks, 4 * (u % 4) + j, u // 4),
                                             K.ident[:, :])
                mm.then_inc(S["c_kt_tp"], 1)

            def turn_queries(n, done):
                c, g = WORK[n]
                for j in range(4):
                    mm = nc.tensor.transpose(ps[:, MISC, P * j:P * (j + 1)], group(qs, 4 * c + j, g), K.ident[:, :])
                mm.then_inc(done, 1)

            def max_unit(n, u, j, h, part):
                c, g = WORK[n]
                unit = MAX_BASE[n] + u
                last = part == c
                width = P * (j + 1) if last else 512
                past(pe, S["c_max"], unit - 1)
                out = ps[:, MX + unit % 2, :]
                mm = nc.tensor.matmul(out[:, 0:width], qmT[:, n % 2, h, P * j:P * (j + 1)],
                                      kT[:, g, 512 * part:512 * part + width], start=True, stop=True)
                if last:
                    mm = nc.tensor.matmul(out[:, width - P:width], K.identb[:, :], cmask[:, 0, :],
                                          start=False, stop=True, skip_group_check=True)
                mm.then_inc(S["c_mx"], 1)

            def score_pair(n, kt, pair):
                c, g = WORK[n]
                unit = 2 * (KEY_BASE[n] + kt) + pair
                off = P * max(0, kt - 4 * c)
                past(pe, S["c_exp"], unit - 1)
                for a in range(2):
                    out = ps[:, 2 * (unit % 2) + a, :]
                    mm = nc.tensor.matmul(out[:, off:], kT[:, g, P * kt:P * (kt + 1)], qT[:, n % 2, 2 * pair + a, off:],
                                          start=True, stop=True)
                    if kt >= 4 * c:
                        mm = nc.tensor.matmul(out[:, off:off + P], K.identb[:, :], cmask[:, 1, :],
                                              start=False, stop=True, skip_group_check=True)
                mm.then_inc(S["c_st"], 1)

            def weigh(n, kt):
                c, g = WORK[n]
                step = KEY_BASE[n] + kt
                off = P * max(0, kt - 4 * c)
                pe.wait_ge(S["c_exp"], 2 * step + 2)
                if kt == 0:
                    past(pe, S["c_acc"], n)
                for h in range(HG):
                    mm = nc.tensor.matmul(ps[SLOT * h:SLOT * (h + 1), ACC, off:], vv[:, kt, HG * g + h, :],
                                          pr[:, step % 2, h, off:], start=(kt == 0), stop=(kt >= 4 * c),
                                          skip_group_check=True)
                mm.then_inc(S["c_pv"], 1)

            def turn_acc(n):
                pe.wait_ge(S["c_acc"], n + 1)
                for j in range(4):
                    mm = nc.tensor.transpose(ps[:, MISC, P * j:P * (j + 1)], acc[:, P * j:P * (j + 1)], K.ident[:, :])
                mm.then_inc(S["c_acc_tp"], 1)

            turn_queries(0, S["c_qm_tp"])
            pe.wait_ge(S["c_qm"], HG)
            turn_queries(1, S["c_qm_tp"])
            for u, (j, h, part) in enumerate(max_units(0)):
                max_unit(0, u, j, h, part)
            pe.wait_ge(S["c_mrow"], 1)
            pe.wait_ge(S["c_mlo"], 1)
            pe.wait_ge(S["c_qm"], 2 * HG)
            turn_queries(0, S["c_q_tp"])
            for n in range(1, len(WORK) + 1):
                last, mid = key_steps(n - 1) - 1, key_steps(n - 1) // 2
                pe.wait_ge(S["c_q"], HG * n)
                if n < len(WORK):
                    pe.wait_ge(S["c_qm"], HG * (n + 1))
                for kt in range(last + 1):
                    share = max_share(n, kt) if n < len(WORK) else []
                    lots = [share[len(share) * q // 4:len(share) * (q + 1) // 4] for q in range(4)]

                    def max_lot(q):
                        for u, (j, h, part) in lots[q]:
                            max_unit(n, u, j, h, part)

                    max_lot(0)
                    score_pair(n - 1, kt, 0)
                    if n >= 2 and kt == 1:
                        turn_acc(n - 2)
                    max_lot(1)
                    if n + 1 < len(WORK) and kt == mid:
                        past(pe, S["c_o"], n - 1)
                        turn_queries(n + 1, S["c_qm_tp"])
                    if n < len(WORK) and kt == last:
                        pe.wait_ge(S["c_mrow"], n + 1)
                        pe.wait_ge(S["c_mlo"], n + 1)
                        pe.wait_ge(S["c_qm"], HG * min(n + 2, len(WORK)))
                        past(pe, S["c_o"], n - 1)
                        turn_queries(n, S["c_q_tp"])
                    score_pair(n - 1, kt, 1)
                    max_lot(2)
                    if kt >= 1:
                        weigh(n - 1, kt - 1)
                    elif n >= 2:
                        weigh(n - 2, key_steps(n - 2) - 1)
                    max_lot(3)
            weigh(len(WORK) - 1, key_steps(len(WORK) - 1) - 1)
            turn_acc(len(WORK) - 1)

            pe.wait_ge(S["c_o"], len(WORK))
            for b in range(4):
                past(pe, S["c_ot"], b - 1)
                for j in range(4):
                    mm = nc.tensor.transpose(ps[:, b % 2, P * j:P * (j + 1)], o[:, 4 * b + j, :], K.ident[:, :])
                mm.then_inc(S["c_ot_tp"], 1)
                pe.wait_ge(S["c_ot"], b + 1)
                past(pe, S["x_attn"], b - 1)
                for j in range(4):
                    mm = nc.tensor.matmul(ps[:, 2 + b % 2, P * j:P * (j + 1)], oT[:, b % 2, P * j:P * (j + 1)],
                                          wproj[:, :], start=True, stop=True)
                mm.then_inc(S["c_proj"], 1)


def build(nc, dram):
    with ExitStack() as stack:
        K = Keep(nc, stack)
        S = {name: stack.enter_context(nc.semaphore(name)) for name in SEMS.split()}
        S["v_stage"] = [stack.enter_context(nc.semaphore(f"v_stage{p}")) for p in range(2)]
        ffn_block(nc, K, S, dram, 0)
        causal_block(nc, K, S, dram)
        ffn_block(nc, K, S, dram, 1)


SEMS = """x_in consts rope_in const_b x_attn x_ffn stored
ln_stat ln_aggr ln_var ln_sd ln_rstd ln_y
w_qkv w_o w_mlp shift_zero shifted v_ones
ys tp ht qkv squares v_out sumsq qk_out norms norm_max inv_norm
unit cos_part sin_part rot tq tk qt kt scores row_max less_max exps ptr pt pv row_sum o_norm otr ot wo_mm y_attn
hid_ones h_stat h_aggr h_var h_sd h_rstd h_norm h_tp hT w1_mm gelu gate w2_mm y_mlp
c_in c_zero c_bias c_ys c_tp c_ht c_qkv c_biased c_cos c_sin c_rot c_hi c_qs c_ks c_lo c_v
c_kt_tp c_kt c_qm_tp c_qm c_mx c_max c_mfin c_neg c_neghi c_mrow c_mlo c_q_tp c_q
c_st c_exp c_pv c_acc c_acc_tp c_rsum c_o c_ot_tp c_ot c_proj c_xb"""


def constants():
    f = np.float32
    t = np.arange(T, dtype=f)
    half = np.arange(0, DH, 2, dtype=f)
    inv = (f(1.0) / np.power(f(10000.0), half / f(DH), dtype=f)).astype(f)
    freq = t[:, None] * inv[None, :]
    base = (half + f(0.4 * DH)) / f(1.4 * DH)
    power = (t - f(T // 2)) / f(WINDOW // 2)
    scale = np.power(base[None, :], power[:, None], dtype=f)
    c, s = np.cos(freq), np.sin(freq)
    cq, sq = f(QK_SCALE) * (c * scale), f(QK_SCALE) * (s * scale)
    ck, sk = c / scale, s / scale
    by_tile = lambda a: np.ascontiguousarray(a.reshape(NT, P, *a.shape[1:]).swapaxes(0, 1).astype(f))
    rope_c = by_tile(np.stack([cq, ck], 1))
    rope_s = by_tile(np.stack([np.stack([sq, -sq], 1), np.stack([sk, -sk], 1)], 1))
    r = np.arange(P)[:, None]
    k = np.arange(P)[None, :]
    w, q = r // 64, r % 64
    i = 64 * w + q
    j = np.where((w == 0) & (k >= 64), k - P, k)
    banned = (j > i) | (j < i - WINDOW)
    local = np.stack([np.where(banned | (j < 0), MASKED, 0.0), np.where(banned, MASKED, 0.0)], 1).astype(f)
    frac = (f(2.0) * np.arange(D2 // 2, dtype=f)) / f(D2)
    ang = t[:, None] / np.power(f(1250.0), frac, dtype=f)[None, :]
    c2, s2 = np.cos(ang), np.sin(ang)
    causal = np.stack([np.where(k > r, MASKED, 0.0), np.where(r > k, MASKED, 0.0)], 1).astype(f)
    return {"ident": np.eye(P, dtype=f), "local_mask": local, "rope_c": rope_c, "rope_s": rope_s,
            "own": (r // SLOT == np.arange(HG)[None, :]).astype(f), "rope2_c": by_tile(c2), "rope2_s": by_tile(np.stack([-s2, s2], 1)), "causal_mask": causal}


_INS = {"x": "L0_attn_x", "W_attn": "L0_attn_W_attn", "b_attn": "L0_attn_b_attn", "W_proj": "L0_attn_W_proj",
        "b_proj": "L0_attn_b_proj", "wqkv": "L0_ffn_wqkv", "q_scale": "L0_ffn_q_scale", "k_scale": "L0_ffn_k_scale",
        "wo": "L0_ffn_wo", "ln_g": "L0_ffn_ln_g", "ln_b": "L0_ffn_ln_b", "w1": "L0_ffn_w1", "b1": "L0_ffn_b1",
        "w2": "L0_ffn_w2", "b2": "L0_ffn_b2"}


def kernel(**inputs):
    import concourse.bacc as _bacc
    from concourse.bass_utils import run_bass_kernel_spmd as _run

    nc = _bacc.Bacc("TRN2", target_bir_lowering=False, num_devices=1)
    arrays, dram = {}, {}
    given = {short: np.ascontiguousarray(inputs[name]) for short, name in _INS.items()}
    given["x"] = given["x"].reshape(T, C)
    for name, a in {**given, **constants()}.items():
        arrays[f"in_{name}"] = a
        dram[name] = nc.dram_tensor(f"in_{name}", a.shape, mybir.dt.from_np(a.dtype), kind="ExternalInput").ap()
    dram["out"] = nc.dram_tensor("out_0", (T, C), F32, kind="ExternalOutput").ap()
    build(nc, dram)
    r = _run(nc, [arrays], core_ids=[0])
    return r.results[0]["out_0"].reshape(1, T, C)
```

```python
from contextlib import ExitStack

import numpy as np
import concourse.bass as bass
from concourse import mybir

F32 = mybir.dt.float32
F32R = mybir.dt.float32r
BF16 = mybir.dt.bfloat16
ALU = mybir.AluOpType
ACT = mybir.ActivationFunctionType
AX_X = mybir.AxisListType.X

P = 128
T = 2048
C = 128
NT = T // P
LN_EPS = 1e-5
MASKED = -1.0e30

DEPTH = 2
HEADS, DH, WINDOW = 8, 64, 64
INNER = HEADS * DH
HID = int(C * 4 * 2 / 3)
CH = [(0, 128), (128, 128), (256, HID - 256)]
NC_ = len(CH)
QK_SCALE = 8.0

H2, D2 = 16, 8
SLOT = 32
NG = 4
HG = H2 // NG
NQ = T // 512
MROW = 24


def past(eng, sem, value):
    if isinstance(value, int) and value <= 0:
        return
    eng.wait_ge(sem, value)


def steps(eng, first, last):
    with eng.Fori(first // 2, last // 2) as pair:
        for slot in range(2):
            yield 2 * pair + slot, slot


def groups(eng):
    yield 0
    with eng.Fori(1, NT // 4) as g:
        yield g


def tiles(eng, n=NT):
    for i in range(2):
        yield i, i
    yield from steps(eng, 2, n)


def ln_stats(nc, K, S, g):
    for i in range(4 * g, 4 * g + 4):
        nc.vector.bn_stats(K.st6[:, i, :], K.x[:, i, :]).then_inc(S["ln_stat"], 1)


def ln_vector(dve, nc, K, S, n):
    dve.wait_ge(S["ln_stat"], 16 * (n + 1))
    for i in range(NT):
        nc.vector.bn_aggr(K.mv[:, i, :], K.st6[:, i, :]).then_inc(S["ln_aggr"], 1)
    dve.wait_ge(S["ln_aggr"], 16 * (n + 1))
    nc.vector.tensor_scalar(K.vare[:, :], K.mv[:, :, 1], LN_EPS, None, ALU.add).then_inc(S["ln_var"], 1)
    dve.wait_ge(S["ln_sd"], n + 1)
    nc.vector.reciprocal(K.rstd[:, :], K.sd[:, :]).then_inc(S["ln_rstd"], 1)
    dve.wait_ge(S["ln_rstd"], n + 1)
    for i in range(NT):
        nc.vector.tensor_scalar(K.y[:, i, :], K.x[:, i, :], K.mv[:, i, 0:1], K.rstd_at(i),
                                ALU.subtract, ALU.mult).then_inc(S["ln_y"], 1)


def ln_scalar(act, nc, K, S, n):
    act.wait_ge(S["ln_var"], n + 1)
    nc.scalar.activation(K.sd[:, :], K.vare[:, :], ACT.Sqrt).then_inc(S["ln_sd"], 1)


class Keep:

    def __init__(self, nc, stack):
        def sb(name, shape, dt=F32):
            return stack.enter_context(nc.sbuf_tensor(name, shape, dt))

        self.x = sb("x_tok", [P, NT, C])
        self.y = sb("y_tok", [P, NT, C])
        self.ident = sb("ident", [P, P])
        self.identb = sb("identb", [P, P], BF16)
        self.st6 = sb("st6", [P, NT, 6])
        self.mv = sb("mv", [P, NT, 2])
        self.vare = sb("vare", [P, NT])
        self.sd = sb("sd", [P, NT])
        self.rstd = sb("rstd", [P, NT])

    def rstd_at(self, i):
        return self.rstd[:, :].rearrange("p (i o) -> p i o", o=1)[:, i, :]


def ffn_block(nc, K, S, dram, which):
    with ExitStack() as stack:
        def sb(name, shape, dt=F32):
            return stack.enter_context(nc.sbuf_tensor(f"{name}_{which}", shape, dt))

        qk = sb("qk", [P, NT, 2 * INNER])
        v = sb("v", [P, NT + 1, HEADS, DH + 1])
        rc = sb("rc", [P, NT, 2, DH // 2])
        rs = sb("rs", [P, NT, 2, 2, DH // 2])
        wqkv = sb("wqkv", [P, 3 * INNER])
        wo = sb("wo", [P, INNER // P, C])
        w1 = sb("w1", [P, 2 * HID])
        w2 = sb("w2", [P, NC_, C])
        b1 = sb("b1", [P, 2 * NC_])
        lng = sb("lng", [P, 1])
        lnb = sb("lnb", [P, 1])
        qks = sb("qks", [P, 2, DH])
        maskf = sb("maskf", [P, 3, P])
        mask = sb("mask", [P, 3, P], BF16)
        ss = sb("ss", [P, NT, 2 * HEADS])
        nrm = sb("nrm", [P, NT, 2 * HEADS])
        PARTS = ((0, 12), (12, NT))
        st = sb("st", [P, 2, 2, NT, 6])
        mvh = sb("mvh", [P, 2, NT, 2])
        vareh = sb("vareh", [P, 2, NT])
        sdh = sb("sdh", [P, 2, NT])
        rstdh = sb("rstdh", [P, 2, NT])
        shifts = sb("shifts", [P, 3 * P])
        zrow = sb("zrow", [1, C])
        zn = sb("zn", [1, C])
        nrm4 = sb("nrm4", [P, 4, 2 * HEADS])
        mx = sb("mx", [P, 2, HEADS])
        rsum = sb("rsum", [P, 2, HEADS])
        ta = sb("ta", [P, 2, 2 * INNER])
        tb = sb("tb", [P, 2 * INNER])
        qk2 = sb("qk2", [P, 2, 2 * INNER])
        qkt = sb("qkt", [P, 4 * INNER])
        sS = sb("sS", [P, 2 * HEADS * P])
        pt = sb("pt", [P, HEADS, P])
        ot = sb("ot", [P, INNER])
        oT = sb("oT", [P, INNER // P, P])
        vs = sb("vs", [P, 2, HEADS, DH + 1])
        ve = sb("ve", [P, 2, HEADS, DH + 1])
        ps = stack.enter_context(nc.psum_tensor(f"ps_{which}", [P, 8, 512], F32))

        prob = sS[:, :].rearrange("p (s h k) -> p s h k", s=2, h=HEADS)
        sq = qkt[:, :].rearrange("p (s n) -> p s n", s=2)
        qt = qkt[:, 0:2 * INNER].rearrange("p (s b t) -> p s b t", s=2, b=INNER // P)
        kt = qkt[:, 2 * INNER:].rearrange("p (b s t) -> p b s t", s=2, b=INNER // P)
        yT = sS[:, :]
        late = qk[:, :, :].rearrange("p i n -> p (i n)")[:, NT * 2 * INNER - T - 4608:]
        hT = late[:, 0:T]
        hid = late[:, T:T + 2 * NC_ * 512].rearrange("p (s c t) -> p s c t", s=2, c=NC_)
        gel = late[:, T + 3072:T + 4096].rearrange("p (s t) -> p s t", s=2)
        hn = late[:, T + 4096:T + 4608].rearrange("p (s t) -> p s t", s=4)

        def qk_view(ap):
            return ap.rearrange("p (z m d) -> p z m d", z=2, d=DH // 2)

        def o_bank(ap):
            return ap[:, 6:8, 0:4 * (DH + 1)].rearrange("p b (h d) -> p b h d", d=DH + 1)

        block = stack.enter_context(nc.Block())

        @block.sync
        def _(sp):
            def load_qkv(l, L):
                past(sp, S["qkv"], 16 * L)
                past(sp, S["qk_out"], 16 * L)
                sp.dma_start(wqkv[:, :], dram["wqkv"][l]).then_inc(S["w_qkv"], 16)
                sp.dma_start(qks[:, 0, :], dram["q_scale"][l:l + 1, :].partition_broadcast(P)
                             .rearrange("p o d -> p (o d)")).then_inc(S["w_qkv"], 16)
                sp.dma_start(qks[:, 1, :], dram["k_scale"][l:l + 1, :].partition_broadcast(P)
                             .rearrange("p o d -> p (o d)")).then_inc(S["w_qkv"], 16)

            def load_wo(l, L):
                past(sp, S["wo_mm"], 16 * L)
                sp.dma_start(wo[:, :, :], dram["wo"][l].rearrange("(b p) n -> p b n", p=P)).then_inc(S["w_o"], 16)

            def load_mlp(l, L):
                past(sp, S["w2_mm"], 4 * L)
                past(sp, S["gelu"], 12 * L)
                past(sp, S["gate"], 12 * L)
                col = lambda ap: ap.rearrange("(p o) -> p o", o=1)
                sp.dma_start(w1[:, :], dram["w1"][l]).then_inc(S["w_mlp"], 16)
                sp.dma_start(lng[:, :], col(dram["ln_g"][l])).then_inc(S["w_mlp"], 16)
                sp.dma_start(lnb[:, :], col(dram["ln_b"][l])).then_inc(S["w_mlp"], 16)
                for c, (h0, hc) in enumerate(CH):
                    sp.dma_start(w2[0:hc, c, :], dram["w2"][l, h0:h0 + hc, :]).then_inc(S["w_mlp"], 16)
                    for half in range(2):
                        sp.dma_start(b1[0:hc, half * NC_ + c:half * NC_ + c + 1],
                                     col(dram["b1"][l, half * HID + h0:half * HID + h0 + hc])
                                     ).then_inc(S["w_mlp"], 16)
                hc = CH[-1][1]
                sp.dma_start(w2[hc:hc + 1, NC_ - 1, :], dram["b2"][l:l + 1, :]).then_inc(S["w_mlp"], 16)

            if which == 0:
                sp.dma_start(K.x[:, :, :], dram["x"].rearrange("(i p) c -> p i c", p=P)).then_inc(S["x_in"], 16)
                sp.dma_start(K.ident[:, :], dram["ident"]).then_inc(S["consts"], 16)
            load_qkv(0, DEPTH * which)
            sp.dma_start(maskf[:, :, :], dram["local_mask"]).then_inc(S["consts"], 16)
            sp.dma_start(shifts[:, :], dram["shifts"]).then_inc(S["consts"], 16)
            sp.dma_start(rc[:, :, :, :], dram["rope_c"]).then_inc(S["rope_in"], 16)
            sp.dma_start(rs[:, :, :, :, :], dram["rope_s"]).then_inc(S["rope_in"], 16)
            load_wo(0, DEPTH * which)
            load_mlp(0, DEPTH * which)
            for l in range(DEPTH):
                L = DEPTH * which + l
                sp.wait_ge(S["v_out"], 16 * (L + 1))
                if l + 1 < DEPTH:
                    load_qkv(l + 1, L + 1)
                if l == 0:
                    sp.wait_ge(S["v_ones"], 2 * (which + 1))
                for i, p in tiles(sp):
                    past(sp, S["pv"], 16 * L + i - 1)
                    sp.dma_start(vs[:, p], v[:, i + 1]).then_inc(S["v_stage"][p], 16)
                    own, before = (slice(64, P), slice(0, 64)) if p else (slice(0, 64), slice(64, P))
                    sp.dma_start(ve[own, p], v[0:64, i + 1]).then_inc(S["v_stage"][p], 16)
                    sp.dma_start(ve[before, p], v[64:P, i]).then_inc(S["v_stage"][p], 16)
                if l + 1 < DEPTH:
                    load_wo(l + 1, L + 1)
                    load_mlp(l + 1, L + 1)
            if which == 1:
                out = dram["out"].rearrange("(i p) c -> p i c", p=P)
                for g in range(NT // 4):
                    sp.wait_ge(S["x_ffn"], 4 + g + 1)
                    sp.dma_start(out[:, 4 * g:4 * g + 4], K.x[:, 4 * g:4 * g + 4]).then_inc(S["stored"], 16)
                sp.wait_ge(S["stored"], 16 * NT // 4)

        @block.gpsimd
        def _(pool):
            nc.gpsimd.memset(v[:, 1:, :, DH:], 1.0).then_inc(S["v_ones"], 1)
            nc.gpsimd.memset(v[:, 0], 0.0).then_inc(S["v_ones"], 1)
            nc.gpsimd.memset(zrow[:, :], 0.0).then_inc(S["z_set"], 1)
            for l in range(DEPTH):
                L = DEPTH * which + l
                if l == 0:
                    pool.wait_ge(S["rope_in"], 32 * (which + 1))
                for g in groups(pool):
                    pool.wait_ge(S["inv_norm"], 4 * L + g + 1)
                    for j in range(4):
                        i, p = 4 * g + j, j % 2
                        nc.gpsimd.tensor_tensor(
                            qk[:, i].rearrange("p (h d) -> p h d", d=DH),
                            qk[:, i].rearrange("p (h d) -> p h d", d=DH),
                            ss[:, i].rearrange("p (h o) -> p h o", o=1).broadcast_to((P, 2 * HEADS, DH)),
                            ALU.mult).then_inc(S["unit"], 1)
                        pool.wait_ge(S["unit"], 16 * L + i + 1)
                        past(pool, S["rot"], 16 * L + i - 1)
                        nc.gpsimd.tensor_tensor(
                            qk_view(ta[:, p]), qk_view(qk[:, i]),
                            rc[:, i].rearrange("p z (o d) -> p z o d", o=1).broadcast_to((P, 2, 16, DH // 2)),
                            ALU.mult).then_inc(S["cos_part"], 1)
                pool.wait_ge(S["rot"], 16 * (L + 1))
                nc.gpsimd.memset(hid[64:P, :, NC_ - 1, :], 1.0).then_inc(S["hid_ones"], 1)

        @block.vector
        def _(dve):
            if which == 0:
                dve.wait_ge(S["x_in"], 16)
                for g in range(NT // 4):
                    ln_stats(nc, K, S, g)
            nc.vector.memset(yT[C // 2:C, 0:1], 0.0).then_inc(S["first_zero"], 1)
            ln_vector(dve, nc, K, S, 2 * which)
            dve.wait_ge(S["consts"], 48 + 32 * which)
            if which == 0:
                nc.vector.tensor_copy(K.identb[:, :], K.ident[:, :]).then_inc(S["const_b"], 1)
            nc.vector.tensor_copy(mask[:, :, :], maskf[:, :, :]).then_inc(S["const_b"], 1)
            for l in range(DEPTH):
                L = DEPTH * which + l
                if l > 0:
                    nc.vector.memset(yT[C // 2:C, 0:1], 0.0).then_inc(S["first_zero"], 1)
                def rotate(i, p):
                    dve.wait_ge(S["cos_part"], 16 * L + i + 1)
                    past(dve, S["rot"], 16 * L + i)
                    for z in range(2):
                        half = qk[:, i, z * INNER:(z + 1) * INNER].rearrange("p (h a d) -> p h a d", a=2, d=DH // 2)
                        nc.vector.tensor_tensor(
                            tb[:, z * INNER:(z + 1) * INNER].rearrange("p (h a d) -> p h a d", a=2, d=DH // 2)[:, :, ::-1, :],
                            half,
                            rs[:, i, z].rearrange("p (o a) d -> p o a d", o=1).broadcast_to((P, HEADS, 2, DH // 2)),
                            ALU.mult).then_inc(S["sin_part"], 1)
                    dve.wait_ge(S["sin_part"], 2 * (16 * L + i) + 2)
                    past(dve, S["tq"], 16 * L + i - 1)
                    past(dve, S["tk"], 16 * L + i - 1)
                    nc.vector.tensor_tensor(qk2[:, p], ta[:, p], tb[:, :], ALU.add).then_inc(S["rot"], 1)

                def sum_squares(i, p):
                    dve.wait_ge(S["squares"], 16 * L + i + 1)
                    nc.vector.tensor_reduce(ss[:, i], sq[:, p].rearrange("p (h d) -> p h d", d=DH),
                                            AX_X, ALU.add).then_inc(S["sumsq"], 1)

                def invert_norms(g, first):
                    four = slice(first, first + 4) if isinstance(g, int) else bass.ds(first, 4)
                    dve.wait_ge(S["norms"], 4 * L + g + 1)
                    past(dve, S["inv_norm"], 4 * L + g)
                    nc.vector.tensor_scalar(nrm4[:, :, :], nrm[:, four], 1e-12, None,
                                            ALU.max).then_inc(S["norm_max"], 1)
                    dve.wait_ge(S["norm_max"], 4 * L + g + 1)
                    nc.vector.reciprocal(nrm4[:, :, :], nrm4[:, :, :]).then_inc(S["norm_over"], 1)
                    dve.wait_ge(S["norm_over"], 4 * L + g + 1)
                    nc.vector.tensor_scalar(ss[:, four], nrm4[:, :, :], 1.0, None, ALU.mult).then_inc(S["inv_norm"], 1)

                def take_group(g):
                    for j in range(4):
                        i, p = 4 * g + j, j % 2
                        if isinstance(g, int) and i == NT - 4:
                            rotate(0, 0)
                        dve.wait_ge(S["qkv"], 16 * L + i + 1)
                        nc.vector.tensor_tensor(
                            qk[:, i].rearrange("p (z h d) -> p z h d", z=2, d=DH),
                            ps[:, 2 * p:2 * p + 2].rearrange("p z (h d) -> p z h d", d=DH),
                            qks[:, :, :].rearrange("p z (o d) -> p z o d", o=1).broadcast_to((P, 2, HEADS, DH)),
                            ALU.mult).then_inc(S["qk_out"], 1)
                        if not isinstance(i, int) or i > 0:
                            sum_squares(i - 1, 1 - p)
                        if j == 1 and (not isinstance(g, int) or g > 0):
                            invert_norms(g - 1, 4 * g - 4)

                dve.wait_ge(S["w_qkv"], 48 * (L + 1))
                take_group(0)
                with dve.Fori(1, NT // 4 - 1) as g:
                    take_group(g)
                take_group(NT // 4 - 1)
                sum_squares(NT - 1, 1)
                rotate(1, 1)
                invert_norms(NT // 4 - 1, NT - 4)

                def soften(i, p):
                    scores = ps[:, 2:4].rearrange("p b (h k) -> p (b h) k", k=P)
                    dve.wait_ge(S["scores"], 16 * L + i + 1)
                    nc.vector.tensor_reduce(mx[:, p], scores, AX_X, ALU.max).then_inc(S["row_max"], 1)
                    dve.wait_ge(S["row_max"], 16 * L + i + 1)
                    past(dve, S["ptr"], 16 * L + i - 1)
                    nc.vector.tensor_tensor(
                        prob[:, p], scores,
                        mx[:, p].rearrange("p (h o) -> p h o", o=1).broadcast_to((P, HEADS, P)),
                        ALU.subtract).then_inc(S["less_max"], 1)

                def normalize(i, p):
                    dve.wait_ge(S["pv"], 16 * L + i + 1)
                    nc.vector.reciprocal(
                        rsum[:, p].rearrange("p (b h o) -> p b h o", b=2, o=1),
                        o_bank(ps)[:, :, :, DH:]).then_inc(S["row_sum"], 1)
                    dve.wait_ge(S["row_sum"], 16 * L + i + 1)
                    past(dve, S["otr"], 16 * L + i)
                    nc.vector.tensor_tensor(
                        ot[:, :].rearrange("p (b h d) -> p b h d", b=2, d=DH), o_bank(ps)[:, :, :, 0:DH],
                        rsum[:, p].rearrange("p (b h o) -> p b h o", b=2, o=1).broadcast_to((P, 2, 4, DH)),
                        ALU.mult).then_inc(S["o_norm"], 1)

                def add_attn(i):
                    dve.wait_ge(S["wo_mm"], 16 * L + i + 1)
                    nc.vector.tensor_tensor(K.y[:, i], K.y[:, i], ps[:, 0, 0:C], ALU.add).then_inc(S["y_attn"], 1)

                def half_stats(i):
                    dve.wait_ge(S["y_attn"], 16 * L + i + 1)
                    for z in range(2):
                        nc.vector.bn_stats(st[:, z, z, i, :], K.y[:, i, z * C // 2:(z + 1) * C // 2]
                                           ).then_inc(S["h_stat"], 1)

                def step(i, p):
                    if not isinstance(i, int) or i < NT:
                        soften(i, p)
                    if not isinstance(i, int) or 2 <= i:
                        add_attn(i - 2)
                    if not isinstance(i, int) or i + 2 < NT:
                        rotate(i + 2, p)
                    if not isinstance(i, int) or 1 <= i <= NT:
                        normalize(i - 1, 1 - p)
                    if not isinstance(i, int) or 2 <= i:
                        half_stats(i - 2)

                for i in range(2):
                    step(i, i)
                for i, p in steps(dve, 2, NT - 2):
                    step(i, p)
                for i in range(NT - 2, NT):
                    step(i, i % 2)

                def half_aggregate(k):
                    a, b = PARTS[k]
                    n = 6 * (b - a)
                    dve.wait_ge(S["exchanged"], 2 * L + k + 1)
                    for out, c0 in ((st[:, 0, 1, a:b], 0), (st[:, 1, 0, a:b], n)):
                        nc.vector.tensor_copy(out, ps[:, 2 + 2 * k, c0:c0 + n].rearrange("p (i s) -> p i s", s=6)
                                              ).then_inc(S["st_in"], 1)
                    if k == 0:
                        dve.wait_ge(S["z_set"], which + 1)
                        dve.wait_ge(S["st_in"], 5 * L + 2)
                        nc.vector.bn_stats(st[0:1, 0, 1, 0, :], zrow[:, 0:C // 2]).then_inc(S["st_in"], 1)
                    dve.wait_ge(S["st_in"], 5 * L + 3 + 2 * k)
                    for z in range(2):
                        for i in range(a, b):
                            nc.vector.bn_aggr(mvh[:, z, i, :], st[:, z, :, i, :]).then_inc(S["h_aggr"], 1)
                    dve.wait_ge(S["h_aggr"], 32 * L + 2 * b)
                    nc.vector.tensor_scalar(vareh[:, :, a:b], mvh[:, :, a:b, 1], LN_EPS, None,
                                            ALU.add).then_inc(S["h_var"], 1)

                def half_rstd(k):
                    a, b = PARTS[k]
                    dve.wait_ge(S["h_sd"], 2 * L + k + 1)
                    nc.vector.reciprocal(rstdh[:, :, a:b], sdh[:, :, a:b]).then_inc(S["h_rstd"], 1)
                    dve.wait_ge(S["h_rstd"], 2 * L + k + 1)

                def norm_group(g):
                    for i in range(4 * g, 4 * g + 4):
                        past(dve, S["h_tp"], 16 * L + i - 3)
                        for z in range(2):
                            cols = slice(z * C // 2, (z + 1) * C // 2)
                            nc.vector.tensor_scalar(hn[:, i % 4, cols], K.y[:, i, cols], mvh[:, z, i, 0:1],
                                                    rstdh[:, z, i:i + 1], ALU.subtract, ALU.mult
                                                    ).then_inc(S["h_norm"], 1)

                def add_mlp(g):
                    dve.wait_ge(S["w2_mm"], 4 * L + g + 1)
                    yg = K.y[:, 4 * g:4 * g + 4].rearrange("p i c -> p (i c)")
                    nc.vector.tensor_tensor(yg, yg, ps[:, 4 + g % 2, :], ALU.add).then_inc(S["y_mlp"], 1)
                    if l == DEPTH - 1:
                        xg = K.x[:, 4 * g:4 * g + 4].rearrange("p i c -> p (i c)")
                        dve.wait_ge(S["y_mlp"], 4 * L + g + 1)
                        nc.vector.scalar_tensor_tensor(out=xg, in0=yg, scalar=0.5, in1=xg,
                                                       op0=ALU.mult, op1=ALU.add).then_inc(S["x_ffn"], 1)
                        if which == 0:
                            dve.wait_ge(S["x_ffn"], g + 1)
                            ln_stats(nc, K, S, g)

                half_aggregate(0)
                add_attn(NT - 2)
                normalize(NT - 1, 1)
                half_stats(NT - 2)
                half_rstd(0)
                norm_group(0)
                past(dve, S["h_first_tp"], L)
                nc.vector.tensor_scalar(zn[:, :], zrow[:, :], mvh[0:1, 0, 0, 0:1], rstdh[0:1, 0, 0:1],
                                        ALU.subtract, ALU.mult).then_inc(S["h_first"], 1)
                add_attn(NT - 1)
                half_stats(NT - 1)
                half_aggregate(1)
                half_rstd(1)
                dve.wait_ge(S["w_mlp"], 208 * (L + 1))
                dve.wait_ge(S["hid_ones"], L + 1)
                for g in range(NT // 4):
                    if g + 1 < NT // 4:
                        norm_group(g + 1)
                    past(dve, S["w2_mm"], 4 * L + g - 1)
                    for c, (_, hc) in enumerate(CH):
                        u = NC_ * g + c
                        dve.wait_ge(S["gelu"], 12 * L + u + 1)
                        nc.vector.scalar_tensor_tensor(
                            out=hid[0:hc, g % 2, c, :], in0=ps[0:hc, 2 * (u % 2), :], scalar=b1[0:hc, c:c + 1],
                            in1=gel[0:hc, u % 2, :], op0=ALU.add, op1=ALU.mult).then_inc(S["gate"], 1)
                    if g >= 1:
                        add_mlp(g - 1)
                add_mlp(NT // 4 - 1)
        @block.scalar
        def _(act):
            ln_scalar(act, nc, K, S, 2 * which)
            for l in range(DEPTH):
                L = DEPTH * which + l
                def out_y(g):
                    n = 512 if g + 1 < NT // 4 else 511
                    act.wait_ge(S["tp"], 4 * L + g + 1)
                    nc.scalar.copy(yT[0:64, 512 * g:512 * g + 512], ps[0:64, 6 + g % 2, :]).then_inc(S["ht"], 1)
                    nc.scalar.copy(yT[64:P, 512 * g + 1:512 * g + 1 + n], ps[64:P, 6 + g % 2, 0:n]).then_inc(S["ht"], 1)

                def root_norms(g, first):
                    four = slice(first, first + 4) if isinstance(g, int) else bass.ds(first, 4)
                    act.wait_ge(S["sumsq"], 16 * L + first + 4)
                    nc.scalar.activation(nrm[:, four], ss[:, four], ACT.Sqrt).then_inc(S["norms"], 1)

                def out_qkv(g):
                    for j in range(4):
                        i, p = 4 * g + j, j % 2
                        act.wait_ge(S["qkv"], 16 * L + i + 1)
                        nc.scalar.copy(v[:, i + 1, :, 0:DH],
                                       ps[:, 4 + p].rearrange("p (h d) -> p h d", d=DH)).then_inc(S["v_out"], 1)
                        act.wait_ge(S["qk_out"], 16 * L + i + 1)
                        past(act, S["sumsq"], 16 * L + i - 1)
                        nc.scalar.activation(sq[:, p], ps[:, 2 * p:2 * p + 2].rearrange("p b n -> p (b n)"),
                                             ACT.Square).then_inc(S["squares"], 1)
                        if j == 0 and (not isinstance(g, int) or g > 0):
                            root_norms(g - 1, 4 * g - 4)

                act.wait_ge(S["v_ones"], 2 * (which + 1))
                out_y(0)
                out_y(1)
                for g in groups(act):
                    out_qkv(g)
                    if isinstance(g, int):
                        out_y(2)
                        out_y(3)

                def out_turned(i, p, z):
                    act.wait_ge(S["tq" if z == 0 else "tk"], 16 * L + i + 1)
                    past(act, S["scores"], 16 * L + i)
                    nc.scalar.copy(kt[:, :, p, :] if z else qt[:, p], ps[:, z].rearrange("p (c t) -> p c t", t=P)
                                   ).then_inc(S["qt" if z == 0 else "kt"], 1)

                def out_pt(i, p):
                    act.wait_ge(S["ptr"], 16 * L + i + 1)
                    past(act, S["pv"], 16 * L + i)
                    nc.scalar.copy(pt[:, :, :], ps[:, 4:6].rearrange("p b (h t) -> p (b h) t", t=P)).then_inc(S["pt"], 1)

                def out_ot(i):
                    act.wait_ge(S["otr"], 16 * L + i + 1)
                    past(act, S["wo_mm"], 16 * L + i)
                    nc.scalar.copy(oT[:, :, :], ps[:, 0].rearrange("p (b t) -> p b t", t=P)).then_inc(S["ot"], 1)

                def exps(i, p):
                    act.wait_ge(S["less_max"], 16 * L + i + 1)
                    nc.scalar.activation(prob[:, p], prob[:, p], ACT.Exp).then_inc(S["exps"], 1)

                def step(i, p):
                    if not isinstance(i, int) or 2 <= i:
                        out_ot(i - 2)
                    if not isinstance(i, int) or 1 <= i <= NT:
                        out_pt(i - 1, 1 - p)
                    if not isinstance(i, int) or i + 1 < NT:
                        out_turned(i + 1, 1 - p, 1)
                    if not isinstance(i, int) or i < NT:
                        exps(i, p)
                    if not isinstance(i, int) or i + 1 < NT:
                        out_turned(i + 1, 1 - p, 0)

                act.wait_ge(S["sumsq"], 16 * (L + 1))
                out_turned(0, 0, 1)
                out_turned(0, 0, 0)
                root_norms(NT // 4 - 1, NT - 4)
                for i in range(2):
                    step(i, i)
                for i, p in steps(act, 2, NT - 2):
                    step(i, p)
                for i in range(NT - 2, NT):
                    step(i, i % 2)

                def half_root(k):
                    a, b = PARTS[k]
                    act.wait_ge(S["h_var"], 2 * L + k + 1)
                    nc.scalar.activation(sdh[:, :, a:b], vareh[:, :, a:b], ACT.Sqrt).then_inc(S["h_sd"], 1)

                out_ot(NT - 2)
                out_pt(NT - 1, 1)
                half_root(0)
                out_ot(NT - 1)
                act.wait_ge(S["w_mlp"], 208 * (L + 1))

                def out_ht(g):
                    act.wait_ge(S["h_tp"], 16 * L + 4 * g + 4)
                    n = 512 if g + 1 < NT // 4 else 511
                    nc.scalar.activation(hT[0:64, 512 * g:512 * g + 512], ps[0:64, 6 + g % 2, :], ACT.Identity,
                                         bias=lnb[0:64, :], scale=lng[0:64, :]).then_inc(S["hT"], 1)
                    nc.scalar.activation(hT[64:P, 512 * g + 1:512 * g + 1 + n], ps[64:P, 6 + g % 2, 0:n], ACT.Identity,
                                         bias=lnb[64:P, :], scale=lng[64:P, :]).then_inc(S["hT"], 1)

                out_ht(0)
                act.wait_ge(S["h_first_tp"], L + 1)
                nc.scalar.activation(hT[64:P, 0:1], ps[64:P, 5, 0:1], ACT.Identity,
                                     bias=lnb[64:P, :], scale=lng[64:P, :]).then_inc(S["hT_first"], 1)
                half_root(1)
                for g in range(NT // 4):
                    for c, (_, hc) in enumerate(CH):
                        u = NC_ * g + c
                        act.wait_ge(S["w1_mm"], 12 * L + u + 1)
                        past(act, S["gate"], 12 * L + u - 1)
                        nc.scalar.activation(gel[0:hc, u % 2, :], ps[0:hc, 2 * (u % 2) + 1, :], ACT.Gelu,
                                             bias=b1[0:hc, NC_ + c:NC_ + c + 1]).then_inc(S["gelu"], 1)
                        if c == 1 and g + 1 < NT // 4:
                            out_ht(g + 1)

        @block.tensor
        def _(pe):
            if which == 0:
                pe.wait_ge(S["consts"], 48)
            for l in range(DEPTH):
                L = DEPTH * which + l

                def turn(L, g):
                    if L % DEPTH == 0:
                        pe.wait_ge(S["ln_y"], 32 * which + 4 * (g + 1))
                    else:
                        pe.wait_ge(S["y_mlp"], 4 * (L - 1) + g + 1)
                        pe.wait_ge(S["hT"], 8 * L)
                    past(pe, S["ht"], 8 * L + 2 * (g - 1))
                    for j in range(4):
                        mm = nc.tensor.transpose(ps[:, 6 + g % 2, j * P:(j + 1) * P], K.y[:, 4 * g + j], K.ident[:, :])
                    mm.then_inc(S["tp"], 1)

                def project(i):
                    p = i % 2
                    pe.wait_ge(S["ht"], 8 * L + 2 * (i // 4 + 1))
                    past(pe, S["qk_out"], 16 * L + i - 1)
                    past(pe, S["squares"], 16 * L + i - 1)
                    past(pe, S["v_out"], 16 * L + i - 1)
                    for z in range(3):
                        bank = 2 * p + z if z < 2 else 4 + p
                        mm = nc.tensor.matmul(ps[:, bank, :], yT[:, P * i:P * (i + 1)],
                                              wqkv[:, INNER * z:INNER * (z + 1)], start=True, stop=True)
                    mm.then_inc(S["qkv"], 1)

                if l == 0:
                    turn(L, 0)
                    turn(L, 1)
                else:
                    pe.wait_ge(S["y_mlp"], 4 * L)
                pe.wait_ge(S["w_qkv"], 48 * (L + 1))
                pe.wait_ge(S["first_zero"], L + 1)
                for i in range(NT):
                    project(i)
                    if i == 1:
                        turn(L, 2)
                        turn(L, 3)

                def turn_k(i, p):
                    pe.wait_ge(S["rot"], 16 * L + i + 1)
                    past(pe, S["kt"], 16 * L + i)
                    for b in range(4):
                        mm = nc.tensor.transpose(ps[:, 1, b * P:(b + 1) * P],
                                                 qk2[:, p, (4 + b) * P:(5 + b) * P], K.ident[:, :])
                    mm.then_inc(S["tk"], 1)

                def turn_q(i, p):
                    past(pe, S["qt"], 16 * L + i)
                    past(pe, S["y_attn"], 16 * L + i - 2)
                    for b in range(4):
                        mm = nc.tensor.transpose(ps[:, 0, b * P:(b + 1) * P], qk2[:, p, b * P:(b + 1) * P],
                                                 K.ident[:, :])
                    mm.then_inc(S["tq"], 1)

                def score(i, p):
                    past(pe, S["less_max"], 16 * L + i)
                    variant = (1 if p else 2) if not isinstance(i, int) or i else 0
                    for b, n in ((0, 4), (1, 3), (1, 1)):
                        if n == 1:
                            pe.wait_ge(S["kt"], 16 * L + i + 1)
                            pe.wait_ge(S["qt"], 16 * L + i + 1)
                        h0 = 3 if n == 1 else 0
                        nc.tensor.matmul(
                            ps[:, 2 + b, h0 * P:(h0 + n) * P].rearrange("p (h k) -> p h k", k=P), K.identb[:, :],
                            mask[:, variant].rearrange("p (o k) -> p o k", o=1).broadcast_to((P, n, P)),
                            start=(h0 == 0), stop=False, skip_group_check=True)
                    for h in range(HEADS):
                        r, b = DH * (h % 2), h // 2
                        out = ps[:, 2 + h % 2, b * P:(b + 1) * P]
                        windows = kt[r:r + DH, b].rearrange("p s (w t) -> p (s w) t", w=2)
                        nc.tensor.matmul(out[0:64, :].rearrange("p (w t) -> p w t", w=2), qt[r:r + DH, p, b, 0:64],
                                         windows[:, 1:3] if p else windows[:, 0:4:3],
                                         start=False, stop=True, skip_group_check=True)
                        mm = nc.tensor.matmul(out[64:P, :], qt[r:r + DH, p, b, 64:P], kt[r:r + DH, b, p, :],
                                              start=False, stop=True, skip_group_check=True)
                    mm.then_inc(S["scores"], 1)

                def turn_p(i, p):
                    pe.wait_ge(S["exps"], 16 * L + i + 1)
                    past(pe, S["pt"], 16 * L + i)
                    for h in range(HEADS):
                        mm = nc.tensor.transpose(ps[:, 4 + h // 4, (h % 4) * P:(h % 4 + 1) * P],
                                                 prob[:, p, h, :], K.ident[:, :])
                    mm.then_inc(S["ptr"], 1)

                def weigh(i, p, heads, v_staged):
                    if heads[0] == 0:
                        pe.wait_ge(S["pt"], 16 * L + i + 1)
                        pe.wait_ge(S["v_stage"][p], v_staged)
                        past(pe, S["o_norm"], 16 * L + i)
                    for h in heads:
                        out = o_bank(ps)[:, h // 4, h % 4, :]
                        s = 4 * (h % 2) + h // 2
                        nc.tensor.matmul(out[0:64], pt[:, s, 0:64], ve[:, p, h, :], start=True, stop=True)
                        mm = nc.tensor.matmul(out[64:P], pt[:, s, 64:P], vs[:, p, h, :], start=True, stop=True)
                    if heads[-1] == HEADS - 1:
                        mm.then_inc(S["pv"], 1)

                def turn_o(i, q_out):
                    pe.wait_ge(S["o_norm"], 16 * L + i + 1)
                    pe.wait_ge(S["qt"], q_out)
                    for b in range(4):
                        mm = nc.tensor.transpose(ps[:, 0, b * P:(b + 1) * P], ot[:, b * P:(b + 1) * P], K.ident[:, :])
                    mm.then_inc(S["otr"], 1)

                def output(i):
                    pe.wait_ge(S["ot"], 16 * L + i + 1)
                    for b in range(4):
                        mm = nc.tensor.matmul(ps[:, 0, 0:C], oT[:, b, :], wo[:, b, :], start=(b == 0), stop=(b == 3))
                    mm.then_inc(S["wo_mm"], 1)

                def step(i, p, v_staged):
                    static = isinstance(i, int)
                    if not static or i < NT:
                        score(i, p)
                    if not static or 2 <= i:
                        turn_o(i - 2, 16 * L + (min(i + 1, NT) if static else i + 1))
                    if not static or 1 <= i <= NT:
                        turn_p(i - 1, 1 - p)
                    if not static or 2 <= i:
                        output(i - 2)
                    if not static or i + 1 < NT:
                        turn_k(i + 1, 1 - p)
                    if not static or 1 <= i <= NT:
                        weigh(i - 1, 1 - p, range(0, 4), v_staged)
                    if not static or i + 1 < NT:
                        turn_q(i + 1, 1 - p)
                    if not static or 1 <= i <= NT:
                        weigh(i - 1, 1 - p, range(4, HEADS), v_staged)

                pe.wait_ge(S["w_o"], 16 * (L + 1))
                pe.wait_ge(S["const_b"], 2 + which)
                pe.wait_ge(S["qk_out"], 16 * L + NT - 1)
                pe.wait_ge(S["squares"], 16 * L + NT - 1)
                turn_k(0, 0)
                turn_q(0, 0)
                pe.wait_ge(S["qk_out"], 16 * (L + 1))
                pe.wait_ge(S["squares"], 16 * (L + 1))
                pe.wait_ge(S["v_out"], 16 * (L + 1))
                for i in range(2):
                    step(i, i, 48 * (8 * L + 1))
                with pe.Fori(1, NT // 2 - 1) as pair:
                    for p in range(2):
                        step(2 * pair + p, p, 48 * (pair + (8 * L + p)))
                def exchange(k):
                    a, b = PARTS[k]
                    n = 6 * (b - a)
                    second = st[:, 1, 1].rearrange("p i s -> p (i s)")
                    first = st[:, 0, 0].rearrange("p i s -> p (i s)")
                    pe.wait_ge(S["h_stat"], 32 * L + 2 * min(b + 1, NT))
                    pe.wait_ge(S["less_max"], 16 * (L + 1))
                    out = ps[:, 2 + 2 * k]
                    a1, b1 = max(a, 1), min(b, NT - 1)
                    nc.tensor.matmul(out[:, 0:n], shifts[:, P - 1:2 * P - 1], second[:, 6 * a:6 * b],
                                     start=True, stop=True, skip_group_check=True)
                    nc.tensor.matmul(out[:, 6 * (a1 - a):n], shifts[:, 2 * P - 1:3 * P - 1],
                                     second[:, 6 * (a1 - 1):6 * (b - 1)], start=False, stop=True, skip_group_check=True)
                    nc.tensor.matmul(out[:, n:2 * n], shifts[:, P + 1:2 * P + 1], first[:, 6 * a:6 * b],
                                     start=True, stop=True, skip_group_check=True)
                    mm = nc.tensor.matmul(out[:, n:n + 6 * (b1 - a)], shifts[:, 1:P + 1],
                                          first[:, 6 * (a + 1):6 * (b1 + 1)], start=False, stop=True,
                                          skip_group_check=True)
                    if b == NT:
                        mm = nc.tensor.matmul(out[:, 2 * n - 6:2 * n], shifts[:, 1:P + 1], first[:, 0:6],
                                              start=False, stop=True, skip_group_check=True)
                    mm.then_inc(S["exchanged"], 1)

                last_v = 48 * (8 * L + 8)
                for i in range(NT - 2, NT):
                    step(i, i % 2, 48 * (8 * L + (i - 1) // 2 + 1))
                turn_o(NT - 2, 16 * (L + 1))
                exchange(0)
                turn_p(NT - 1, 1)
                output(NT - 2)
                weigh(NT - 1, 1, range(HEADS), last_v)
                turn_o(NT - 1, 16 * (L + 1))
                output(NT - 1)

                def turn_h(g):
                    past(pe, S["hT"], 8 * L + 2 * (g - 1))
                    for i in range(4 * g, 4 * g + 4):
                        pe.wait_ge(S["h_norm"], 32 * L + 2 * i + 2)
                        nc.tensor.transpose(ps[:, 6 + g % 2, (i % 4) * P:(i % 4 + 1) * P], hn[:, i % 4, :],
                                            K.ident[:, :]).then_inc(S["h_tp"], 1)

                def down(g):
                    pe.wait_ge(S["gate"], 12 * L + NC_ * (g + 1))
                    past(pe, S["y_mlp"], 4 * L + g - 1)
                    for j in range(4):
                        for c, (_, hc) in enumerate(CH):
                            rows = hc + (c == NC_ - 1)
                            mm = nc.tensor.matmul(ps[:, 4 + g % 2, j * P:(j + 1) * P],
                                                  hid[0:rows, g % 2, c, j * P:(j + 1) * P], w2[0:rows, c, :],
                                                  start=(c == 0), stop=(c == NC_ - 1))
                    mm.then_inc(S["w2_mm"], 1)

                pe.wait_ge(S["w_mlp"], 208 * (L + 1))
                pe.wait_ge(S["o_norm"], 16 * (L + 1))
                turn_h(0)
                pe.wait_ge(S["h_first"], L + 1)
                nc.tensor.transpose(ps[:, 5, 0:1], zn[:, :], K.ident[0:1, 0:1]).then_inc(S["h_first_tp"], 1)
                exchange(1)
                pe.wait_ge(S["y_attn"], 16 * (L + 1))
                for g in range(NT // 4):
                    pe.wait_ge(S["hT"], 8 * L + 2 * (g + 1))
                    pe.wait_ge(S["hT_first"], L + 1)
                    for c, (h0, hc) in enumerate(CH):
                        u = NC_ * g + c
                        past(pe, S["gate"], 12 * L + u - 1)
                        for half in range(2):
                            mm = nc.tensor.matmul(ps[0:hc, 2 * (u % 2) + half, :],
                                                  w1[:, half * HID + h0:half * HID + h0 + hc],
                                                  hT[:, 512 * g:512 * g + 512], start=True, stop=True)
                        mm.then_inc(S["w1_mm"], 1)
                        if c == 1 and g + 1 < NT // 4:
                            turn_h(g + 1)
                        if c == 0 and g >= 1:
                            down(g - 1)
                if l + 1 < DEPTH:
                    turn(L + 1, 0)
                    turn(L + 1, 1)
                down(NT // 4 - 1)


CHUNKS = (0, 2, 3, 1)
WORK = [(c, g) for c in CHUNKS for g in range(NG)]


def key_steps(n):
    return 4 * (WORK[n][0] + 1)


def max_units(n):
    c = WORK[n][0]
    return [(j, h, part) for j in range(4) for h in range(HG) for part in range(c + 1)]


MAX_BASE = [sum(len(max_units(m)) for m in range(n)) for n in range(len(WORK) + 1)]
KEY_BASE = [sum(key_steps(m) for m in range(n)) for n in range(len(WORK) + 1)]
KEY_STEPS = [(n, kt) for n in range(len(WORK)) for kt in range(key_steps(n))]


def lay_out():
    maxima, bank = [], []
    done, turned = MAX_BASE[1], 2
    for s, (n, kt) in enumerate(KEY_STEPS):
        rate = [-(-(MAX_BASE[m + 1] - done) // max(1, KEY_BASE[m] - 4 - s))
                for m in range(1, len(WORK)) if MAX_BASE[m + 1] > done]
        new = min(done + max(rate, default=0), MAX_BASE[turned])
        job = None
        if n >= 1 and kt == 1:
            job = ("acc", n - 1)
        elif n + 1 < len(WORK) and kt == key_steps(n) - 2:
            job = ("q", n + 1)
        elif n >= NG and n % NG == 0 and kt in (2, 3) and n + 1 < len(WORK) and key_steps(n) > 4:
            job = ("ot" if kt == 2 else "proj", n // NG - 1)
        elif turned < len(WORK) and done >= MAX_BASE[turned - 1]:
            job = ("qm", turned)
            turned += 1
        maxima.append(range(done, new))
        bank.append(job)
        done = new
    return maxima, bank


MAX_UNITS = [(n, *unit) for n in range(len(WORK)) for unit in max_units(n)]
MAX_AT, MISC_AT = lay_out()
MISC_ORDER = ([("qm", 0), ("qm", 1), ("q", 0)] + [job for job in MISC_AT if job]
              + [("acc", len(WORK) - 1), ("ot", NQ - 1), ("proj", NQ - 1)])


def causal_block(nc, K, S, dram):
    with ExitStack() as stack:
        def sb(name, shape, dt=F32):
            return stack.enter_context(nc.sbuf_tensor(f"c_{name}", shape, dt))

        qs = sb("qs", [P, NT, H2, SLOT])
        ks = sb("ks", [P, NT, H2, SLOT])
        vv = sb("vv", [P, NT, H2, SLOT])
        kT = sb("kT", [P, NG, T], F32R)
        qmT = sb("qmT", [P, 2, HG, 512], F32R)
        qT = sb("qT", [P, 2, HG, 512], F32R)
        own = sb("own", [P, HG])
        pr = sb("pr", [P, 2, HG, 512])
        watt = sb("watt", [P, 3 * C])
        batt = sb("batt", [P, 3 * C])
        wproj = sb("wproj", [P, C])
        bproj = sb("bproj", [P, C])
        r2c = sb("r2c", [P, NT, D2 // 2])
        r2s = sb("r2s", [P, NT, 2, D2 // 2])
        cmf = sb("cmf", [P, 2, P])
        cmask = sb("cmask", [P, 2, P], BF16)
        acc = sb("acc", [P, 512])
        spare = pr[:, :, :, :].rearrange("p s h t -> p (s h t)")
        raw = spare[:, 0:2048].rearrange("p (s i n) -> p s i n", s=2, i=4)
        cb = spare[:, 3072:4096].rearrange("p (i n) -> p i n", i=4)
        hi = kT[:, NG - 1, T - 1024:T].rearrange("p (i n) -> p i n", i=4)
        yT2 = sb("yT2", [P, 512])
        oT = yT2
        mparts = sb("mparts", [P, 2, 4 * HG, NQ])
        m16 = sb("m16", [P, 4 * HG])
        neg = sb("neg", [P, 4 * HG])
        neghi = sb("neghi", [P, 4 * HG], F32R)
        rsum = sb("rsum", [P, 4, HG])
        o = K.y[:, :, :]
        ps = stack.enter_context(nc.psum_tensor("c_ps", [P, 8, 512], F32))
        MX, ACC, MISC = 4, 6, 7

        yT = (acc[:, :], yT2[:, :])

        def slots(ap):
            return ap.rearrange("p i (h d) -> p i h d", d=D2)

        block = stack.enter_context(nc.Block())

        @block.sync
        def _(sp):
            sp.dma_start(watt[:, :], dram["W_attn"]).then_inc(S["c_in"], 16)
            sp.dma_start(wproj[:, :], dram["W_proj"]).then_inc(S["c_in"], 16)
            sp.dma_start(batt[:, :], dram["b_attn"].partition_broadcast(P)).then_inc(S["c_in"], 16)
            sp.dma_start(bproj[:, :], dram["b_proj"].partition_broadcast(P)).then_inc(S["c_in"], 16)
            sp.dma_start(cmf[:, :, :], dram["causal_mask"]).then_inc(S["c_in"], 16)
            sp.dma_start(own[:, :], dram["own"]).then_inc(S["c_in"], 16)
            sp.dma_start(r2c[:, :, :], dram["rope2_c"]).then_inc(S["c_in"], 16)
            sp.dma_start(r2s[:, :, :, :], dram["rope2_s"]).then_inc(S["c_in"], 16)

        @block.gpsimd
        def _(pool):
            nc.gpsimd.memset(qs[:, :, :, MROW:], 0.0).then_inc(S["c_zero"], 1)
            nc.gpsimd.memset(ks[:, :, :, MROW:MROW + 2], 1.0).then_inc(S["c_zero"], 1)
            nc.gpsimd.memset(ks[:, :, :, MROW + 2:], 0.0).then_inc(S["c_zero"], 1)
            nc.gpsimd.memset(vv[:, :, :, D2:D2 + 1], 1.0).then_inc(S["c_zero"], 1)
            nc.gpsimd.memset(vv[:, :, :, D2 + 1:], 0.0).then_inc(S["c_zero"], 1)
            pool.wait_ge(S["c_in"], 16 * 8)
            pool.wait_ge(S["ln_y"], 32)

            for g in range(NT // 4):
                pool.wait_ge(S["c_sin"], 2 * (g + 1))
                qk = raw[:, g % 2, :, 0:2 * C].rearrange("p i (m d) -> p i m d", d=4)
                nc.gpsimd.tensor_tensor(
                    qk, qk, r2c[:, 4 * g:4 * g + 4].rearrange("p i (o d) -> p i o d", o=1).broadcast_to((P, 4, 64, 4)),
                    ALU.mult).then_inc(S["c_cos"], 1)
            nc.gpsimd.tensor_tensor(
                K.x[:, :, :], K.x[:, :, :],
                bproj[:, :].rearrange("p (o c) -> p o c", o=1).broadcast_to((P, NT, C)), ALU.add).then_inc(S["c_xb"], 1)

        @block.vector
        def _(dve):
            ln_vector(dve, nc, K, S, 1)
            dve.wait_ge(S["c_in"], 16 * 8)
            nc.vector.tensor_copy(cmask[:, :, :], cmf[:, :, :]).then_inc(S["c_bias"], 1)

            def biased(g):
                dve.wait_ge(S["c_qkv"], g + 1)
                past(dve, S["c_lo"], 2 * (g - 1))
                b = 3 * (g % 2)
                nc.vector.tensor_tensor(
                    raw[:, g % 2], ps[:, b:b + 2].rearrange("p b (i n) -> p (b i) n", n=2 * C),
                    batt[:, 0:2 * C].rearrange("p (o n) -> p o n", o=1).broadcast_to((P, 4, 2 * C)),
                    ALU.add).then_inc(S["c_biased"], 1)
                bv = batt[:, 2 * C:].rearrange("p (o h d) -> p o h d", o=1, d=D2)
                nc.vector.tensor_tensor(
                    vv[:, 4 * g:4 * g + 4, :, 0:D2], slots(ps[:, b + 2].rearrange("p (i n) -> p i n", n=C)),
                    bv.broadcast_to((P, 4, H2, D2)), ALU.add).then_inc(S["c_v"], 1)

            def sine(g):
                dve.wait_ge(S["c_biased"], g + 1)
                past(dve, S["c_rot"], g)
                for a in range(2):
                    halves = raw[:, g % 2, :, 0:2 * C].rearrange("p i (h a d) -> p i h a d", a=2, d=4)
                    nc.vector.tensor_tensor(
                        cb[:, :, :].rearrange("p i (h a d) -> p i h a d", a=2, d=4)[:, :, :, a],
                        halves[:, :, :, 1 - a],
                        r2s[:, 4 * g:4 * g + 4, a].rearrange("p i (o d) -> p i o d", o=1).broadcast_to((P, 4, 32, 4)),
                        ALU.mult).then_inc(S["c_sin"], 1)

            def parts(g):
                dve.wait_ge(S["c_cos"], g + 1)
                qk = raw[:, g % 2, :, 0:2 * C]
                dve.wait_ge(S["c_sin"], 2 * (g + 1))
                nc.vector.tensor_tensor(qk, qk, cb[:, :, :], ALU.add).then_inc(S["c_rot"], 1)
                dve.wait_ge(S["c_rot"], g + 1)
                past(dve, S["c_qs"], 2 * g)
                nc.vector.tensor_copy(hi[:, :, :], qk).then_inc(S["c_hi"], 1)
                dve.wait_ge(S["c_hi"], g + 1)
                for z, out in ((0, qs[:, 4 * g:4 * g + 4, :, 16:24]), (1, ks[:, 4 * g:4 * g + 4, :, 8:16])):
                    nc.vector.tensor_tensor(out, slots(qk[:, :, z * C:(z + 1) * C]),
                                            slots(hi[:, :, z * C:(z + 1) * C].bitcast(F32)),
                                            ALU.subtract).then_inc(S["c_lo"], 1)

            for g in range(NT // 4):
                biased(g)
                if g >= 1:
                    parts(g - 1)
                sine(g)
            parts(NT // 4 - 1)

            def finish_max(n):
                c, g = WORK[n]
                dve.wait_ge(S["c_max"], MAX_BASE[n + 1])
                past(dve, S["c_neg"], n)
                nc.vector.tensor_reduce(m16[:, :], mparts[:, n % 2, :, 0:c + 1], AX_X, ALU.max).then_inc(S["c_mfin"], 1)
                dve.wait_ge(S["c_mfin"], n + 1)
                past(dve, S["c_mlo"], n)
                nc.vector.tensor_scalar(neg[:, :], m16[:, :], -1.0, None, ALU.mult).then_inc(S["c_neg"], 1)
                dve.wait_ge(S["c_neg"], n + 1)
                nc.vector.tensor_copy(neghi[:, :], neg[:, :]).then_inc(S["c_neghi"], 1)
                dve.wait_ge(S["c_neghi"], n + 1)
                dve.wait_ge(S["c_qm_tp"], n + 1)
                high = neghi[:, :].bitcast(F32).rearrange("p (j h) -> p j h", h=HG)
                nc.vector.tensor_copy(qs[:, 4 * c:4 * c + 4, HG * g:HG * (g + 1), MROW], high).then_inc(S["c_mrow"], 1)
                nc.vector.tensor_tensor(qs[:, 4 * c:4 * c + 4, HG * g:HG * (g + 1), MROW + 1],
                                        neg[:, :].rearrange("p (j h) -> p j h", h=HG), high,
                                        ALU.subtract).then_inc(S["c_mlo"], 1)

            def take_out(n):
                dve.wait_ge(S["c_pv"], KEY_BASE[n + 1])
                past(dve, S["c_acc_tp"], n)
                nc.vector.tensor_copy(acc[:, :], ps[:, ACC, :]).then_inc(S["c_acc"], 1)

            def finish_out(n):
                c, g = WORK[n]
                dve.wait_ge(S["c_acc_tp"], n + 1)
                past(dve, S["c_o"], n)
                by_head = ps[:, MISC].rearrange("p (j h d) -> p j h d", j=4, d=SLOT)
                nc.vector.reciprocal(rsum[:, :, :], by_head[:, :, :, D2]).then_inc(S["c_rsum"], 1)
                dve.wait_ge(S["c_rsum"], n + 1)
                nc.vector.tensor_tensor(
                    o[:, 4 * c:4 * c + 4, 32 * g:32 * (g + 1)].rearrange("p j (h d) -> p j h d", d=D2),
                    by_head[:, :, :, 0:D2],
                    rsum[:, :, :].rearrange("p j (h o) -> p j h o", o=1).broadcast_to((P, 4, HG, D2)),
                    ALU.mult).then_inc(S["c_o"], 1)

            def unit_max(unit):
                n, j, h, part = MAX_UNITS[unit]
                width = 512 if part < WORK[n][0] else P * (j + 1)
                dve.wait_ge(S["c_mx"], unit + 1)
                past(dve, S["c_mfin"], n - 1)
                nc.vector.tensor_reduce(mparts[:, n % 2, HG * j + h, part:part + 1],
                                        ps[:, MX + unit % 2, 0:width], AX_X, ALU.max).then_inc(S["c_max"], 1)
                if unit + 1 == MAX_BASE[n + 1]:
                    finish_max(n)

            def add_chunk(m):
                c = CHUNKS[m]
                dve.wait_ge(S["c_xb"], 1)
                dve.wait_ge(S["c_proj"], m + 1)
                xc = K.x[:, 4 * c:4 * c + 4].rearrange("p i c -> p (i c)")
                nc.vector.tensor_tensor(xc, xc, ps[:, MISC], ALU.add).then_inc(S["x_attn"], 1)
                dve.wait_ge(S["x_attn"], m + 1)
                ln_stats(nc, K, S, c)

            for unit in range(MAX_BASE[1]):
                unit_max(unit)
            for s, (n, kt) in enumerate(KEY_STEPS):
                for unit in MAX_AT[s]:
                    unit_max(unit)
                if n >= 1 and kt == 0:
                    take_out(n - 1)
                if n >= 1 and kt == 1:
                    finish_out(n - 1)
                if MISC_AT[s] and MISC_AT[s][0] == "proj":
                    add_chunk(MISC_AT[s][1])
            take_out(len(WORK) - 1)
            finish_out(len(WORK) - 1)

            add_chunk(NQ - 1)

        @block.scalar
        def _(act):
            ln_scalar(act, nc, K, S, 1)
            def spread(n, heads, out, turned, done):
                act.wait_ge(turned, n + 1)
                for h in heads:
                    nc.scalar.activation(out[:, n % 2, h], ps[:, MISC], ACT.Identity,
                                         scale=own[:, h:h + 1]).then_inc(done, 1)

            def spread_qm(n, heads):
                past(act, S["c_mx"], MAX_BASE[n - 1] if n else 0)
                spread(n, heads, qmT, S["c_qm_tp"], S["c_qm"])

            def out_turned(t):
                act.wait_ge(S["c_tp"], t + 1)
                if t < 4:
                    past(act, S["c_qkv"], t - 1)
                    out = yT[t % 2]
                else:
                    out = kT[:, t % 4, 512 * (t // 4 - 1):512 * (t // 4)]
                nc.scalar.copy(out, ps[:, 6 + t % 2]).then_inc(S["c_turned"], 1)

            def high_parts(g):
                four = slice(4 * g, 4 * g + 4)
                act.wait_ge(S["c_hi"], g + 1)
                high = hi[:, :, :].bitcast(F32)
                for a in range(2):
                    nc.scalar.copy(ks[:, four, :, 2 * D2 * a:2 * D2 * a + D2], slots(high[:, :, C:])
                                   ).then_inc(S["c_ks"], 1)
                for a in range(2):
                    nc.scalar.copy(qs[:, four, :, D2 * a:D2 * (a + 1)], slots(high[:, :, 0:C])).then_inc(S["c_qs"], 1)

            out_turned(0)
            out_turned(1)
            act.wait_ge(S["c_zero"], 5)
            for g in range(NT // 4):
                if g + 2 < 4:
                    out_turned(g + 2)
                high_parts(g)
                if g >= 1:
                    for t in range(4 * g, 4 * g + 4):
                        out_turned(t)
                if g == 1:
                    spread_qm(0, range(HG))
                    spread_qm(1, range(HG))
            for t in range(16, 20):
                out_turned(t)

            def spread_q(n, heads):
                past(act, S["c_st"], 2 * KEY_BASE[n - 1] if n else 0)
                spread(n, heads, qT, S["c_q_tp"], S["c_q"])

            def exps(n, kt, pair):
                c = WORK[n][0]
                step = KEY_BASE[n] + kt
                off = P * max(0, kt - 4 * c)
                unit = 2 * step + pair
                act.wait_ge(S["c_st"], unit + 1)
                past(act, S["c_pv"], step - 1)
                nc.scalar.activation(pr[:, step % 2, 2 * pair:2 * pair + 2, off:],
                                     ps[:, 2 * (unit % 2):2 * (unit % 2) + 2, off:], ACT.Exp,
                                     scale=float(D2) ** -0.5).then_inc(S["c_exp"], 1)

            def out_ot(m):
                act.wait_ge(S["c_ot_tp"], m + 1)
                past(act, S["c_proj"], m)
                nc.scalar.copy(oT[:, :], ps[:, MISC]).then_inc(S["c_ot"], 1)

            def spread_job(s, heads):
                if MISC_AT[s] and MISC_AT[s][0] == "ot" and heads[0] == 0:
                    out_ot(MISC_AT[s][1])
                if MISC_AT[s] and MISC_AT[s][0] == "qm":
                    spread_qm(MISC_AT[s][1], heads)
                if MISC_AT[s] and MISC_AT[s][0] == "q":
                    spread_q(MISC_AT[s][1], heads)

            spread_q(0, range(HG))
            for s, (n, kt) in enumerate(KEY_STEPS):
                exps(n, kt, 0)
                spread_job(s, (0, 1))
                exps(n, kt, 1)
                spread_job(s, (2, 3))
            out_ot(NQ - 1)

        @block.tensor
        def _(pe):
            def group(ap, t, g):
                return ap[:, t, HG * g:HG * (g + 1)].rearrange("p h s -> p (h s)")

            def turn_next(t):
                past(pe, S["c_turned"], t - 1)
                if t < 4:
                    pe.wait_ge(S["ln_y"], 16 + 4 * (t + 1))
                else:
                    pe.wait_ge(S["c_ks"], 2 * (t // 4))
                    pe.wait_ge(S["c_lo"], 8 if t == 15 else 2 * (t // 4))
                    pe.wait_ge(S["c_zero"], 5)
                for j in range(4):
                    src = K.y[:, 4 * t + j] if t < 4 else group(ks, 4 * (t // 4 - 1) + j, t % 4)
                    mm = nc.tensor.transpose(ps[:, 6 + t % 2, P * j:P * (j + 1)], src, K.ident[:, :])
                mm.then_inc(S["c_tp"], 1)

            def project(g):
                pe.wait_ge(S["c_turned"], g + 1)
                past(pe, S["c_v"], g - 1)
                for j in range(4):
                    yj = yT[g % 2][:, P * j:P * (j + 1)]
                    nc.tensor.matmul(ps[:, 3 * (g % 2) + j // 2, 2 * C * (j % 2):2 * C * (j % 2 + 1)], yj,
                                     watt[:, 0:2 * C], start=True, stop=True)
                    mm = nc.tensor.matmul(ps[:, 3 * (g % 2) + 2, C * j:C * (j + 1)], yj, watt[:, 2 * C:],
                                          start=True, stop=True)
                mm.then_inc(S["c_qkv"], 1)

            turn_next(0)
            turn_next(1)
            pe.wait_ge(S["c_in"], 16 * 8)
            for g in range(NT // 4):
                project(g)
                if g + 2 < 4:
                    turn_next(g + 2)
            def misc_free(kind, n):
                k = MISC_ORDER.index((kind, n))
                if k:
                    before, m = MISC_ORDER[k - 1]
                    if before == "acc":
                        pe.wait_ge(S["c_o"], m + 1)
                    elif before == "ot":
                        pe.wait_ge(S["c_ot"], m + 1)
                    elif before == "proj":
                        pe.wait_ge(S["x_attn"], m + 1)
                    elif before == "q":
                        pe.wait_ge(S["c_q"], HG * (m + 1))
                    else:
                        pe.wait_ge(S["c_qm"], HG * (m + 1))

            def turn_queries(kind, n):
                c, g = WORK[n]
                misc_free(kind, n)
                if kind == "q":
                    pe.wait_ge(S["c_mrow"], n + 1)
                    pe.wait_ge(S["c_mlo"], n + 1)
                for j in range(4):
                    mm = nc.tensor.transpose(ps[:, MISC, P * j:P * (j + 1)], group(qs, 4 * c + j, g), K.ident[:, :])
                mm.then_inc(S["c_q_tp" if kind == "q" else "c_qm_tp"], 1)

            def max_unit(unit):
                n, j, h, part = MAX_UNITS[unit]
                c, g = WORK[n]
                if unit == MAX_BASE[n]:
                    pe.wait_ge(S["c_qm"], HG * (n + 1))
                last = part == c
                width = P * (j + 1) if last else 512
                past(pe, S["c_max"], unit - 1)
                out = ps[:, MX + unit % 2, :]
                mm = nc.tensor.matmul(out[:, 0:width], qmT[:, n % 2, h, P * j:P * (j + 1)],
                                      kT[:, g, 512 * part:512 * part + width], start=True, stop=True)
                if last:
                    mm = nc.tensor.matmul(out[:, width - P:width], K.identb[:, :], cmask[:, 0, :],
                                          start=False, stop=True, skip_group_check=True)
                mm.then_inc(S["c_mx"], 1)

            def score_pair(n, kt, pair):
                c, g = WORK[n]
                unit = 2 * (KEY_BASE[n] + kt) + pair
                off = P * max(0, kt - 4 * c)
                past(pe, S["c_exp"], unit - 1)
                for a in range(2):
                    out = ps[:, 2 * (unit % 2) + a, :]
                    mm = nc.tensor.matmul(out[:, off:], kT[:, g, P * kt:P * (kt + 1)], qT[:, n % 2, 2 * pair + a, off:],
                                          start=True, stop=True)
                    if kt >= 4 * c:
                        mm = nc.tensor.matmul(out[:, off:off + P], K.identb[:, :], cmask[:, 1, :],
                                              start=False, stop=True, skip_group_check=True)
                mm.then_inc(S["c_st"], 1)

            def weigh(n, kt):
                c, g = WORK[n]
                step = KEY_BASE[n] + kt
                off = P * max(0, kt - 4 * c)
                pe.wait_ge(S["c_exp"], 2 * step + 2)
                if kt == 0:
                    past(pe, S["c_acc"], n)
                for h in range(HG):
                    mm = nc.tensor.matmul(ps[SLOT * h:SLOT * (h + 1), ACC, off:], vv[:, kt, HG * g + h, :],
                                          pr[:, step % 2, h, off:], start=(kt == 0), stop=(kt >= 4 * c),
                                          skip_group_check=True)
                mm.then_inc(S["c_pv"], 1)

            def turn_acc(n):
                misc_free("acc", n)
                pe.wait_ge(S["c_acc"], n + 1)
                for j in range(4):
                    mm = nc.tensor.transpose(ps[:, MISC, P * j:P * (j + 1)], acc[:, P * j:P * (j + 1)], K.ident[:, :])
                mm.then_inc(S["c_acc_tp"], 1)

            def turn_out(m):
                misc_free("ot", m)
                pe.wait_ge(S["c_o"], NG * (m + 1))
                for j in range(4):
                    mm = nc.tensor.transpose(ps[:, MISC, P * j:P * (j + 1)], o[:, 4 * CHUNKS[m] + j, :], K.ident[:, :])
                mm.then_inc(S["c_ot_tp"], 1)

            def project_out(m):
                misc_free("proj", m)
                for j in range(4):
                    mm = nc.tensor.matmul(ps[:, MISC, P * j:P * (j + 1)], oT[:, P * j:P * (j + 1)],
                                          wproj[:, :], start=True, stop=True)
                mm.then_inc(S["c_proj"], 1)

            for t in range(4, 8):
                turn_next(t)
            pe.wait_ge(S["c_turned"], 8)
            pe.wait_ge(S["c_qs"], 2)
            turn_queries("qm", 0)
            turn_queries("qm", 1)
            pe.wait_ge(S["c_qm"], 2 * HG)
            for t in range(8, 12):
                turn_next(t)
            pe.wait_ge(S["c_bias"], 1)
            pe.wait_ge(S["c_v"], NT // 4)
            for t in range(12, 20):
                turn_next(t)
                for unit in range(MAX_BASE[1] * (t - 12) // 8, MAX_BASE[1] * (t - 11) // 8):
                    max_unit(unit)
            pe.wait_ge(S["c_turned"], 20)
            pe.wait_ge(S["c_qs"], 2 * NT // 4)
            turn_queries("q", 0)
            for s, (n, kt) in enumerate(KEY_STEPS):
                lots = [MAX_AT[s][len(MAX_AT[s]) * q // 4:len(MAX_AT[s]) * (q + 1) // 4] for q in range(4)]
                for unit in lots[0]:
                    max_unit(unit)
                if kt == 0:
                    pe.wait_ge(S["c_q"], HG * (n + 1))
                score_pair(n, kt, 0)
                for unit in lots[1]:
                    max_unit(unit)
                score_pair(n, kt, 1)
                if MISC_AT[s] and MISC_AT[s][0] == "acc":
                    turn_acc(MISC_AT[s][1])
                elif MISC_AT[s] and MISC_AT[s][0] == "ot":
                    turn_out(MISC_AT[s][1])
                elif MISC_AT[s] and MISC_AT[s][0] == "proj":
                    project_out(MISC_AT[s][1])
                elif MISC_AT[s]:
                    turn_queries(*MISC_AT[s])
                for unit in lots[2]:
                    max_unit(unit)
                if s >= 1:
                    weigh(*KEY_STEPS[s - 1])
                for unit in lots[3]:
                    max_unit(unit)
            weigh(*KEY_STEPS[-1])
            turn_acc(len(WORK) - 1)

            turn_out(NQ - 1)
            project_out(NQ - 1)


def build(nc, dram):
    with ExitStack() as stack:
        K = Keep(nc, stack)
        S = {name: stack.enter_context(nc.semaphore(name)) for name in SEMS.split()}
        S["v_stage"] = [stack.enter_context(nc.semaphore(f"v_stage{p}")) for p in range(2)]
        ffn_block(nc, K, S, dram, 0)
        causal_block(nc, K, S, dram)
        ffn_block(nc, K, S, dram, 1)


SEMS = """first_zero x_in consts rope_in const_b x_attn x_ffn stored
ln_stat ln_aggr ln_var ln_sd ln_rstd ln_y
w_qkv w_o w_mlp exchanged v_ones z_set st_in
tp ht qkv squares v_out sumsq qk_out norms norm_max norm_over inv_norm
unit cos_part sin_part rot tq tk qt kt scores row_max less_max exps ptr pt pv row_sum o_norm otr ot wo_mm y_attn
hid_ones h_first h_first_tp hT_first h_stat h_aggr h_var h_sd h_rstd h_norm h_tp hT w1_mm gelu gate w2_mm y_mlp
c_in c_zero c_bias c_tp c_turned c_qkv c_biased c_cos c_sin c_rot c_hi c_qs c_ks c_lo c_v
c_qm_tp c_qm c_mx c_max c_mfin c_neg c_neghi c_mrow c_mlo c_q_tp c_q
c_st c_exp c_pv c_acc c_acc_tp c_rsum c_o c_ot_tp c_ot c_proj c_xb"""


def constants():
    f = np.float32
    t = np.arange(T, dtype=f)
    half = np.arange(0, DH, 2, dtype=f)
    inv = (f(1.0) / np.power(f(10000.0), half / f(DH), dtype=f)).astype(f)
    freq = t[:, None] * inv[None, :]
    base = (half + f(0.4 * DH)) / f(1.4 * DH)
    power = (t - f(T // 2)) / f(WINDOW // 2)
    scale = np.power(base[None, :], power[:, None], dtype=f)
    c, s = np.cos(freq), np.sin(freq)
    cq, sq = f(QK_SCALE) * (c * scale), f(QK_SCALE) * (s * scale)
    ck, sk = c / scale, s / scale
    by_tile = lambda a: np.ascontiguousarray(a.reshape(NT, P, *a.shape[1:]).swapaxes(0, 1).astype(f))
    rope_c = by_tile(np.stack([cq, ck], 1))
    rope_s = by_tile(np.stack([np.stack([sq, -sq], 1), np.stack([sk, -sk], 1)], 1))
    r = np.arange(P)[:, None]
    k = np.arange(P)[None, :]
    w, q = r // 64, r % 64
    i = 64 * w + q
    j = np.where((w == 0) & (k >= 64), k - P, k)
    banned = (j > i) | (j < i - WINDOW)
    even = np.where(banned, MASKED, 0.0)
    odd = np.where(w == 0, np.roll(even, 64, axis=1), even)
    local = np.stack([np.where(banned | (j < 0), MASKED, 0.0), odd, even], 1).astype(f)
    frac = (f(2.0) * np.arange(D2 // 2, dtype=f)) / f(D2)
    ang = t[:, None] / np.power(f(1250.0), frac, dtype=f)[None, :]
    c2, s2 = np.cos(ang), np.sin(ang)
    causal = np.stack([np.where(k > r, MASKED, 0.0), np.where(r > k, MASKED, 0.0)], 1).astype(f)
    return {"ident": np.eye(P, dtype=f), "local_mask": local, "shifts": np.eye(P, 3 * P, P, dtype=f), "rope_c": rope_c, "rope_s": rope_s,
            "own": (r // SLOT == np.arange(HG)[None, :]).astype(f), "rope2_c": by_tile(c2), "rope2_s": by_tile(np.stack([-s2, s2], 1)), "causal_mask": causal}


_INS = {"x": "L0_attn_x", "W_attn": "L0_attn_W_attn", "b_attn": "L0_attn_b_attn", "W_proj": "L0_attn_W_proj",
        "b_proj": "L0_attn_b_proj", "wqkv": "L0_ffn_wqkv", "q_scale": "L0_ffn_q_scale", "k_scale": "L0_ffn_k_scale",
        "wo": "L0_ffn_wo", "ln_g": "L0_ffn_ln_g", "ln_b": "L0_ffn_ln_b", "w1": "L0_ffn_w1", "b1": "L0_ffn_b1",
        "w2": "L0_ffn_w2", "b2": "L0_ffn_b2"}


def kernel(**inputs):
    import concourse.bacc as _bacc
    from concourse.bass_utils import run_bass_kernel_spmd as _run

    nc = _bacc.Bacc("TRN2", target_bir_lowering=False, num_devices=1)
    arrays, dram = {}, {}
    given = {short: np.ascontiguousarray(inputs[name]) for short, name in _INS.items()}
    given["x"] = given["x"].reshape(T, C)
    for name, a in {**given, **constants()}.items():
        arrays[f"in_{name}"] = a
        dram[name] = nc.dram_tensor(f"in_{name}", a.shape, mybir.dt.from_np(a.dtype), kind="ExternalInput").ap()
    dram["out"] = nc.dram_tensor("out_0", (T, C), F32, kind="ExternalOutput").ap()
    build(nc, dram)
    r = _run(nc, [arrays], core_ids=[0])
    return r.results[0]["out_0"].reshape(1, T, C)
```
